# Optimizing a Trainium2 kernel written in Bass

```python
import numpy as np
import jax
import jax.numpy as jnp

def _softmax(x, axis=-1):
    return jax.nn.softmax(x, axis=axis)

def _gelu(x):
    return jax.nn.gelu(x, approximate=True)

def _silu(x):
    return jax.nn.silu(x)

def _sigmoid(x):
    return jax.nn.sigmoid(x)

def _layernorm(x, axis=-1, eps=1e-05):
    m = jnp.mean(x, axis=axis, keepdims=True)
    v = jnp.var(x, axis=axis, keepdims=True)
    return (x - m) / jnp.sqrt(v + eps)

def _scatter_add(tgt, idx, src, axis=0):
    return tgt.at[idx].add(src)

def _segment_sum(src, seg, n):
    return jax.ops.segment_sum(src, seg, n)
kernel_name = 'mk_gnn_resnorm_d2_gnn_r8_f44dae'

def setup_inputs(seed: int=0):
    np.random.seed(seed)
    _w = jnp.asarray

    def _rec_inputs():
        import jax
        import jax.numpy as jnp
        _gk = jax.random.key(seed)
        x = -8.776e-05 + 1 * jax.random.normal(jax.random.fold_in(_gk, 1), (6250, 256), jnp.float32)
        src = jax.random.randint(jax.random.fold_in(_gk, 2), (100000,), 0, 6250, jnp.int32)
        dst = jax.random.randint(jax.random.fold_in(_gk, 3), (100000,), 0, 6250, jnp.int32)
        _o = jnp.argsort(dst, stable=True)
        src = src[_o]
        dst = dst[_o]
        edge_attr_64 = 0.000279952 + 1.00013 * jax.random.normal(jax.random.fold_in(_gk, 12), (100000, 64), jnp.float32)
        return (x, src, dst, edge_attr_64)
    x, src, dst, edge_attr_64 = _rec_inputs()

    def _L0_gnn_setup():
        import jax, jax.numpy as jnp
        import numpy as np
        N, E, H, ED = (2500, 40000, 256, 64)
        key = jax.random.key(seed)
        ks = jax.random.split(key, 12)

        def init_w(k, shape, fan_in):
            return (jax.random.normal(k, shape, jnp.float32) / np.sqrt(fan_in)).astype(jnp.float32)
        h = jax.random.normal(ks[0], (N, H), jnp.float32)
        edge_indices = jax.random.randint(ks[1], (2, E), 0, N, jnp.int32)
        edge_attr = jax.random.normal(ks[2], (E, ED), jnp.float32)
        din = 2 * H + ED
        W1 = init_w(ks[3], (H, din), din)
        b1 = jnp.zeros((H,), jnp.float32)
        W2 = init_w(ks[4], (H, H), H)
        b2 = jnp.zeros((H,), jnp.float32)
        W_ih = init_w(ks[5], (3 * H, H), H)
        b_ih = jnp.zeros((3 * H,), jnp.float32)
        W_hh = init_w(ks[6], (3 * H, H), H)
        b_hh = jnp.zeros((3 * H,), jnp.float32)
        return {'h': h, 'edge_indices': edge_indices, 'edge_attr': edge_attr, 'W1': W1, 'b1': b1, 'W2': W2, 'b2': b2, 'W_ih': W_ih, 'b_ih': b_ih, 'W_hh': W_hh, 'b_hh': b_hh}
    _L0_gnn_all = _L0_gnn_setup()
    _L0_gnn_in = {k: v for k, v in _L0_gnn_all.items() if k in ('W1', 'b1', 'W2', 'b2', 'W_ih', 'b_ih', 'W_hh', 'b_hh')}
    del _L0_gnn_all

    def _L1_gnn_setup():
        import jax, jax.numpy as jnp
        import numpy as np
        N_NODES = 6250
        N_EDGES = 100000
        DIM = 256
        NUM_HEADS = 8
        key = jax.random.key(seed)
        k_x, k_wu, k_bu, k_wv, k_src, k_dst = jax.random.split(key, 6)
        x = jax.random.normal(k_x, (N_NODES, DIM), dtype=jnp.float32)
        W_u = jax.random.normal(k_wu, (NUM_HEADS, DIM), dtype=jnp.float32) * (1.0 / np.sqrt(DIM))
        b_u = jax.random.normal(k_bu, (NUM_HEADS,), dtype=jnp.float32) * 0.01
        W_v = jax.random.normal(k_wv, (NUM_HEADS, DIM), dtype=jnp.float32) * (1.0 / np.sqrt(DIM))
        src = jax.random.randint(k_src, (N_EDGES,), 0, N_NODES, dtype=jnp.int32)
        dst = jax.random.randint(k_dst, (N_EDGES,), 0, N_NODES, dtype=jnp.int32)
        return {'x': x, 'W_u': W_u, 'b_u': b_u, 'W_v': W_v, 'src': src, 'dst': dst}
    _L1_gnn_all = _L1_gnn_setup()
    _L1_gnn_in = {k: v for k, v in _L1_gnn_all.items() if k in ('W_u', 'b_u', 'W_v')}
    del _L1_gnn_all
    return {'x': x, 'src': src, 'dst': dst, 'edge_attr_64': edge_attr_64, 'L0_gnn_W1': _L0_gnn_in['W1'], 'L0_gnn_b1': _L0_gnn_in['b1'], 'L0_gnn_W2': _L0_gnn_in['W2'], 'L0_gnn_b2': _L0_gnn_in['b2'], 'L0_gnn_W_ih': _L0_gnn_in['W_ih'], 'L0_gnn_b_ih': _L0_gnn_in['b_ih'], 'L0_gnn_W_hh': _L0_gnn_in['W_hh'], 'L0_gnn_b_hh': _L0_gnn_in['b_hh'], 'L1_gnn_W_u': _L1_gnn_in['W_u'], 'L1_gnn_b_u': _L1_gnn_in['b_u'], 'L1_gnn_W_v': _L1_gnn_in['W_v']}

def reference(x, src, dst, edge_attr_64, L0_gnn_W1, L0_gnn_b1, L0_gnn_W2, L0_gnn_b2, L0_gnn_W_ih, L0_gnn_b_ih, L0_gnn_W_hh, L0_gnn_b_hh, L1_gnn_W_u, L1_gnn_b_u, L1_gnn_W_v):
    import jax
    import jax.numpy as jnp

    def _L0_gnn_ref(h, edge_indices, edge_attr, W1, b1, W2, b2, W_ih, b_ih, W_hh, b_hh):
        import jax, jax.numpy as jnp
        import numpy as np
        N, E, H, ED = (2500, 40000, 256, 64)
        row, col = (edge_indices[0], edge_indices[1])
        edge_in = jnp.concatenate([h[row], h[col], edge_attr], axis=-1)
        msg = jax.nn.relu(edge_in @ W1.T + b1) @ W2.T + b2
        agg = jax.ops.segment_sum(msg, row, num_segments=h.shape[0])
        gx = agg @ W_ih.T + b_ih
        gh = h @ W_hh.T + b_hh
        xr, xz, xn = jnp.split(gx, 3, axis=-1)
        hr, hz, hn = jnp.split(gh, 3, axis=-1)
        r = jax.nn.sigmoid(xr + hr)
        z = jax.nn.sigmoid(xz + hz)
        n = jnp.tanh(xn + r * hn)
        h_new = (1.0 - z) * n + z * h
        return h_new

    def _L1_gnn_ref(x, W_u, b_u, W_v, src, dst):
        import jax, jax.numpy as jnp
        import numpy as np
        N_NODES = 6250
        N_EDGES = 100000
        DIM = 256
        NUM_HEADS = 8
        n_nodes, dim = x.shape
        num_heads = W_u.shape[0]
        head_dim = dim // num_heads
        s_u = x @ W_u.T + b_u
        s_v = x @ W_v.T
        e = s_u[src] + s_v[dst]
        e = jnp.where(e >= 0, e, 0.2 * e)
        m = jax.ops.segment_max(e, dst, num_segments=n_nodes)
        e_exp = jnp.exp(e - m[dst])
        denom = jax.ops.segment_sum(e_exp, dst, num_segments=n_nodes)
        probs = e_exp / denom[dst]
        xh = x.reshape(n_nodes, head_dim, num_heads)
        msg = xh[src] * probs[:, None, :]
        out = jax.ops.segment_sum(msg, dst, num_segments=n_nodes)
        return out.reshape(n_nodes, dim)
    edge_index = jnp.stack([src, dst])
    x = _layernorm(x + _L0_gnn_ref(x, edge_index, edge_attr_64, L0_gnn_W1, L0_gnn_b1, L0_gnn_W2, L0_gnn_b2, L0_gnn_W_ih, L0_gnn_b_ih, L0_gnn_W_hh, L0_gnn_b_hh), axis=-1)
    x = _layernorm(x + _L1_gnn_ref(x, L1_gnn_W_u, L1_gnn_b_u, L1_gnn_W_v, src, dst), axis=-1)
    return x

_drawn_inputs = setup_inputs


def setup_inputs(seed=0):
    import zlib

    import numpy as np

    out = dict(_drawn_inputs(seed))
    spreads = {'L0_gnn_b1': (0.0, 0.1),
     'L0_gnn_b2': (0.0, 0.1),
     'L0_gnn_b_ih': (0.0, 0.607),
     'L0_gnn_b_hh': (0.0, 0.764)}
    factors = {'L1_gnn_b_u': 64.0}
    for name, (base, spread) in spreads.items():
        noise = np.random.default_rng([zlib.crc32(name.encode()), seed]).standard_normal(out[name].shape)
        drawn = base * np.exp(spread * noise) if base else spread * noise
        out[name] = jnp.asarray(drawn.astype(out[name].dtype))
    for name, factor in factors.items():
        out[name] = (out[name] * factor).astype(out[name].dtype)
    return out
```

```python
import concourse.bass as bass
from concourse import mybir
from contextlib import ExitStack

F32 = mybir.dt.float32
I32 = mybir.dt.int32
ALU = mybir.AluOpType
ACT = mybir.ActivationFunctionType
AX = mybir.AxisListType

P = 128
N, E, H, ED, NH = 6250, 100000, 256, 64, 8
NB = -(-N // P)
NP = NB * P
PAD = NP - 1
HALF = 8
GROUP = 2 * HALF
NG = -(-E // (P * GROUP))
NT = NG * GROUP
NTX = NT + 2 * GROUP
HC = H // P
CH = 7
CQ = NT // CH
UNR = 7
NI = NB // UNR
NTAB = 2
UW = H + 1
XW = H + NH
PW = H + 2 * NH
EPS = 1e-5
SLOPE = 0.2
LOW = -1e30
assert NB % UNR == 0 and NT % CH == 0


def flat(ap):
    return ap.rearrange("p o n -> p (o n)")


class Mem:

    def __init__(self, nc, stack, prefix=""):
        self.nc, self.stack, self.prefix = nc, stack, prefix

    def sb(self, name, shape, dt=F32):
        return self.stack.enter_context(self.nc.sbuf_tensor(self.prefix + name, shape, dt))

    def ps(self, name, shape, dt=F32):
        return self.stack.enter_context(self.nc.psum_tensor(self.prefix + name, shape, dt))

    def sem(self, name):
        return self.stack.enter_context(self.nc.semaphore(self.prefix + name))


class Chain:

    def __init__(self, engine, sem, base=0):
        self.engine, self.sem, self.base, self.n = engine, sem, base, 0

    def link(self, instruction):
        self.n += 1
        instruction.then_inc(self.sem, 1)
        self.engine.wait_ge(self.sem, self.base + self.n)


def window_shifts(width):
    shifts, reach = [], 0
    while reach < width - 1:
        shifts.append(min(reach + 1, width - 1 - reach))
        reach += shifts[-1]
    return shifts


def segment_max(nc, chain, value, key, width, apart, left, right):
    shifts = window_shifts(width)
    for n, d in enumerate(shifts):
        w = width - d
        chain.link(nc.vector.tensor_tensor(apart[:, 0:w], key[:, d:width], key[:, 0:w], ALU.not_equal))
        nc.vector.scalar_tensor_tensor(left[:, 0:w], apart[:, 0:w], LOW, value[:, 0:w], ALU.mult, ALU.add)
        chain.link(nc.vector.scalar_tensor_tensor(right[:, 0:w], apart[:, 0:w], LOW, value[:, d:width], ALU.mult, ALU.add))
        chain.link(nc.vector.tensor_tensor(value[:, d:width], value[:, d:width], left[:, 0:w], ALU.max))
        wider = nc.vector.tensor_tensor(value[:, 0:w], value[:, 0:w], right[:, 0:w], ALU.max)
        if n < len(shifts) - 1:
            chain.link(wider)
    return wider


def setup_phase(nc, K, D, A):
    with ExitStack() as st:
        m = Mem(nc, st, "su_")
        rawi = {"src": m.sb("srci", [CQ, CH, P], I32), "dst": m.sb("dsti", [CQ, CH, P], I32)}
        rawf = {"src": m.sb("srcf", [CQ, CH, P]), "dst": m.sb("dstf", [CQ, CH, P])}
        padrow = m.sb("padrow", [NTX - NT, P])
        w1 = m.sb("w1", [P, HC, 2 * H + ED])
        w1c2 = m.sb("w1c2", [P, HC, 2 * ED])
        w2 = m.sb("w2", [P, HC, H])
        wih = m.sb("wih", [P, 3 * HC, H])
        whh = m.sb("whh", [P, 3 * HC, H])
        wuv = m.sb("wuv", [2 * NH, H])
        zeros = m.sb("zeros", [P, 2570])
        abias = m.sb("abias", [P, 2 * H])
        xs = m.sb("xs", [P, UNR, H])
        xT = m.sb("xT", [P, UNR, H])
        ab = m.sb("ab", [P, UNR, 2 * H])
        bhh = m.sb("bhh", [P, 2 * H])
        psJ = [m.ps(f"psJ{i}", [P, 512]) for i in range(4)]
        psX = [m.ps(f"psX{i}", [P, 512]) for i in range(2)]
        psA = [m.ps(f"psA{i}", [P, 512]) for i in range(2)]
        consts = m.sem("consts")
        masks = m.sem("masks")
        edges_in = m.sem("edges_in")
        weights_in = m.sem("weights_in")
        bias_in = m.sem("bias_in")
        x_in = [m.sem(f"x_in{j}") for j in range(UNR)]
        floats = m.sem("floats")
        rows_out = m.sem("rows_out")
        turned = m.sem("turned")
        kept = m.sem("kept")
        dve_step = m.sem("dve_step")
        x_turned = m.sem("x_turned")
        xT_ready = m.sem("xT_ready")
        ab_done = m.sem("ab_done")
        ab_ready = m.sem("ab_ready")
        ab_out = [m.sem(f"ab_out{j}") for j in range(UNR)]
        tables_clear = m.sem("tables_clear")

        jobs = [(rawf[s][:, c, :], K[f"{s}T"][:, c * CQ:(c + 1) * CQ]) for s in ("src", "dst") for c in range(CH)]
        n_index = len(jobs)
        for o in range(HC):
            rows = slice(o * P, (o + 1) * P)
            for k in range(2 * HC):
                at = (k // HC) * H + o * P
                jobs.append((w1[:, o, k * P:(k + 1) * P], K["W1abT"][:, k % HC, at:at + P]))
            jobs.append((w1c2[:, o, :], K["W1cT"][:, rows]))
            jobs += [(w2[:, o, k * P:(k + 1) * P], K["W2T"][:, k, rows]) for k in range(HC)]
        for o in range(3 * HC):
            for k in range(HC):
                jobs.append((wih[:, o, k * P:(k + 1) * P], K["WihT"][:, k, o * P:(o + 1) * P]))
                jobs.append((whh[:, o, k * P:(k + 1) * P], K["WhhT"][:, k, o * P:(o + 1) * P]))
        jobs += [(wuv[:, k * P:(k + 1) * P], K["WuvT"][:, k, :]) for k in range(HC)]

        block = st.enter_context(nc.Block())

        @block.sync
        def _(sp):
            sp.wait_ge(consts, 2)
            full = (CH - 1) * CQ * P
            for name in ("src", "dst"):
                e = A[name]
                tail = (E - full) // P
                sp.dma_start(rawi[name][:, 0:CH - 1, :],
                             e[0:full].rearrange("(c q p) -> q c p", q=CQ, p=P)).then_inc(edges_in, 16)
                sp.dma_start(rawi[name][0:tail, CH - 1, :],
                             e[full:full + tail * P].rearrange("(q p) -> q p", p=P)).then_inc(edges_in, 16)
                sp.dma_start(rawi[name][tail:tail + 1, CH - 1, 0:E - full - tail * P],
                             e[full + tail * P:E].rearrange("(q p) -> q p", q=1)).then_inc(edges_in, 16)
            sp.dma_start(w1[:, :, :], A["W1"].rearrange("(o p) k -> p o k", p=P)).then_inc(weights_in, 16)
            for n in range(2):
                sp.dma_start(w1c2[:, :, n * ED:(n + 1) * ED],
                             A["W1"][:, 2 * H:2 * H + ED].rearrange("(o p) k -> p o k", p=P)).then_inc(weights_in, 16)
            sp.dma_start(w2[:, :, :], A["W2"].rearrange("(o p) k -> p o k", p=P)).then_inc(weights_in, 16)
            sp.dma_start(wih[:, :, :], A["W_ih"].rearrange("(o p) k -> p o k", p=P)).then_inc(weights_in, 16)
            sp.dma_start(whh[:, :, :], A["W_hh"].rearrange("(o p) k -> p o k", p=P)).then_inc(weights_in, 16)
            sp.dma_start(wuv[0:NH, :], A["W_u"]).then_inc(weights_in, 16)
            sp.dma_start(wuv[NH:2 * NH, :], A["W_v"]).then_inc(weights_in, 16)
            for j in range(UNR):
                sp.dma_start(xs[:, j, :], A["x"][j * P:(j + 1) * P, :]).then_inc(x_in[j], 16)
            sp.wait_ge(floats, 2)
            for name in ("src", "dst"):
                sp.dma_start(D[f"{name}_rows"][0:NT, :].rearrange("(c q) p -> q c p", q=CQ),
                             rawf[name][:, :, :]).then_inc(rows_out, 16)
                sp.dma_start(D[f"{name}_rows"][NT:NTX, :], padrow[:, :]).then_inc(rows_out, 16)
            def load_x(i, j, count):
                sp.wait_ge(x_turned, i * UNR + (j + 1))
                sp.dma_start(xs[0:count, j, :], A["x"][bass.ds(i * (UNR * P) + (UNR + j) * P, count), :]).then_inc(x_in[j], 16)

            def store_ab(i, j):
                sp.wait_ge(ab_ready, i * UNR + (j + 1))
                rows = bass.ds(i * (UNR * P) + j * P, P)
                sp.dma_start(D["A"][rows, :], ab[:, j, 0:H]).then_inc(ab_out[j], 16)
                sp.dma_start(D["B"][rows, :], ab[:, j, H:2 * H]).then_inc(ab_out[j], 16)

            with sp.Fori(0, NI - 2) as i:
                for j in range(UNR):
                    load_x(i, j, P)
                    store_ab(i, j)
            for j in range(UNR):
                load_x(NI - 2, j, P if j < UNR - 1 else N - (NB - 1) * P)
                store_ab(NI - 2, j)
            for j in range(UNR):
                store_ab(NI - 1, j)
            sp.wait_ge(rows_out, 64)
            for j in range(UNR):
                sp.wait_ge(ab_out[j], 32 * NI)

        @block.scalar
        def _(act):
            act.wait_ge(consts, 4)
            act.dma_start(abias[:, H:2 * H], A["b1"].partition_broadcast(P)).then_inc(bias_in, 16)
            act.dma_start(K["bgate"][:, 0:3 * H], A["b_ih"].partition_broadcast(P)).then_inc(bias_in, 16)
            act.dma_start(bhh[:, :], A["b_hh"][0:2 * H].partition_broadcast(P)).then_inc(bias_in, 16)
            act.dma_start(K["bgate"][:, 3 * H:4 * H], A["b_hh"][2 * H:3 * H].partition_broadcast(P)).then_inc(bias_in, 16)
            act.dma_start(K["bu"][:, 0:NH], A["b_u"].partition_broadcast(P)).then_inc(bias_in, 16)
            act.dma_start(K["b2row"][:, :], A["b2"].rearrange("(o h) -> o h", o=1)).then_inc(bias_in, 16)
            for t in range(NTAB):
                v = D[f"S{t}"].rearrange("n w -> (n w)").rearrange("(p r w) -> p r w", p=P, w=2570)
                for r in range(v.shape[1]):
                    act.dma_start(v[:, r, :], zeros[:, :]).then_inc(tables_clear, 16)
            with act.Fori(0, NI) as i:
                for j in range(UNR):
                    act.wait_ge(x_turned, i * UNR + (j + 1))
                    nc.scalar.copy(xT[:, j, :], psX[j % 2][:, 0:H]).then_inc(xT_ready, 1)
            act.wait_ge(bias_in, 96)
            act.wait_ge(tables_clear, 16 * NTAB * 5)

        @block.gpsimd
        def _(pool):
            nc.gpsimd.memset(K["ident"][:, :], 0.0).then_inc(masks, 1)
            nc.gpsimd.memset(K["before"][:, :], 1.0).then_inc(masks, 1)
            nc.gpsimd.iota(K["nodeid_i"][:, :], pattern=[[P, NB]], base=0, channel_multiplier=1).then_inc(masks, 1)
            pool.wait_ge(masks, 3)
            nc.gpsimd.affine_select(out=K["ident"][:, :], in_=K["ident"][:, :], compare_op=ALU.not_equal, fill=1.0,
                                    base=0, pattern=[[-1, P]], channel_multiplier=1).then_inc(masks, 1)
            nc.gpsimd.affine_select(out=K["before"][:, :], in_=K["before"][:, :], compare_op=ALU.is_gt, fill=0.0,
                                    base=0, pattern=[[-1, P]], channel_multiplier=1).then_inc(masks, 1)

        @block.tensor
        def _(pe):
            pe.wait_ge(masks, 5)
            pe.wait_ge(floats, 2)
            for n, (source, _) in enumerate(jobs):
                if n == n_index:
                    pe.wait_ge(weights_in, 128)
                if n >= 4:
                    pe.wait_ge(kept, n - 3)
                rows, cols = source.shape
                nc.tensor.transpose(psJ[n % 4][0:cols, 0:rows], source, K["ident"][0:rows, 0:rows]).then_inc(turned, 1)
            pe.wait_ge(kept, len(jobs))
            with pe.Fori(0, NI) as i:
                def turn(j):
                    pe.wait_ge(xT_ready, i * UNR + max(j - 1, 0))
                    pe.wait_ge(x_in[j], i * 16 + 16)
                    for k in range(HC):
                        t = nc.tensor.transpose(psX[j % 2][:, k * P:(k + 1) * P], xs[:, j, k * P:(k + 1) * P],
                                                K["ident"][:, :])
                    t.then_inc(x_turned, 1)
                turn(0)
                for j in range(UNR):
                    if j < UNR - 1:
                        turn(j + 1)
                    pe.wait_ge(xT_ready, i * UNR + (j + 1))
                    pe.wait_ge(ab_ready, i * UNR + max(j - 1, 0))
                    for k in range(HC):
                        t = nc.tensor.matmul(psA[j % 2][:, :], xT[:, j, k * P:(k + 1) * P],
                                             K["W1abT"][:, k, :], start=(k == 0), stop=(k == HC - 1))
                    t.then_inc(ab_done, 1)

        @block.vector
        def _(dve):
            nc.vector.memset(rawi["src"][:, :, :], PAD).then_inc(consts, 1)
            nc.vector.memset(rawi["dst"][:, :, :], PAD).then_inc(consts, 1)
            nc.vector.memset(zeros[:, :], 0.0).then_inc(consts, 1)
            nc.vector.memset(abias[:, 0:H], 0.0).then_inc(consts, 1)
            nc.vector.memset(padrow[:, :], float(PAD))
            nc.vector.memset(K["bu"][:, NH:2 * NH], 0.0)
            nc.vector.memset(K["eps"][:, :], EPS)
            nc.vector.memset(K["neghalf"][:, :], -0.5)
            for s in ("src", "dst"):
                nc.vector.memset(K[f"{s}T"][:, NT:NTX], float(PAD))
            dve.wait_ge(edges_in, 96)
            nc.vector.tensor_copy(rawf["src"][:, :, :], rawi["src"][:, :, :]).then_inc(floats, 1)
            nc.vector.tensor_copy(rawf["dst"][:, :, :], rawi["dst"][:, :, :]).then_inc(floats, 1)
            for n, (source, target) in enumerate(jobs):
                rows, cols = source.shape
                dve.wait_ge(turned, n + 1)
                nc.vector.tensor_copy(target, psJ[n % 4][0:cols, 0:rows]).then_inc(kept, 1)
            dve.wait_ge(kept, n_index)
            dve.wait_ge(masks, 3)
            nc.vector.tensor_copy(K["srcT_i"][:, :], K["srcT"][:, :])
            nc.vector.tensor_copy(K["dstT_i"][:, :], K["dstT"][:, :])
            nc.vector.tensor_copy(K["nodeid"][:, :], K["nodeid_i"][:, :])
            dve.wait_ge(bias_in, 96)
            nc.vector.tensor_tensor(K["bgate"][:, 0:2 * H], K["bgate"][:, 0:2 * H], bhh[:, :], ALU.add).then_inc(dve_step, 1)
            with dve.Fori(0, NI) as i:
                for j in range(UNR):
                    dve.wait_ge(ab_done, i * UNR + (j + 1))
                    dve.wait_ge(ab_out[j], i * 32)
                    nc.vector.tensor_tensor(ab[:, j, :], psA[j % 2][:, :], abias[:, :], ALU.add).then_inc(ab_ready, 1)


def layer0_phase(nc, K, D, A):
    with ExitStack() as st:
        m = Mem(nc, st, "l0_")
        SLOTS = HALF
        ga = m.sb("ga", [P, SLOTS, H])
        gb = m.sb("gb", [P, SLOTS, H])
        gsrc = [m.sb(f"gsrc{h}", [P, HALF], I32) for h in range(2)]
        gdst = [m.sb(f"gdst{h}", [P, HALF], I32) for h in range(2)]
        sink = [m.sb(f"sink{h}", [P, HALF], I32) for h in range(2)]
        srcb = [m.sb(f"srcb{h}", [P, HALF, P]) for h in range(2)]
        same = [m.sb(f"same{h}", [P, HALF, P]) for h in range(2)]
        attr = [m.sb(f"attr{h}", [P, HALF, ED]) for h in range(2)]
        earlier = m.sb("earlier", [P, HALF, P])
        dup = m.sb("dup", [P, HALF])
        togo = m.sb("togo", [P, HALF])
        spare = m.sb("spare", [P, 1])
        attrT = [m.sb(f"attrT{q}", [2 * ED, 2 * P]) for q in range(2)]
        hid = m.sb("hid", [P, 4, UW])
        msum = m.sb("msum", [P, 4, UW])
        psT = [m.ps(f"psT{q}", [P, 512]) for q in range(2)]
        psC = [m.ps(f"psC{q}", [P, 512]) for q in range(4)]
        psU = [m.ps(f"psU{q}", [P, 512]) for q in range(2)]
        gathered = [m.sem(f"gathered{s}") for s in range(SLOTS)]
        scattered = [m.sem(f"scattered{t}") for t in range(NTAB)]
        src_in = [m.sem(f"src_in{h}") for h in range(2)]
        attr_in = [m.sem(f"attr_in{h}") for h in range(2)]
        index_ready = m.sem("index_ready")
        same_ready = m.sem("same_ready")
        dve_step = m.sem("dve_step")
        ab_sum = m.sem("ab_sum")
        pre_ready = m.sem("pre_ready")
        hid_ready = m.sem("hid_ready")
        attr_turned = m.sem("attr_turned")
        attrT_ready = m.sem("attrT_ready")
        c_done = m.sem("c_done")
        agg_done = m.sem("agg_done")
        msum_ready = m.sem("msum_ready")
        ones = m.sem("ones")
        pool_waited = m.sem("pool_waited")
        attr_end = m.sem("attr_end")
        block = st.enter_context(nc.Block())

        def pc(t):
            return psC[t % 4][:, 0:H]

        @block.sync
        def _(sp):
            def src_rows(h, row):
                sp.dma_start(srcb[h][:, :, :].rearrange("p t e -> p (t e)"),
                             D["src_rows"][row, :].rearrange("t e -> (t e)").partition_broadcast(P)).then_inc(src_in[h], 16)

            def attr_tiles(h, edge):
                sp.dma_start(attr[h][:, :, :],
                             A["edge_attr"][edge, :].rearrange("(t p) d -> p t d", p=P)).then_inc(attr_in[h], 16)

            for h in range(2):
                src_rows(h, slice(h * HALF, (h + 1) * HALF))
                attr_tiles(h, slice(h * HALF * P, (h + 1) * HALF * P))
            with sp.Fori(0, NG - 2) as g:
                for h in range(2):
                    sp.wait_ge(same_ready, g * 2 + (h + 1))
                    src_rows(h, bass.ds(g * GROUP + (GROUP + h * HALF), HALF))
                    sp.wait_ge(attr_turned, g * 4 + 2 * (h + 1))
                    attr_tiles(h, bass.ds(g * (GROUP * P) + (GROUP + h * HALF) * P, HALF * P))
            g = NG - 2
            for h in range(2):
                sp.wait_ge(same_ready, g * 2 + (h + 1))
                src_rows(h, slice((g + 1) * GROUP + h * HALF, (g + 1) * GROUP + (h + 1) * HALF))
                sp.wait_ge(attr_turned, g * 4 + 2 * (h + 1))
                first = (g + 1) * GROUP * P + h * HALF * P
                if h == 0:
                    attr_tiles(h, slice(first, first + HALF * P))
                else:
                    whole = (E - first) // P
                    sp.dma_start(attr[h][0:E - first - whole * P, whole, :],
                                 A["edge_attr"][first + whole * P:E, :]).then_inc(attr_end, 16)
                    sp.wait_ge(attr_end, 16)
                    sp.dma_start(attr[h][:, 0:whole, :],
                                 A["edge_attr"][first:first + whole * P, :].rearrange("(t p) d -> p t d", p=P)).then_inc(attr_in[h], 16)
            sp.wait_ge(same_ready, 2 * NG - 1)
            src_rows(0, slice(NT, NT + HALF))
            sp.wait_ge(attr_turned, 4 * NG - 2)
            attr_tiles(0, slice(0, HALF * P))
            sp.wait_ge(src_in[0], 16 * (NG + 1))
            sp.wait_ge(attr_in[0], 16 * (NG + 1))

        @block.gpsimd
        def _(pool):
            def gather(j):
                s, h = j % SLOTS, j // HALF
                pool.indirect_dma_start(ga[:, s, :], None, D["A"],
                                        bass.IndirectOffsetOnAxis(ap=gsrc[h][:, s:s + 1], axis=0)).then_inc(gathered[s], 16)
                pool.indirect_dma_start(gb[:, s, :], None, D["B"],
                                        bass.IndirectOffsetOnAxis(ap=gdst[h][:, s:s + 1], axis=0)).then_inc(gathered[s], 16)

            pool.wait_ge(index_ready, 2)
            for j in range(SLOTS):
                gather(j)

            def group(g, last=False):
                for j in range(GROUP):
                    pool.wait_ge(msum_ready, g * GROUP + (j + 1))
                    pool.wait_ge(scattered[j % NTAB], g * (16 * GROUP // NTAB) + 16 * (j // NTAB))
                    pool.sem_inc(pool_waited, 1)
                    pool.indirect_dma_start(D[f"S{j % NTAB}"],
                                            bass.IndirectOffsetOnAxis(ap=sink[j // HALF][:, j % HALF:j % HALF + 1], axis=0),
                                            msum[:, j % 4, :], None, compute_op=ALU.add).then_inc(scattered[j % NTAB], 16)
                    if last and j >= HALF:
                        continue
                    if j == 0 or j == HALF:
                        pool.wait_ge(index_ready, g * 2 + (2 + j // HALF))
                    pool.wait_ge(hid_ready, g * GROUP + (j + 1))
                    pool.sem_inc(pool_waited, 1)
                    gather((j + SLOTS) % GROUP)

            with pool.Fori(0, NG - 1) as g:
                group(g)
            group(NG - 1, last=True)
            for t in range(NTAB):
                pool.wait_ge(scattered[t], 16 * NT // NTAB)
            for s in range(SLOTS):
                pool.wait_ge(gathered[s], 32 * (NT // SLOTS))

        @block.tensor
        def _(pe):
            def turn(g, q):
                h, at = q % 4 // 2, q % 2 * 4
                if q % 2 == 0:
                    pe.wait_ge(attr_in[h], g * 16 + 16 * (1 + q // 4))
                for n in range(2):
                    pair = attr[h][:, at + 2 * n:at + 2 * n + 2, :].rearrange("p t d -> p (t d)")
                    t = nc.tensor.transpose(psT[q % 2][:, n * P:(n + 1) * P], pair, K["ident"][:, :])
                t.then_inc(attr_turned, 1)

            def project(g, j):
                if j % 4 == 0:
                    pe.wait_ge(attrT_ready, g * 4 + (j // 4 + 1))
                side = slice(j % 2 * ED, (j % 2 + 1) * ED)
                nc.tensor.matmul(pc(j), attrT[j // 4 % 2][side, j % 4 // 2 * P:(j % 4 // 2 + 1) * P], K["W1cT"][side, :],
                                 start=True, stop=True).then_inc(c_done, 1)

            turn(0, 0)
            turn(0, 1)
            for j in range(4):
                project(0, j)
            with pe.Fori(0, NG) as g:
                for j in range(GROUP):
                    if j % 4 == 0:
                        pe.wait_ge(attrT_ready, g * 4 + (j // 4 + 1))
                        turn(g, j // 4 + 2)
                    pe.wait_ge(pre_ready, g * GROUP + (j + 1))
                    project(g, j + 4)
                    if j % HALF == 0:
                        pe.wait_ge(same_ready, g * 2 + (j // HALF + 1))
                    pe.wait_ge(hid_ready, g * GROUP + (j + 1))
                    nc.tensor.matmul(psU[j % 2][:, 0:UW], same[j // HALF][:, j % HALF, :], hid[:, j % 4, :],
                                     start=True, stop=True).then_inc(agg_done, 1)

        @block.scalar
        def _(act):
            def keep_attr(g, q):
                act.wait_ge(attr_turned, g * 4 + (q + 1))
                nc.scalar.copy(attrT[q % 2][:, :], psT[q % 2][:, 0:2 * P]).then_inc(attrT_ready, 1)

            act.wait_ge(ones, 1)
            keep_attr(0, 0)
            keep_attr(0, 1)
            with act.Fori(0, NG) as g:
                for j in range(GROUP):
                    if j % 4 == 0:
                        act.wait_ge(c_done, g * GROUP + (j + 4))
                        keep_attr(g, j // 4 + 2)
                    act.wait_ge(pre_ready, g * GROUP + (j + 1))
                    nc.scalar.activation(hid[:, j % 4, 0:H], ga[:, j % SLOTS, :], ACT.Relu).then_inc(hid_ready, 1)
                    act.wait_ge(agg_done, g * GROUP + (j + 1))
                    act.wait_ge(scattered[j % NTAB], g * (16 * GROUP // NTAB) + max(16 * (j // NTAB) - 16, 0))
                    nc.scalar.copy(msum[:, j % 4, :], psU[j % 2][:, 0:UW]).then_inc(msum_ready, 1)

        @block.vector
        def _(dve):
            def stage_index(g, h):
                at = bass.ds(g * GROUP + h * HALF, HALF)
                nc.vector.tensor_copy(gsrc[h % 2][:, :], K["srcT_i"][:, at])
                nc.vector.tensor_copy(gdst[h % 2][:, :], K["dstT_i"][:, at]).then_inc(index_ready, 1)

            def compare(chain, g, h):
                ids = K["srcT"][:, bass.ds(g * GROUP + h * HALF, HALF)]
                dve.wait_ge(src_in[h % 2], g * 16 + 16 * (1 + h // 2))
                chain.link(nc.vector.tensor_tensor(same[h % 2][:, :, :], srcb[h % 2][:, :, :],
                                                   ids.unsqueeze(2).to_broadcast([P, HALF, P]), ALU.is_equal))
                chain.link(nc.vector.tensor_tensor(earlier[:, :, :], same[h % 2][:, :, :],
                                                   K["before"][:, :].unsqueeze(1).to_broadcast([P, HALF, P]), ALU.mult))
                chain.link(nc.vector.tensor_reduce(dup[:, :], earlier[:, :, :], AX.X, ALU.max))
                chain.link(nc.vector.tensor_scalar(togo[:, :], ids, -1.0, spare[:, 0:1], ALU.mult, ALU.add))
                chain.link(nc.vector.tensor_tensor(togo[:, :], togo[:, :], dup[:, :], ALU.mult))
                nc.vector.tensor_tensor(sink[h % 2][:, :], togo[:, :], ids, ALU.add).then_inc(same_ready, 1)

            nc.vector.memset(hid[:, :, :], 1.0).then_inc(ones, 1)
            first = Chain(dve, dve_step)
            first.link(nc.vector.tensor_scalar(spare[:, :], K["nodeid"][:, 0:1], float(NP), None, ALU.add))
            stage_index(0, 0)
            stage_index(0, 1)
            compare(first, 0, 0)
            PER = 10
            with dve.Fori(0, NG) as g:
                chain = Chain(dve, dve_step, g * PER + first.n)
                for j in range(GROUP):
                    s = j % SLOTS
                    dve.wait_ge(gathered[s], g * (32 * GROUP // SLOTS) + 32 * (j // SLOTS + 1))
                    nc.vector.tensor_tensor(ga[:, s, :], ga[:, s, :], gb[:, s, :], ALU.add).then_inc(ab_sum, 1)
                    dve.wait_ge(ab_sum, g * GROUP + (j + 1))
                    dve.wait_ge(c_done, g * GROUP + (j + 1))
                    nc.vector.tensor_tensor(ga[:, s, :], ga[:, s, :], pc(j), ALU.add).then_inc(pre_ready, 1)
                    if j % HALF == HALF // 2:
                        h = j // HALF
                        dve.wait_ge(agg_done, g * GROUP + h * HALF)
                        for t in range(NTAB):
                            dve.wait_ge(scattered[t], g * (16 * GROUP // NTAB) + h * (16 * HALF // NTAB))
                        compare(chain, g, h + 1)
                    if j % HALF == HALF - 1:
                        stage_index(g, 2 + j // HALF)
                assert chain.n == PER


def nodes_phase(nc, K, D, A):
    with ExitStack() as st:
        m = Mem(nc, st, "nd_")
        sums = [m.sb(f"sums{t}", [P, UNR, UW]) for t in range(NTAB)]
        xs = m.sb("xs", [P, UNR, H])
        turnedT = m.sb("turnedT", [P, UNR, 4 * P])
        degT = m.sb("degT", [1, UNR, P])
        aggT = m.sb("aggT", [P, UNR, H])
        rz = m.sb("rz", [P, UNR, 2 * H])
        cand = m.sb("cand", [P, UNR, 2 * H])
        tmp = m.sb("tmp", [P, UNR, H])
        y = m.sb("y", [P, UNR, H])
        stats = m.sb("stats", [P, UNR, 6])
        moments = m.sb("moments", [P, UNR, 2])
        rstd = m.sb("rstd", [P, UNR, 1])
        x1 = m.sb("x1", [P, UNR, H + 2 * NH])
        x1T = m.sb("x1T", [P, UNR, H])
        psT = m.ps("psT", [P, 512])
        psD = m.ps("psD", [P, 512])
        psG = m.ps("psG", [P, 512])
        psRZ = m.ps("psRZ", [P, 512])
        psN = m.ps("psN", [P, 512])
        psX = m.ps("psX", [P, 512])
        psS = m.ps("psS", [P, 512])
        loaded = [m.sem(f"loaded{j}") for j in range(UNR)]
        stored = [m.sem(f"stored{j}") for j in range(UNR)]
        summed, turned, turned_kept = m.sem("summed"), m.sem("turned"), m.sem("turned_kept")
        agg_done, agg_kept = m.sem("agg_done"), m.sem("agg_kept")
        gates_done, gates_kept, gates_open = m.sem("gates_done"), m.sem("gates_kept"), m.sem("gates_open")
        cand_ready, cand_done = m.sem("cand_ready"), m.sem("cand_done")
        x1_ready, x1_turned, x1T_ready = m.sem("x1_ready"), m.sem("x1_turned"), m.sem("x1T_ready")
        scores_done, rows_ready = m.sem("scores_done"), m.sem("rows_ready")
        var_ready = m.sem("var_ready")
        moments_ready, rstd_ready = m.sem("moments_ready"), m.sem("rstd_ready")
        dve_step = m.sem("dve_step")
        dve_waited = m.sem("dve_waited")
        block = st.enter_context(nc.Block())

        def iterations(engine, body):
            body(0, True, False)
            with engine.Fori(1, NI - 1) as i:
                body(i, False, False)
            body(NI - 1, False, True)

        @block.sync
        def _(sp):
            def load(row, j, count=P):
                for t in range(NTAB):
                    sp.dma_start(sums[t][:, j, :], D[f"S{t}"][bass.ds(row, P), :]).then_inc(loaded[j], 16)
                sp.dma_start(xs[0:count, j, :], A["x"][bass.ds(row, count), :]).then_inc(loaded[j], 16)

            def store(i, j):
                sp.wait_ge(rows_ready, i * UNR + (j + 1))
                rows = bass.ds(i * (UNR * P) + j * P, P)
                sp.dma_start(D["X1"][rows, :], x1[:, j, 0:XW]).then_inc(stored[j], 16)
                sp.dma_start(D["sv"][rows, :], x1[:, j, XW:XW + NH]).then_inc(stored[j], 16)

            for j in range(UNR):
                load(j * P, j)
            with sp.Fori(0, NI - 2) as i:
                for j in range(UNR):
                    store(i, j)
                    load(i * (UNR * P) + (UNR + j) * P, j)
            for j in range(UNR):
                store(NI - 2, j)
                row = (NI - 1) * UNR * P + j * P
                load(row, j, min(P, N - row))
            for j in range(UNR):
                store(NI - 1, j)
            for j in range(UNR):
                sp.wait_ge(stored[j], 32 * NI)

        @block.gpsimd
        def _(pool):
            with pool.Fori(0, NI) as i:
                for j in range(UNR):
                    pool.wait_ge(moments_ready, i * UNR + (j + 1))
                    nc.gpsimd.tensor_tensor(rstd[:, j, :], moments[:, j, 1:2], K["eps"][:, :], ALU.add).then_inc(var_ready, 1)
                    pool.wait_ge(var_ready, i * UNR + (j + 1))
                    nc.gpsimd.tensor_tensor(rstd[:, j, :], rstd[:, j, :], K["neghalf"][:, :], ALU.pow).then_inc(rstd_ready, 1)

        @block.tensor
        def _(pe):
            def turn(i, j):
                pe.wait_ge(turned_kept, i * UNR + j)
                pe.wait_ge(summed, i * UNR + (j + 1))
                for k in range(HC):
                    nc.tensor.transpose(psT[:, k * P:(k + 1) * P], sums[0][:, j, k * P:(k + 1) * P], K["ident"][:, :])
                    nc.tensor.transpose(psT[:, (HC + k) * P:(HC + k + 1) * P], xs[:, j, k * P:(k + 1) * P], K["ident"][:, :])
                nc.tensor.transpose(psD[0:1, 0:P], sums[0][:, j, H:UW], K["ident"][:, :]).then_inc(turned, 1)

            def aggregate(i, j):
                pe.wait_ge(agg_kept, i * UNR + j)
                pe.wait_ge(turned_kept, i * UNR + (j + 1))
                for f in range(HC):
                    cols = slice(f * P, (f + 1) * P)
                    for k in range(HC):
                        nc.tensor.matmul(psG[:, cols], K["W2T"][:, k, cols], turnedT[:, j, k * P:(k + 1) * P],
                                         start=(k == 0), stop=False)
                    t = nc.tensor.matmul(psG[:, cols], K["b2row"][:, cols], degT[:, j, :], start=False, stop=True)
                t.then_inc(agg_done, 1)

            def gates(i, j):
                pe.wait_ge(gates_kept, i * UNR + j)
                pe.wait_ge(agg_kept, i * UNR + (j + 1))
                for k in range(HC):
                    a, xk = aggT[:, j, k * P:(k + 1) * P], turnedT[:, j, (HC + k) * P:(HC + k + 1) * P]
                    nc.tensor.matmul(psRZ[:, :], a, K["WihT"][:, k, 0:2 * H], start=(k == 0), stop=False)
                    nc.tensor.matmul(psRZ[:, :], xk, K["WhhT"][:, k, 0:2 * H], start=False, stop=(k == HC - 1))
                for w, at in (("WihT", 0), ("WhhT", H)):
                    for k in range(HC):
                        lhs = aggT[:, j, k * P:(k + 1) * P] if at == 0 else turnedT[:, j, (HC + k) * P:(HC + k + 1) * P]
                        t = nc.tensor.matmul(psN[:, at:at + H], lhs, K[w][:, k, 2 * H:3 * H],
                                             start=(k == 0), stop=(k == HC - 1))
                t.then_inc(gates_done, 1)

            def turn_x1(i, j):
                pe.wait_ge(x1T_ready, i * UNR + j)
                pe.wait_ge(x1_ready, i * UNR + (j + 1))
                for k in range(HC):
                    t = nc.tensor.transpose(psX[:, k * P:(k + 1) * P], x1[:, j, k * P:(k + 1) * P], K["ident"][:, :])
                t.then_inc(x1_turned, 1)

            def scores(i, j):
                pe.wait_ge(rows_ready, i * UNR + j)
                pe.wait_ge(x1T_ready, i * UNR + (j + 1))
                for k in range(HC):
                    t = nc.tensor.matmul(psS[:, 0:2 * NH], x1T[:, j, k * P:(k + 1) * P], K["WuvT"][:, k, :],
                                         start=(k == 0), stop=(k == HC - 1))
                t.then_inc(scores_done, 1)

            def before(i, j, n, first):
                if j >= n:
                    return i, j - n
                return None if first else (i - 1, UNR + j - n)

            turn(0, 0)
            aggregate(0, 0)

            def body(i, first, last):
                for j in range(UNR):
                    if at := before(i, j, 2, first):
                        scores(*at)
                    gates(i, j)
                    after = (i, j + 1) if j + 1 < UNR else (None if last else (i + 1, 0))
                    if after:
                        turn(*after)
                    if at := before(i, j, 1, first):
                        turn_x1(*at)
                    if after:
                        aggregate(*after)

            iterations(pe, body)
            scores(NI - 1, UNR - 2)
            turn_x1(NI - 1, UNR - 1)
            scores(NI - 1, UNR - 1)

        @block.scalar
        def _(act):
            def keep_turned(i, j):
                act.wait_ge(turned, i * UNR + (j + 1))
                nc.scalar.copy(degT[:, j, :], psD[0:1, 0:P])
                nc.scalar.copy(turnedT[:, j, :], psT[:, :]).then_inc(turned_kept, 1)

            def keep_agg(i, j):
                act.wait_ge(agg_done, i * UNR + (j + 1))
                nc.scalar.copy(aggT[:, j, :], psG[:, 0:H]).then_inc(agg_kept, 1)

            def keep_x1(i, j):
                act.wait_ge(x1_turned, i * UNR + (j + 1))
                nc.scalar.copy(x1T[:, j, :], psX[:, 0:H]).then_inc(x1T_ready, 1)

            keep_turned(0, 0)
            keep_agg(0, 0)

            def body(i, first, last):
                for j in range(UNR):
                    act.wait_ge(gates_kept, i * UNR + (j + 1))
                    nc.scalar.activation(rz[:, j, :], rz[:, j, :], ACT.Sigmoid).then_inc(gates_open, 1)
                    after = (i, j + 1) if j + 1 < UNR else (None if last else (i + 1, 0))
                    if after:
                        keep_turned(*after)
                    if j >= 1 or not first:
                        keep_x1(*((i, j - 1) if j >= 1 else (i - 1, UNR - 1)))
                    act.wait_ge(cand_ready, i * UNR + (j + 1))
                    nc.scalar.activation(cand[:, j, 0:H], cand[:, j, 0:H], ACT.Tanh).then_inc(cand_done, 1)
                    if after:
                        keep_agg(*after)

            iterations(act, body)
            keep_x1(NI - 1, UNR - 1)

        @block.vector
        def _(dve):
            def add_tables(i, j):
                dve.wait_ge(loaded[j], i * (16 * (NTAB + 1)) + 16 * (NTAB + 1))
                for t in range(1, NTAB):
                    nc.vector.tensor_tensor(sums[0][:, j, :], sums[0][:, j, :], sums[t][:, j, :], ALU.add).then_inc(summed, 1)

            def finish(i, j):
                dve.wait_ge(scores_done, i * UNR + (j + 1))
                nc.vector.tensor_tensor(x1[:, j, H:H + 2 * NH], psS[:, 0:2 * NH], K["bu"][:, :], ALU.add).then_inc(rows_ready, 1)

            add_tables(0, 0)
            PER = 6 * UNR

            def body(i, first, last):
                c = Chain(dve, dve_step, i * PER)
                for j in range(UNR):
                    after = (i, j + 1) if j + 1 < UNR else (None if last else (i + 1, 0))
                    if after:
                        add_tables(*after)
                    if j >= 2 or not first:
                        finish(*((i, j - 2) if j >= 2 else (i - 1, UNR + j - 2)))
                    dve.wait_ge(gates_done, i * UNR + (j + 1))
                    nc.vector.tensor_tensor(rz[:, j, :], psRZ[:, :], K["bgate"][:, 0:2 * H], ALU.add)
                    nc.vector.tensor_tensor(cand[:, j, :], psN[:, :], K["bgate"][:, 2 * H:4 * H], ALU.add).then_inc(gates_kept, 1)
                    dve.wait_ge(gates_open, i * UNR + (j + 1))
                    c.link(nc.vector.tensor_tensor(tmp[:, j, :], rz[:, j, 0:H], cand[:, j, H:2 * H], ALU.mult))
                    nc.vector.tensor_tensor(cand[:, j, 0:H], cand[:, j, 0:H], tmp[:, j, :], ALU.add).then_inc(cand_ready, 1)
                    dve.wait_ge(cand_done, i * UNR + (j + 1))
                    c.link(nc.vector.tensor_tensor(tmp[:, j, :], xs[:, j, :], cand[:, j, 0:H], ALU.subtract))
                    c.link(nc.vector.tensor_tensor(tmp[:, j, :], tmp[:, j, :], rz[:, j, H:2 * H], ALU.mult))
                    c.link(nc.vector.tensor_tensor(y[:, j, :], xs[:, j, :], cand[:, j, 0:H], ALU.add))
                    c.link(nc.vector.tensor_tensor(y[:, j, :], y[:, j, :], tmp[:, j, :], ALU.add))
                    c.link(nc.vector.bn_stats(stats[:, j, :], y[:, j, :]))
                    dve.sem_inc(dve_waited, 1)
                    nc.vector.bn_aggr(moments[:, j, :], stats[:, j, :]).then_inc(moments_ready, 1)
                    dve.wait_ge(rstd_ready, i * UNR + (j + 1))
                    dve.wait_ge(stored[j], i * 32)
                    nc.vector.tensor_scalar(x1[:, j, 0:H], y[:, j, :], moments[:, j, 0:1], rstd[:, j, :],
                                            ALU.subtract, ALU.mult).then_inc(x1_ready, 1)
                assert c.n == PER, c.n

            iterations(dve, body)
            finish(NI - 1, UNR - 2)
            finish(NI - 1, UNR - 1)


def layer1_phase(nc, K, D, A):
    with ExitStack() as st:
        m = Mem(nc, st, "l1_")
        feats = [m.sb(f"feats{r}", [P, GROUP, XW]) for r in range(2)]
        svd = [m.sb(f"svd{r}", [P, GROUP, NH]) for r in range(2)]
        gsrc = [m.sb(f"gsrc{r}", [P, GROUP], I32) for r in range(2)]
        gdst = [m.sb(f"gdst{r}", [P, GROUP], I32) for r in range(2)]
        dstb = [m.sb(f"dstb{r}", [P, GROUP, P]) for r in range(2)]
        same = [m.sb(f"same{r}", [P, GROUP, P]) for r in range(2)]
        part = [m.sb(f"part{r}", [P, GROUP, PW]) for r in range(2)]
        score = m.sb("score", [P, GROUP, NH])
        below = m.sb("below", [P, GROUP, NH])
        dst8 = m.sb("dst8", [P, GROUP, NH])
        ed = m.sb("ed", [P, 2 * P])
        apart = m.sb("apart", [P, P])
        left = m.sb("left", [P, P])
        right = m.sb("right", [P, P])
        psE = m.ps("psE", [P, 512])
        psM = m.ps("psM", [P, 512])
        psU = [m.ps(f"psU{q}", [P, 512]) for q in range(4)]
        gathered = [m.sem(f"gathered{r}") for r in range(2)]
        dst_in = [m.sem(f"dst_in{r}") for r in range(2)]
        stored = [m.sem(f"stored{r}") for r in range(2)]
        index_ready, same_ready = m.sem("index_ready"), m.sem("same_ready")
        scores_ready, scores_turned = m.sem("scores_ready"), m.sem("scores_turned")
        max_ready, max_turned = m.sem("max_ready"), m.sem("max_turned")
        below_ready, weights_ready = m.sem("below_ready"), m.sem("weights_ready")
        weighted, agg_done, part_ready = m.sem("weighted"), m.sem("agg_done"), m.sem("part_ready")
        max_kept, ed_ready = m.sem("max_kept"), m.sem("ed_ready")
        dve_step = m.sem("dve_step")
        pool_waited = m.sem("pool_waited")
        block = st.enter_context(nc.Block())

        def groups(engine, body, count=NG):
            with engine.Fori(0, count // 2) as u:
                for r in range(2):
                    body(u * 2 + r, r, u, False)
            if count % 2:
                body(count - 1, 0, count // 2, True)

        @block.sync
        def _(sp):
            def dst_rows(r, row):
                sp.dma_start(dstb[r][:, :, :].rearrange("p t e -> p (t e)"),
                             D["dst_rows"][row, :].rearrange("t e -> (t e)").partition_broadcast(P)).then_inc(dst_in[r], 16)

            for r in range(2):
                dst_rows(r, slice(r * GROUP, (r + 1) * GROUP))

            def body(g, r, u, last):
                sp.wait_ge(same_ready, g + 1)
                dst_rows(r, bass.ds(g * GROUP + 2 * GROUP, GROUP))
                sp.wait_ge(part_ready, g * GROUP + GROUP)
                sp.wait_ge(max_kept, g + 1)
                sp.dma_start(D["PT"][bass.ds(g * (GROUP * P), GROUP * P), :].rearrange("(t p) w -> p t w", p=P),
                             part[r][:, :, :]).then_inc(stored[r], 16)

            groups(sp, body)
            for r in range(2):
                sp.wait_ge(stored[r], 16 * ((NG + 1 - r) // 2))
                sp.wait_ge(dst_in[r], 16 * ((NG + 1 - r) // 2 + 1))

        @block.gpsimd
        def _(pool):
            def gather(r, t):
                pool.indirect_dma_start(feats[r][:, t, :], None, D["X1"],
                                        bass.IndirectOffsetOnAxis(ap=gsrc[r][:, t:t + 1], axis=0)).then_inc(gathered[r], 16)
                pool.indirect_dma_start(svd[r][:, t, :], None, D["sv"],
                                        bass.IndirectOffsetOnAxis(ap=gdst[r][:, t:t + 1], axis=0)).then_inc(gathered[r], 16)

            pool.wait_ge(index_ready, 2)
            for r in range(2):
                for t in range(GROUP):
                    gather(r, t)

            def body(g, r, u, last):
                pool.wait_ge(index_ready, g + 3)
                for t in range(GROUP):
                    pool.wait_ge(agg_done, g * GROUP + (t + 1))
                    pool.sem_inc(pool_waited, 1)
                    gather(r, t)

            groups(pool, body, NG - 2)

        @block.tensor
        def _(pe):
            def body(g, r, u, last):
                pe.wait_ge(scores_ready, g + 1)
                nc.tensor.transpose(psE[:, 0:P], score[:, :, :].rearrange("p t h -> p (t h)"), K["ident"][:, :])
                nc.tensor.transpose(psE[:, P:2 * P], dst8[:, :, :].rearrange("p t h -> p (t h)"),
                                    K["ident"][:, :]).then_inc(scores_turned, 1)
                pe.wait_ge(max_ready, g + 1)
                nc.tensor.transpose(psM[:, 0:P], ed[:, 0:P], K["ident"][:, :]).then_inc(max_turned, 1)
                pe.wait_ge(same_ready, g + 1)
                for t in range(GROUP):
                    if t % 4 == 0:
                        pe.wait_ge(weighted, g * (GROUP // 4) + (t // 4 + 1))
                    pe.wait_ge(part_ready, g * GROUP + t - 3) if t >= 4 else pe.wait_ge(part_ready, g * GROUP)
                    nc.tensor.matmul(psU[t % 4][:, 0:XW], same[r][:, t, :], feats[r][:, t, :],
                                     start=True, stop=True).then_inc(agg_done, 1)

            groups(pe, body)

        @block.scalar
        def _(act):
            def body(g, r, u, last):
                act.wait_ge(below_ready, g + 1)
                nc.scalar.activation(feats[r][:, :, H:XW], below[:, :, :], ACT.Exp).then_inc(weights_ready, 1)
                act.wait_ge(stored[r], u * 16)
                nc.scalar.copy(part[r][:, :, XW:PW], psM[:, 0:P].rearrange("p (t h) -> p t h", h=NH)).then_inc(max_kept, 1)
                for t in range(GROUP):
                    act.wait_ge(agg_done, g * GROUP + (t + 1))
                    nc.scalar.copy(part[r][:, t, 0:XW], psU[t % 4][:, 0:XW]).then_inc(part_ready, 1)

            groups(act, body)

        @block.vector
        def _(dve):
            def stage_index(g, r):
                at = bass.ds(g * GROUP, GROUP)
                nc.vector.tensor_copy(gsrc[r][:, :], K["srcT_i"][:, at])
                nc.vector.tensor_copy(gdst[r][:, :], K["dstT_i"][:, at]).then_inc(index_ready, 1)

            def compare(g, r, u):
                dve.wait_ge(dst_in[r], u * 16 + 16)
                nc.vector.tensor_tensor(same[r][:, :, :], dstb[r][:, :, :],
                                        K["dstT"][:, bass.ds(g * GROUP, GROUP)].unsqueeze(2).to_broadcast([P, GROUP, P]),
                                        ALU.is_equal).then_inc(same_ready, 1)

            stage_index(0, 0)
            stage_index(1, 1)
            compare(0, 0, 0)
            PER = 4 * len(window_shifts(P))
            eT, dT = ed[:, 0:P], ed[:, P:2 * P]

            def body(g, r, u, last):
                c = Chain(dve, dve_step, g * PER)
                dve.wait_ge(gathered[r], u * (32 * GROUP) + 32 * GROUP)
                stage_index(g + 2, r)
                nc.vector.tensor_copy(dst8[:, :, :],
                                      K["dstT"][:, bass.ds(g * GROUP, GROUP)].unsqueeze(2).to_broadcast([P, GROUP, NH]))
                c.link(nc.vector.tensor_tensor(score[:, :, :], feats[r][:, :, H:XW], svd[r][:, :, :], ALU.add))
                nc.vector.scalar_tensor_tensor(score[:, :, :], score[:, :, :], SLOPE, score[:, :, :],
                                               ALU.mult, ALU.max).then_inc(scores_ready, 1)
                dve.wait_ge(scores_turned, g + 1)
                nc.vector.tensor_copy(ed[:, :], psE[:, 0:2 * P]).then_inc(ed_ready, 1)
                dve.wait_ge(ed_ready, g + 1)
                segment_max(nc, c, eT, dT, P, apart, left, right).then_inc(max_ready, 1)
                dve.wait_ge(max_turned, g + 1)
                nc.vector.tensor_tensor(below[:, :, :], score[:, :, :], psM[:, 0:P].rearrange("p (t h) -> p t h", h=NH),
                                        ALU.subtract).then_inc(below_ready, 1)
                dve.wait_ge(weights_ready, g + 1)
                for q in range(GROUP // 4):
                    f = feats[r][:, q * 4:(q + 1) * 4, :]
                    f3 = f[:, :, 0:H].rearrange("p t (c h) -> p t c h", h=NH)
                    w3 = f[:, :, H:XW].unsqueeze(2).to_broadcast([P, 4, H // NH, NH])
                    nc.vector.tensor_tensor(f3, f3, w3, ALU.mult).then_inc(weighted, 1)
                if not last:
                    dve.wait_ge(agg_done, g * GROUP)
                    compare(g + 1, 1 - r, u + r)
                assert c.n == PER

            groups(dve, body)


def places_phase(nc, K, D, A):
    with ExitStack() as st:
        m = Mem(nc, st, "pl_")
        firstb = m.sb("firstb", [P, NT])
        found = m.sb("found", [P, UNR, NT])
        tiles = m.sb("tiles", [P, NB])
        tile = m.sb("tile", [P, NB])
        tile_i = m.sb("tile_i", [P, NB], I32)
        rows = m.sb("rows", [P, NB, P])
        within = m.sb("within", [P, NB])
        upto = m.sb("upto", [P, NB])
        until = m.sb("until", [P, NB])
        begin = m.sb("begin", [P, NB])
        full = m.sb("full", [P, NB])
        cross = m.sb("cross", [P, NB])
        zero = m.sb("zero", [1, 1])
        firsts_out, firsts_in = m.sem("firsts_out"), m.sem("firsts_in")
        zero_set, counted = m.sem("zero_set"), m.sem("counted")
        gathered = m.sem("gathered")
        upto_ready, upto_out, until_in = m.sem("upto_ready"), m.sem("upto_out"), m.sem("until_in")
        tile_ready = m.sem("tile_ready")
        dve_step = m.sem("dve_step")
        block = st.enter_context(nc.Block())

        @block.sync
        def _(sp):
            with nc.allow_non_contiguous_dma(reason="one word of each tile"):
                sp.dma_start(D["first"], D["dst_rows"][0:NT, 0:1]).then_inc(firsts_out, 16)
                sp.dma_start(D["last"], D["dst_rows"][0:NT, P - 1:P]).then_inc(firsts_out, 16)
                sp.wait_ge(firsts_out, 32)
                sp.dma_start(firstb[:, :], D["first"].rearrange("t o -> (t o)").partition_broadcast(P)).then_inc(firsts_in, 16)
                sp.wait_ge(zero_set, 1)
                sp.dma_start(D["upto"][0:1, :], zero[:, :]).then_inc(upto_out, 16)
                sp.wait_ge(upto_ready, 1)
                sp.dma_start(D["upto"][1:NP + 1, :].rearrange("(b p) o -> p (b o)", p=P), upto[:, :]).then_inc(upto_out, 16)
                sp.wait_ge(upto_out, 32)
                sp.dma_start(until[:, :], D["upto"][0:NP, :].rearrange("(b p) o -> p (b o)", p=P)).then_inc(until_in, 16)
            sp.wait_ge(until_in, 16)

        @block.gpsimd
        def _(pool):
            pool.wait_ge(tile_ready, 1)
            for b in range(NB):
                pool.indirect_dma_start(rows[:, b, :], None, D["dst_rows"],
                                        bass.IndirectOffsetOnAxis(ap=tile_i[:, b:b + 1], axis=0)).then_inc(gathered, 16)
            pool.wait_ge(gathered, 16 * NB)

        @block.vector
        def _(dve):
            nc.vector.memset(zero[:, :], 0.0).then_inc(zero_set, 1)
            nc.vector.memset(K["own_row"][:, NB:], 0.0)
            nc.vector.memset(K["ends_row"][:, NB:], 0.0)
            dve.wait_ge(firsts_in, 16)
            with dve.Fori(0, NI) as i:
                nodes = K["nodeid"][:, bass.ds(i * UNR, UNR)].unsqueeze(2).to_broadcast([P, UNR, NT])
                dve.wait_ge(counted, i * 2)
                nc.vector.tensor_tensor(found[:, :, :], firstb[:, :].unsqueeze(1).to_broadcast([P, UNR, NT]), nodes,
                                        ALU.is_le).then_inc(counted, 1)
                dve.wait_ge(counted, i * 2 + 1)
                nc.vector.tensor_reduce(tiles[:, bass.ds(i * UNR, UNR)], found[:, :, :], AX.X, ALU.add).then_inc(counted, 1)
            dve.wait_ge(counted, 2 * NI)
            c = Chain(dve, dve_step)
            c.link(nc.vector.tensor_scalar(tile[:, :], tiles[:, :], -1.0, 0.0, ALU.add, ALU.max))
            nc.vector.tensor_copy(tile_i[:, :], tile[:, :]).then_inc(tile_ready, 1)
            dve.wait_ge(gathered, 16 * NB)
            c.link(nc.vector.tensor_tensor(rows[:, :, :], rows[:, :, :],
                                           K["nodeid"][:, :].unsqueeze(2).to_broadcast([P, NB, P]), ALU.is_le))
            c.link(nc.vector.tensor_reduce(within[:, :], rows[:, :, :], AX.X, ALU.add))
            c.link(nc.vector.tensor_scalar(begin[:, :], tile[:, :], float(P), None, ALU.mult))
            nc.vector.tensor_tensor(upto[:, :], begin[:, :], within[:, :], ALU.add).then_inc(upto_ready, 1)
            dve.wait_ge(until_in, 16)
            dve.wait_ge(upto_ready, 1)
            c.link(nc.vector.tensor_tensor(K["any"][:, :], upto[:, :], until[:, :], ALU.is_gt))
            c.link(nc.vector.tensor_scalar(full[:, :], within[:, :], float(P), None, ALU.is_equal))
            c.link(nc.vector.tensor_tensor(cross[:, :], until[:, :], begin[:, :], ALU.is_lt))
            c.link(nc.vector.tensor_tensor(cross[:, :], cross[:, :], full[:, :], ALU.max))
            c.link(nc.vector.tensor_tensor(K["ends"][:, :], cross[:, :], K["any"][:, :], ALU.mult))
            c.link(nc.vector.tensor_scalar(cross[:, :], full[:, :], -1.0, 1.0, ALU.mult, ALU.add))
            c.link(nc.vector.tensor_tensor(K["own"][:, :], cross[:, :], K["any"][:, :], ALU.mult))
            c.link(nc.vector.tensor_scalar(K["own_row"][:, 0:NB], upto[:, :], -1.0, 0.0, ALU.add, ALU.max))
            c.link(nc.vector.tensor_tensor(tile[:, :], tile[:, :], cross[:, :], ALU.subtract))
            c.link(nc.vector.tensor_scalar(K["ends_row"][:, 0:NB], tile[:, :], 0.0, None, ALU.max))


def merge_phase(nc, K, D, A):
    with ExitStack() as st:
        m = Mem(nc, st, "mg_")
        rows = m.sb("rows", [CQ, CH, PW])
        t2 = m.sb("t2", [CQ, CH, PW])
        last = m.sb("last", [CQ, CH])
        lastb = m.sb("lastb", [CQ, NT])
        same = m.sb("same", [CQ, CH, NT])
        maxT = m.sb("maxT", [NH, NT])
        apart = m.sb("apart", [NH, NT])
        left = m.sb("left", [NH, NT])
        right = m.sb("right", [NH, NT])
        scale = m.sb("scale", [CQ, CH, NH])
        psA = [m.ps(f"psA{i}", [P, 512]) for i in range(2)]
        psM = m.ps("psM", [P, 512])
        psS = [m.ps(f"psS{i}", [P, 512]) for i in range(2)]
        rows_in, last_in = m.sem("rows_in"), m.sem("last_in")
        turned, kept, max_ready, max_turned = m.sem("turned"), m.sem("kept"), m.sem("max_ready"), m.sem("max_turned")
        below_ready, scale_ready, scaled = m.sem("below_ready"), m.sem("scale_ready"), m.sem("scaled")
        summed, t2_ready, t2_out = m.sem("summed"), m.sem("t2_ready"), m.sem("t2_out")
        dve_step = m.sem("dve_step")
        block = st.enter_context(nc.Block())
        split = 4

        @block.sync
        def _(sp):
            sp.dma_start(rows[:, :, :], D["PT"].rearrange("(c q p) w -> q c p w", q=CQ, p=P)[:, :, P - 1, :]).then_inc(rows_in, 16)
            sp.dma_start(lastb[:, :], D["last"].rearrange("t o -> (t o)").partition_broadcast(CQ)).then_inc(last_in, 16)
            with nc.allow_non_contiguous_dma(reason="one word of each tile"):
                sp.dma_start(last[:, :], D["last"].rearrange("(c q) o -> q (c o)", q=CQ)).then_inc(last_in, 16)
            sp.wait_ge(t2_ready, CH + 1)
            sp.dma_start(D["T2"].rearrange("(c q) w -> q c w", q=CQ), t2[:, :, :]).then_inc(t2_out, 16)
            sp.wait_ge(t2_out, 16)

        @block.tensor
        def _(pe):
            pe.wait_ge(rows_in, 16)
            for c in range(CH):
                at = c % split * CQ
                i = nc.tensor.transpose(psA[c // split][0:NH, at:at + CQ], rows[:, c, XW:PW], K["ident"][0:CQ, 0:CQ])
            i.then_inc(turned, 1)
            pe.wait_ge(max_ready, 1)
            for c in range(CH):
                i = nc.tensor.transpose(psM[0:CQ, c * NH:(c + 1) * NH], maxT[:, c * CQ:(c + 1) * CQ], K["ident"][0:NH, 0:NH])
            i.then_inc(max_turned, 1)
            pe.wait_ge(scaled, 2)
            for a in range(CH):
                if a >= 2:
                    pe.wait_ge(t2_ready, a)
                for c in range(CH):
                    i = nc.tensor.matmul(psS[a % 2][0:CQ, 0:XW], same[:, c, a * CQ:(a + 1) * CQ], rows[:, c, 0:XW],
                                         start=(c == 0), stop=(c == CH - 1))
                i.then_inc(summed, 1)

        @block.scalar
        def _(act):
            act.wait_ge(below_ready, 1)
            nc.scalar.activation(scale[:, :, :], scale[:, :, :], ACT.Exp).then_inc(scale_ready, 1)
            nc.scalar.copy(t2[:, :, XW:PW], psM[0:CQ, 0:CH * NH].rearrange("p (c h) -> p c h", h=NH)).then_inc(t2_ready, 1)
            for a in range(CH):
                act.wait_ge(summed, a + 1)
                nc.scalar.copy(t2[:, a, 0:XW], psS[a % 2][0:CQ, 0:XW]).then_inc(t2_ready, 1)

        @block.vector
        def _(dve):
            c = Chain(dve, dve_step)
            dve.wait_ge(turned, 1)
            dve.wait_ge(last_in, 32)
            c.link(nc.vector.tensor_copy(maxT[:, 0:split * CQ], psA[0][0:NH, 0:split * CQ]))
            c.link(nc.vector.tensor_copy(maxT[:, split * CQ:NT], psA[1][0:NH, 0:NT - split * CQ]))
            segment_max(nc, c, maxT, lastb[0:NH, :], NT, apart, left, right).then_inc(max_ready, 1)
            nc.vector.tensor_tensor(same[:, :, :], lastb[:, :].unsqueeze(1).to_broadcast([CQ, CH, NT]),
                                    last[:, :].unsqueeze(2).to_broadcast([CQ, CH, NT]), ALU.is_equal).then_inc(scaled, 1)
            dve.wait_ge(max_turned, 1)
            nc.vector.tensor_tensor(scale[:, :, :], rows[:, :, XW:PW],
                                    psM[0:CQ, 0:CH * NH].rearrange("p (c h) -> p c h", h=NH), ALU.subtract).then_inc(below_ready, 1)
            dve.wait_ge(scale_ready, 1)
            u = rows[:, :, 0:XW].rearrange("p c (n h) -> p c n h", h=NH)
            nc.vector.tensor_tensor(u, u, scale[:, :, :].unsqueeze(2).to_broadcast([CQ, CH, XW // NH, NH]),
                                    ALU.mult).then_inc(scaled, 1)


def output_phase(nc, K, D, A):
    with ExitStack() as st:
        m = Mem(nc, st, "ot_")
        idx = [m.sb(f"idx{r}", [P, 2, UNR], I32) for r in range(2)]
        ends = [m.sb(f"ends{r}", [P, UNR, PW]) for r in range(2)]
        own = [m.sb(f"own{r}", [P, UNR, PW]) for r in range(2)]
        x1 = [m.sb(f"x1{r}", [P, UNR, H]) for r in range(2)]
        y = [m.sb(f"y{r}", [P, UNR, H]) for r in range(2)]
        w = m.sb("w", [P, 2, UNR, NH])
        den = m.sb("den", [P, 2, UNR, NH])
        top = m.sb("top", [P, UNR, NH])
        valid = m.sb("valid", [P, 2, UNR])
        mask = m.sb("mask", [P, 2, UNR])
        none = m.sb("none", [P, UNR])
        stats = m.sb("stats", [P, UNR, 6])
        moments = m.sb("moments", [P, UNR, 2])
        rstd = m.sb("rstd", [P, UNR])
        index_ready = m.sem("index_ready")
        gathered = [m.sem(f"gathered{r}") for r in range(2)]
        x1_in = [m.sem(f"x1_in{r}") for r in range(2)]
        out_sent = [m.sem(f"out_sent{r}") for r in range(2)]
        below_ready, weights_ready, added = m.sem("below_ready"), m.sem("weights_ready"), m.sem("added")
        moments_ready, var_ready, rstd_ready, y_ready = m.sem("moments_ready"), m.sem("var_ready"), m.sem("rstd_ready"), m.sem("y_ready")
        dve_step = m.sem("dve_step")
        pool_waited, dve_waited = m.sem("pool_waited"), m.sem("dve_waited")
        block = st.enter_context(nc.Block())

        def units(engine, body):
            with engine.Fori(0, NI // 2) as u:
                for r in range(2):
                    body(u * 2 + r, r, u, False)
            body(NI - 1, 0, NI // 2, True)

        span = UNR * P

        @block.sync
        def _(sp):
            def load(u, r):
                sp.dma_start(x1[r][:, :, :], D["X1"][bass.ds(u * span, span), 0:H].rearrange("(b p) h -> p b h", p=P)).then_inc(x1_in[r], 16)

            for r in range(2):
                load(r, r)

            def step(u, ahead):
                for r in range(2):
                    sp.wait_ge(y_ready, u * (2 * UNR) + UNR * (r + 1))
                    sp.dma_start(A["out"][bass.ds(u * (2 * span) + r * span, span), :].rearrange("(b p) h -> p b h", p=P),
                                 y[r][:, :, :]).then_inc(out_sent[r], 16)
                    if r < ahead:
                        sp.wait_ge(added, u * 2 + (r + 1))
                        load(u * 2 + (2 + r), r)

            with sp.Fori(0, NI // 2 - 1) as u:
                step(u, 2)
            step(NI // 2 - 1, 1)
            first = (NI - 1) * span
            whole = (N - first) // P
            sp.wait_ge(y_ready, NI * UNR)
            sp.dma_start(A["out"][first:first + whole * P, :].rearrange("(b p) h -> p b h", p=P),
                         y[0][:, 0:whole, :]).then_inc(out_sent[0], 16)
            sp.dma_start(A["out"][first + whole * P:N, :], y[0][0:N - first - whole * P, whole, :]).then_inc(out_sent[0], 16)
            sp.wait_ge(out_sent[0], 16 * (NI // 2 + 2))
            sp.wait_ge(out_sent[1], 16 * (NI // 2))

        @block.gpsimd
        def _(pool):
            def norm(u):
                pool.wait_ge(moments_ready, u * UNR + UNR)
                nc.gpsimd.tensor_tensor(rstd[:, :], moments[:, :, 1], K["eps"][:, 0:1].to_broadcast([P, UNR]), ALU.add).then_inc(var_ready, 1)
                pool.wait_ge(var_ready, u + 1)
                nc.gpsimd.tensor_tensor(rstd[:, :], rstd[:, :], K["neghalf"][:, 0:1].to_broadcast([P, UNR]), ALU.pow).then_inc(rstd_ready, 1)

            def gather(u, r):
                pool.wait_ge(index_ready, u + 1)
                pool.sem_inc(pool_waited, 1)
                for j in range(UNR):
                    pool.indirect_dma_start(ends[r][:, j, :], None, D["T2"],
                                            bass.IndirectOffsetOnAxis(ap=idx[r][:, 0, j:j + 1], axis=0)).then_inc(gathered[r], 16)
                    pool.indirect_dma_start(own[r][:, j, :], None, D["PT"],
                                            bass.IndirectOffsetOnAxis(ap=idx[r][:, 1, j:j + 1], axis=0)).then_inc(gathered[r], 16)

            gather(0, 0)
            gather(1, 1)
            with pool.Fori(0, NI // 2 - 1) as u:
                norm(u * 2)
                gather(u * 2 + 2, 0)
                norm(u * 2 + 1)
                gather(u * 2 + 3, 1)
            norm(NI - 3)
            gather(NI - 1, 0)
            norm(NI - 2)
            norm(NI - 1)
        @block.scalar
        def _(act):
            def body(u, r, v, last):
                act.wait_ge(below_ready, u + 1)
                nc.scalar.activation(w[:, :, :, :], w[:, :, :, :], ACT.Exp).then_inc(weights_ready, 1)

            units(act, body)

        @block.vector
        def _(dve):
            def stage_index(u, r):
                at = bass.ds(u * UNR, UNR)
                nc.vector.tensor_copy(idx[r][:, 0, :], K["ends_row"][:, at])
                nc.vector.tensor_copy(idx[r][:, 1, :], K["own_row"][:, at]).then_inc(index_ready, 1)

            stage_index(0, 0)
            stage_index(1, 1)
            PER = 13

            def body(u, r, v, last):
                c = Chain(dve, dve_step, u * PER)
                at = bass.ds(u * UNR, UNR)
                pair = (ends[r], own[r])
                dve.wait_ge(gathered[r], v * (32 * UNR) + 32 * UNR)
                if not last:
                    stage_index(u + 2, r)
                nc.vector.tensor_scalar(none[:, :], K["any"][:, at], -1.0, 1.0, ALU.mult, ALU.add)
                nc.vector.tensor_copy(valid[:, 0, :], K["ends"][:, at])
                c.link(nc.vector.tensor_copy(valid[:, 1, :], K["own"][:, at]))
                c.link(nc.vector.tensor_scalar(mask[:, :, :], valid[:, :, :], -1.0, -LOW, ALU.add, ALU.mult))
                for n in range(2):
                    t = nc.vector.tensor_tensor(w[:, n, :, :], pair[n][:, :, XW:PW],
                                                mask[:, n, :].unsqueeze(2).to_broadcast([P, UNR, NH]), ALU.add)
                c.link(t)
                c.link(nc.vector.tensor_tensor(top[:, :, :], w[:, 0, :, :], w[:, 1, :, :], ALU.max))
                nc.vector.tensor_tensor(w[:, :, :, :], w[:, :, :, :], top[:, :, :].unsqueeze(1).to_broadcast([P, 2, UNR, NH]),
                                        ALU.subtract).then_inc(below_ready, 1)
                dve.wait_ge(weights_ready, u + 1)
                c.link(nc.vector.tensor_tensor(w[:, :, :, :], w[:, :, :, :],
                                               valid[:, :, :].unsqueeze(3).to_broadcast([P, 2, UNR, NH]), ALU.mult))
                for n in range(2):
                    t = nc.vector.tensor_tensor(den[:, n, :, :], pair[n][:, :, H:XW], w[:, n, :, :], ALU.mult)
                c.link(t)
                c.link(nc.vector.tensor_tensor(top[:, :, :], den[:, 0, :, :], den[:, 1, :, :], ALU.add))
                c.link(nc.vector.tensor_tensor(top[:, :, :], top[:, :, :], none[:, :].unsqueeze(2).to_broadcast([P, UNR, NH]), ALU.add))
                c.link(nc.vector.reciprocal(top[:, :, :], top[:, :, :]))
                c.link(nc.vector.tensor_tensor(w[:, :, :, :], w[:, :, :, :], top[:, :, :].unsqueeze(1).to_broadcast([P, 2, UNR, NH]), ALU.mult))
                for n in range(2):
                    f = pair[n][:, :, 0:H].rearrange("p b (c h) -> p b c h", h=NH)
                    t = nc.vector.tensor_tensor(f, f, w[:, n, :, :].unsqueeze(2).to_broadcast([P, UNR, H // NH, NH]), ALU.mult)
                c.link(t)
                c.link(nc.vector.tensor_tensor(ends[r][:, :, 0:H], ends[r][:, :, 0:H], own[r][:, :, 0:H], ALU.add))
                dve.wait_ge(x1_in[r], v * 16 + 16)
                dve.wait_ge(out_sent[r], v * 16)
                nc.vector.tensor_tensor(y[r][:, :, :], ends[r][:, :, 0:H], x1[r][:, :, :], ALU.add).then_inc(added, 1)
                dve.wait_ge(added, u + 1)
                for j in range(UNR):
                    t = nc.vector.bn_stats(stats[:, j, :], y[r][:, j, :])
                c.link(t)
                dve.sem_inc(dve_waited, 1)
                for j in range(UNR):
                    nc.vector.bn_aggr(moments[:, j, :], stats[:, j, :]).then_inc(moments_ready, 1)
                dve.wait_ge(rstd_ready, u + 1)
                for j in range(UNR):
                    nc.vector.tensor_scalar(y[r][:, j, :], y[r][:, j, :], moments[:, j, 0:1], rstd[:, j:j + 1],
                                            ALU.subtract, ALU.mult).then_inc(y_ready, 1)
                assert c.n == PER, c.n

            units(dve, body)


def build(nc, x, src, dst, edge_attr, W1, b1, W2, b2, W_ih, b_ih, W_hh, b_hh, W_u, b_u, W_v, out, stop=99):
    A = dict(x=x, src=src, dst=dst, edge_attr=edge_attr, W1=W1, b1=b1, W2=W2, b2=b2, W_ih=W_ih, b_ih=b_ih,
             W_hh=W_hh, b_hh=b_hh, W_u=W_u, b_u=b_u, W_v=W_v, out=out)

    def dram(name, shape, dt=F32):
        return nc.dram_tensor(name, shape, dt, kind="Internal").ap()

    D = {"A": dram("A_rows", [NP, H]), "B": dram("B_rows", [NP, H]),
         "src_rows": dram("src_rows", [NTX, P]), "dst_rows": dram("dst_rows", [NTX, P])}
    D["first"], D["last"], D["upto"] = dram("first", [NT, 1]), dram("last", [NT, 1]), dram("upto", [NP + 1, 1])
    D["T2"] = dram("T2", [NT, PW])
    D["PT"] = dram("PT", [NT * P, PW])
    D["X1"], D["sv"] = dram("X1_rows", [NP, XW]), dram("sv_rows", [NP, NH])
    for t in range(NTAB):
        D[f"S{t}"] = dram(f"S{t}", [NP + P, UW])
    with ExitStack() as st:
        m = Mem(nc, st)
        K = {"ident": m.sb("ident", [P, P]), "before": m.sb("before", [P, P]),
             "nodeid_i": m.sb("nodeid_i", [P, NB], I32), "nodeid": m.sb("nodeid", [P, NB]),
             "srcT": m.sb("srcT", [P, NTX]), "dstT": m.sb("dstT", [P, NTX]),
             "srcT_i": m.sb("srcT_i", [P, NTX], I32), "dstT_i": m.sb("dstT_i", [P, NTX], I32),
             "W1abT": m.sb("W1abT", [P, HC, 2 * H]), "W1cT": m.sb("W1cT", [2 * ED, H]), "W2T": m.sb("W2T", [P, HC, H]),
             "WihT": m.sb("WihT", [P, HC, 3 * H]), "WhhT": m.sb("WhhT", [P, HC, 3 * H]),
             "WuvT": m.sb("WuvT", [P, HC, 2 * NH]),
             "any": m.sb("any", [P, NB]), "ends": m.sb("ends", [P, NB]), "own": m.sb("own", [P, NB]),
             "ends_row": m.sb("ends_row", [P, NB + UNR]), "own_row": m.sb("own_row", [P, NB + UNR]),
             "eps": m.sb("eps", [P, 1]), "neghalf": m.sb("neghalf", [P, 1]),
             "bgate": m.sb("bgate", [P, 4 * H]), "bu": m.sb("bu", [P, 2 * NH]), "b2row": m.sb("b2row", [1, H])}
        setup_phase(nc, K, D, A)
        if stop < 1:
            return
        layer0_phase(nc, K, D, A)
        if stop < 2:
            return
        nodes_phase(nc, K, D, A)
        if stop < 3:
            return
        places_phase(nc, K, D, A)
        layer1_phase(nc, K, D, A)
        if stop < 4:
            return
        merge_phase(nc, K, D, A)
        output_phase(nc, K, D, A)


def kernel(**inputs):
    import numpy as np
    import concourse.bacc as bacc
    from concourse.bass_utils import run_bass_kernel_spmd

    names = ["x", "src", "dst", "edge_attr_64", "L0_gnn_W1", "L0_gnn_b1", "L0_gnn_W2", "L0_gnn_b2", "L0_gnn_W_ih",
             "L0_gnn_b_ih", "L0_gnn_W_hh", "L0_gnn_b_hh", "L1_gnn_W_u", "L1_gnn_b_u", "L1_gnn_W_v"]
    nc = bacc.Bacc("TRN2", target_bir_lowering=False, num_devices=1)
    arrays, args = {}, []
    for name in names:
        a = np.ascontiguousarray(inputs[name])
        arrays[f"in_{name}"] = a
        args.append(nc.dram_tensor(f"in_{name}", a.shape, mybir.dt.from_np(a.dtype), kind="ExternalInput").ap())
    out = nc.dram_tensor("out_0", (N, H), F32, kind="ExternalOutput").ap()
    build(nc, *args, out)
    result = run_bass_kernel_spmd(nc, [arrays], core_ids=[0])
    return result.results[0]["out_0"]
```

```python
import concourse.bass as bass
from concourse import mybir
from contextlib import ExitStack

F32 = mybir.dt.float32
I32 = mybir.dt.int32
BF16 = mybir.dt.bfloat16
ALU = mybir.AluOpType
ACT = mybir.ActivationFunctionType
AX = mybir.AxisListType

P = 128
N, E, H, ED, NH = 6250, 100000, 256, 64, 8
NB = -(-N // P)
NP = NB * P
PAD = NP - 1
HALF = 8
GROUP = 2 * HALF
NG = -(-E // (P * GROUP))
NT = NG * GROUP
NTX = NT + 2 * GROUP
HC = H // P
CH = 7
CQ = NT // CH
UNR = 7
NI = NB // UNR
NTAB = 2
UW = H + 1
XW = H + NH
PW = H + 2 * NH
EPS = 1e-5
SLOPE = 0.2
LOW = -1e30
NSPLIT = 3
WIN = 2
PACK = 4
PACKED = NTX // PACK
assert NB + 1 < 64 and NTX % PACK == 0
assert NB % UNR == 0 and NT % CH == 0


def flat(ap):
    return ap.rearrange("p o n -> p (o n)")


class Mem:

    def __init__(self, nc, stack, prefix=""):
        self.nc, self.stack, self.prefix, self.sems = nc, stack, prefix, []

    def sb(self, name, shape, dt=F32):
        return self.stack.enter_context(self.nc.sbuf_tensor(self.prefix + name, shape, dt))

    def ps(self, name, shape, dt=F32):
        return self.stack.enter_context(self.nc.psum_tensor(self.prefix + name, shape, dt))

    def sem(self, name):
        self.sems.append(self.stack.enter_context(self.nc.semaphore(self.prefix + name)))
        return self.sems[-1]

    def clear_sems(self):
        with self.nc.Block() as block:
            @block.gpsimd
            def _(pool):
                pool.sem_clear(range(self.sems[0].num, self.sems[-1].num + 1))


class Chain:

    def __init__(self, engine, sem, base=0):
        self.engine, self.sem, self.base, self.n = engine, sem, base, 0

    def link(self, instruction):
        self.n += 1
        instruction.then_inc(self.sem, 1)
        self.engine.wait_ge(self.sem, self.base + self.n)


def segment_max(nc, chain, value, start, width, run):
    chain.link(nc.vector.tensor_tensor_scan(run[:, 0:width], start[:, 0:width], value[:, 0:width], LOW, ALU.add, ALU.max))
    return nc.vector.tensor_tensor_scan(value[:, 0:width][:, ::-1], start[:, 1:width + 1][:, ::-1], run[:, 0:width][:, ::-1],
                                        LOW, ALU.add, ALU.max)


def running_sums(nc, chain, a, b, width):
    d = 1
    while d < width:
        chain.link(nc.vector.tensor_copy(b[:, 0:d], a[:, 0:d]))
        chain.link(nc.vector.tensor_tensor(b[:, d:width], a[:, d:width], a[:, 0:width - d], ALU.add))
        a, b, d = b, a, 2 * d
    return a


def split_float(nc, chain, source, rest, parts):
    chain.link(nc.vector.tensor_copy(parts[0], source))
    chain.link(nc.vector.tensor_tensor(rest, source, parts[0], ALU.subtract))
    chain.link(nc.vector.tensor_copy(parts[1], rest))
    chain.link(nc.vector.tensor_tensor(parts[2], rest, parts[1], ALU.subtract))


def window_blocks(nc, pe, K, at):
    word = pe.value_load(K["blocks"][0:1, bass.ds(at, 1)], min_val=0, max_val=64 ** PACK - 1)
    return [nc.s_assert_within((word // 64 ** n) % 64, 0, NB - 1, skip_runtime_bounds_check_because="a rank is below the number of nodes")
            for n in range(PACK)]


def setup_phase(nc, K, D, A):
    CLEAR = NSPLIT * H * (NP + P) // P // 6
    with ExitStack() as st:
        m = Mem(nc, st, "su_")
        rawi = {"src": m.sb("srci", [CQ, CH, P], I32), "dst": m.sb("dsti", [CQ, CH, P], I32)}
        rawf = {"src": m.sb("srcf", [CQ, CH, P]), "dst": m.sb("dstf", [CQ, CH, P])}
        padrow = m.sb("padrow", [NTX - NT, P])
        locpad = m.sb("locpad", [NTX - NT, P], BF16)
        minus = m.sb("minus", [1, P])
        w1 = m.sb("w1", [P, HC, 2 * H + ED])
        w1c2 = m.sb("w1c2", [P, HC, 2 * ED])
        w2 = m.sb("w2", [P, HC, H])
        wih = m.sb("wih", [P, 3 * HC, H])
        whh = m.sb("whh", [P, 3 * HC, H])
        wuv = m.sb("wuv", [2 * NH, H])
        W1abT = m.sb("W1abT", [P, HC, 2 * H])
        zeros = m.sb("zeros", [P, CLEAR // 2])
        bias1 = m.sb("bias1", [P, H])
        xs = m.sb("xs", [P, UNR, H])
        xT = m.sb("xT", [P, UNR, H])
        a_rows = m.sb("a_rows", [P, UNR, H])
        b_rows = m.sb("b_rows", [P, UNR, H])
        b_rest = m.sb("b_rest", [P, UNR, H])
        parts = m.sb("parts", [P, UNR, NSPLIT * H], BF16)
        bhh = m.sb("bhh", [P, 2 * H])
        upto = m.sb("upto", [P, P])
        under = m.sb("under", [P, P])
        ones = m.sb("ones", [P, P])
        prev = m.sb("prev", [CQ, CH, P])
        fresh = m.sb("fresh", [CQ, CH, P])
        freshT = m.sb("freshT", [P, NT])
        count = m.sb("count", [CQ, CH, P])
        total = m.sb("total", [CQ, CH])
        run = [m.sb(f"run{i}", [CQ, CH]) for i in range(2)]
        before = m.sb("before", [CQ, CH])
        rank0 = m.sb("rank0", [CQ, CH])
        rank0_i = m.sb("rank0_i", [CQ, CH], I32)
        block = m.sb("block", [CQ, CH])
        shift = m.sb("shift", [CQ, CH])
        loc16 = m.sb("loc16", [CQ, CH, P], BF16)
        blockT = m.sb("blockT", [CH, CQ // PACK, PACK])
        word = m.sb("word", [CH, CQ // PACK])
        word_i = m.sb("word_i", [CH, CQ // PACK], I32)
        node = m.sb("node", [P, NB])
        column = m.sb("column", [P, P])
        node_i = m.sb("node_i", [P, NB], I32)
        column_i = m.sb("column_i", [P, P], I32)
        hi_i = m.sb("hi_i", [CQ, CH], I32)
        lo_i = m.sb("lo_i", [CQ, CH], I32)
        hi = m.sb("hi", [CQ, CH])
        lo = m.sb("lo", [CQ, CH])
        hotp = m.sb("hotp", [CQ, CH, P])
        hotb = m.sb("hotb", [CQ, CH, NB])
        hist = m.sb("hist", [P, NB])
        sums = [m.sb(f"sums{i}", [P, NB]) for i in range(2)]
        tile = m.sb("tile", [P, NB])
        tile_i = m.sb("tile_i", [P, NB], I32)
        rows = m.sb("rows", [P, NB, P])
        within = m.sb("within", [P, NB])
        edges_to = m.sb("edges_to", [P, NB])
        edges_before = m.sb("edges_before", [P, NB])
        begin = m.sb("begin", [P, NB])
        full = m.sb("full", [P, NB])
        cross = m.sb("cross", [P, NB])
        rank_i = m.sb("rank_i", [P, NB], I32)
        zero = m.sb("zero", [1, 1])

        psJ = [m.ps(f"psJ{i}", [P, 512]) for i in range(2)]
        psR = m.ps("psR", [P, 512])
        psK = m.ps("psK", [P, 512])
        psX = [m.ps(f"psX{i}", [P, 512]) for i in range(2)]
        psA = [m.ps(f"psA{i}", [P, 512]) for i in range(2)]
        edges_in, weights_in, bias_in = m.sem("edges_in"), m.sem("weights_in"), m.sem("bias_in")
        consts, masks, floats, rows_out = m.sem("consts"), m.sem("masks"), m.sem("floats"), m.sem("rows_out")
        prev_in, turned, kept, dve_step = m.sem("prev_in"), m.sem("turned"), m.sem("kept"), m.sem("dve_step")
        x_in = [m.sem(f"x_in{j}") for j in range(UNR)]
        x_turned, xT_ready, ab_done = m.sem("x_turned"), m.sem("xT_ready"), m.sem("ab_done")
        a_ready, b_ready, parts_ready = m.sem("a_ready"), m.sem("b_ready"), m.sem("parts_ready")
        hi_ready, rest_ready = m.sem("hi_ready"), m.sem("rest_ready")
        a_out = [m.sem(f"a_out{j}") for j in range(UNR)]
        b_out, gathered = K["b_out"], K["edges_gathered"]
        tables_clear, ranked = m.sem("tables_clear"), m.sem("ranked")
        ask, answer = m.sem("ask"), m.sem("answer")
        loc_out, words_out, words_in = m.sem("loc_out"), m.sem("words_out"), m.sem("words_in")
        edges_ready, edges_out, before_in = m.sem("edges_ready"), m.sem("edges_out"), m.sem("before_in")

        jobs = []
        for o in range(HC):
            cols = slice(o * P, (o + 1) * P)
            for k in range(2 * HC):
                at = (k // HC) * H + o * P
                jobs.append((w1[:, o, k * P:(k + 1) * P], W1abT[:, k % HC, at:at + P]))
            jobs.append((w1c2[:, o, :], K["W1cT"][:, cols]))
            jobs += [(w2[:, o, k * P:(k + 1) * P], K["W2T"][:, k, cols]) for k in range(HC)]
        for o in range(3 * HC):
            for k in range(HC):
                jobs.append((wih[:, o, k * P:(k + 1) * P], K["WihT"][:, k, o * P:(o + 1) * P]))
                jobs.append((whh[:, o, k * P:(k + 1) * P], K["WhhT"][:, k, o * P:(o + 1) * P]))
        jobs += [(wuv[:, k * P:(k + 1) * P], K["WuvT"][:, k, :]) for k in range(HC)]

        CLEARS = NTAB * 5 + 6 + 1
        phase = ExitStack()
        blk = phase.enter_context(nc.Block())

        @blk.sync
        def _(sp):
            sp.wait_ge(consts, 2)
            whole = (CH - 1) * CQ * P
            tail = (E - whole) // P
            for name in ("dst", "src"):
                e = A[name]
                sp.dma_start(rawi[name][:, 0:CH - 1, :],
                             e[0:whole].rearrange("(c q p) -> q c p", q=CQ, p=P)).then_inc(edges_in, 16)
                sp.dma_start(rawi[name][0:tail, CH - 1, :],
                             e[whole:whole + tail * P].rearrange("(q p) -> q p", p=P)).then_inc(edges_in, 16)
                sp.dma_start(rawi[name][tail:tail + 1, CH - 1, 0:E - whole - tail * P],
                             e[whole + tail * P:E].rearrange("(q p) -> q p", q=1)).then_inc(edges_in, 16)
            sp.dma_start(w1[:, :, :], A["W1"].rearrange("(o p) k -> p o k", p=P)).then_inc(weights_in, 16)
            for n in range(2):
                sp.dma_start(w1c2[:, :, n * ED:(n + 1) * ED],
                             A["W1"][:, 2 * H:2 * H + ED].rearrange("(o p) k -> p o k", p=P)).then_inc(weights_in, 16)
            for j in range(UNR):
                sp.dma_start(xs[:, j, :], A["x"][j * P:(j + 1) * P, :]).then_inc(x_in[j], 16)
            sp.dma_start(w2[:, :, :], A["W2"].rearrange("(o p) k -> p o k", p=P)).then_inc(weights_in, 16)
            sp.dma_start(wih[:, :, :], A["W_ih"].rearrange("(o p) k -> p o k", p=P)).then_inc(weights_in, 16)
            sp.dma_start(whh[:, :, :], A["W_hh"].rearrange("(o p) k -> p o k", p=P)).then_inc(weights_in, 16)
            sp.dma_start(wuv[0:NH, :], A["W_u"]).then_inc(weights_in, 16)
            sp.dma_start(wuv[NH:2 * NH, :], A["W_v"]).then_inc(weights_in, 16)

            def load_x(i, j, rows):
                sp.wait_ge(x_turned, i * UNR + (j + 1))
                sp.dma_start(xs[0:rows, j, :], A["x"][bass.ds(i * (UNR * P) + (UNR + j) * P, rows), :]).then_inc(x_in[j], 16)

            def store_a(i, j):
                sp.wait_ge(a_ready, i * UNR + (j + 1))
                sp.dma_start(D["A"][bass.ds(i * (UNR * P) + j * P, P), :], a_rows[:, j, :]).then_inc(a_out[j], 16)

            with sp.Fori(0, NI - 2) as i:
                for j in range(UNR):
                    load_x(i, j, P)
                    store_a(i, j)
            for j in range(UNR):
                load_x(NI - 2, j, P if j < UNR - 1 else N - (NB - 1) * P)
                store_a(NI - 2, j)
            for j in range(UNR):
                store_a(NI - 1, j)
            for j in range(UNR):
                sp.wait_ge(a_out[j], 16 * NI)

        @blk.gpsimd
        def _(pool):
            nc.gpsimd.memset(K["ident"][:, :], 0.0).then_inc(masks, 1)
            for mat in (K["before"], upto, under):
                nc.gpsimd.memset(mat[:, :], 1.0).then_inc(masks, 1)
            nc.gpsimd.iota(node_i[:, :], pattern=[[P, NB]], base=0, channel_multiplier=1).then_inc(masks, 1)
            nc.gpsimd.iota(column_i[:, :], pattern=[[1, P]], base=0, channel_multiplier=0).then_inc(masks, 1)
            pool.wait_ge(masks, 6)
            for mat, op, fill, sign in ((K["ident"], ALU.not_equal, 1.0, 1), (K["before"], ALU.is_gt, 0.0, 1),
                                        (upto, ALU.is_ge, 0.0, -1), (under, ALU.is_gt, 0.0, -1)):
                nc.gpsimd.affine_select(out=mat[:, :], in_=mat[:, :], compare_op=op, fill=fill, base=0,
                                        pattern=[[-sign, P]], channel_multiplier=sign).then_inc(masks, 1)
            pool.wait_ge(ask, 4)
            for b in range(NB):
                pool.indirect_dma_start(rows[:, b, :], None, D["dst_rows"],
                                        bass.IndirectOffsetOnAxis(ap=tile_i[:, b:b + 1], axis=0)).then_inc(gathered, 16)
            pool.wait_ge(gathered, 16 * NB)
            pool.wait_ge(ranked, 1)
            pool.wait_ge(tables_clear, 16 * CLEARS)
            for b in range(NB):
                pool.wait_ge(parts_ready, b + 1)
                pool.indirect_dma_start(D["B"], bass.IndirectOffsetOnAxis(ap=rank_i[:, b:b + 1], axis=0),
                                        parts[:, b % UNR, :], None).then_inc(b_out[b % UNR], 16)
            for j in range(UNR):
                pool.wait_ge(b_out[j], 16 * NI)

        @blk.scalar
        def _(act):
            act.wait_ge(floats, 1)
            act.dma_start(D["dst_rows"][1:NT + 1, :].rearrange("(c q) p -> q c p", q=CQ), rawf["dst"][:, :, :]).then_inc(rows_out, 16)
            act.dma_start(D["dst_rows"][0:1, :], minus[:, :]).then_inc(rows_out, 16)
            act.wait_ge(rows_out, 32)
            flat_dst = D["dst_rows"].rearrange("t p -> (t p)")
            act.dma_start(prev[:, :, :], flat_dst[P - 1:P - 1 + NT * P].rearrange("(c q p) -> q c p", q=CQ, p=P)).then_inc(prev_in, 16)
            act.wait_ge(floats, 2)
            act.dma_start(D["src_rows"][0:NT, :].rearrange("(c q) p -> q c p", q=CQ), rawf["src"][:, :, :]).then_inc(rows_out, 16)
            act.dma_start(D["src_rows"][NT:NTX, :], padrow[:, :]).then_inc(rows_out, 16)
            with nc.allow_non_contiguous_dma(reason="one word of each tile"):
                act.dma_start(D["last"], D["dst_rows"][1:NT + 1, P - 1:P]).then_inc(rows_out, 16)
            act.dma_start(bias1[:, :], A["b1"].partition_broadcast(P)).then_inc(bias_in, 16)
            act.dma_start(K["bgate"][:, 0:3 * H], A["b_ih"].partition_broadcast(P)).then_inc(bias_in, 16)
            act.dma_start(bhh[:, :], A["b_hh"][0:2 * H].partition_broadcast(P)).then_inc(bias_in, 16)
            act.dma_start(K["bgate"][:, 3 * H:4 * H], A["b_hh"][2 * H:3 * H].partition_broadcast(P)).then_inc(bias_in, 16)
            act.dma_start(K["bu"][:, 0:NH], A["b_u"].partition_broadcast(P)).then_inc(bias_in, 16)
            act.dma_start(K["b2row"][:, :], A["b2"].rearrange("(o h) -> o h", o=1)).then_inc(bias_in, 16)
            b_table = D["B"].rearrange("n w -> (n w)").rearrange("(p r w) -> p r w", p=P, w=CLEAR)
            for r in range(b_table.shape[1]):
                act.dma_start(b_table[:, r, :], zeros[:, :].bitcast(BF16)).then_inc(tables_clear, 16)
            act.dma_start(D["sv"].rearrange("n w -> (n w)").rearrange("(p w) -> p w", p=P), zeros[:, 0:(NP + P) * NH // P]).then_inc(tables_clear, 16)
            for t in range(NTAB):
                v = D[f"S{t}"].rearrange("n w -> (n w)").rearrange("(p r w) -> p r w", p=P, w=2570)
                for r in range(v.shape[1]):
                    act.dma_start(v[:, r, :], zeros[:, 0:2570]).then_inc(tables_clear, 16)
            act.wait_ge(ask, 6)
            act.dma_start(D["loc_rows"][0:NT, :].rearrange("(c q) p -> q c p", q=CQ), loc16[:, :, :]).then_inc(loc_out, 16)
            act.dma_start(D["loc_rows"][NT:NTX, :], locpad[:, :]).then_inc(loc_out, 16)
            act.wait_ge(ask, 7)
            act.dma_start(D["blocks"].rearrange("(c n) o -> c (n o)", c=CH), word_i[:, :]).then_inc(words_out, 16)
            act.wait_ge(words_out, 16)
            act.dma_start(K["blocks"][0:1, 0:NT // PACK], D["blocks"].rearrange("n o -> o n")).then_inc(words_in, 16)
            act.wait_ge(edges_ready, 1)
            with nc.allow_non_contiguous_dma(reason="the nodes are over partitions"):
                act.dma_start(D["upto"][0:1, :], zero[:, :]).then_inc(edges_out, 16)
                act.dma_start(D["upto"][1:NP + 1, :].rearrange("(b p) o -> p (b o)", p=P), edges_to[:, :]).then_inc(edges_out, 16)
                act.wait_ge(edges_out, 32)
                act.dma_start(edges_before[:, :], D["upto"][0:NP, :].rearrange("(b p) o -> p (b o)", p=P)).then_inc(before_in, 16)
            def keep(i, j):
                act.wait_ge(b_ready, i * UNR + (j + 1))
                act.wait_ge(a_out[j], i * 16)
                nc.scalar.copy(a_rows[:, j, :], psA[j % 2][:, 0:H]).then_inc(a_ready, 1)
                act.wait_ge(b_out[j], i * 16)
                nc.scalar.copy(parts[:, j, 0:H], b_rows[:, j, :]).then_inc(hi_ready, 1)

            with act.Fori(0, NI) as i:
                for j in range(UNR):
                    act.wait_ge(x_turned, i * UNR + (j + 1))
                    nc.scalar.copy(xT[:, j, :], psX[j % 2][:, 0:H]).then_inc(xT_ready, 1)
                    if j > 0:
                        keep(i, j - 1)
                keep(i, UNR - 1)
            act.wait_ge(tables_clear, 16 * CLEARS)
            act.wait_ge(rows_out, 80)
            act.wait_ge(loc_out, 32)
            act.wait_ge(words_in, 16)

        @blk.tensor
        def _(pe):
            def turn(source, target):
                nrows, ncols = source.shape
                return nc.tensor.transpose(target[0:ncols, 0:nrows], source, K["ident"][0:nrows, 0:nrows])

            pe.wait_ge(masks, 10)
            pe.wait_ge(ask, 1)
            for c in range(4):
                turn(fresh[:, c, :], psR[:, c * CQ:(c + 1) * CQ])
            for c in range(4, CH):
                t = turn(fresh[:, c, :], psK[:, (c - 4) * CQ:(c - 3) * CQ])
            t.then_inc(answer, 1)
            pe.wait_ge(ask, 2)
            for c in range(CH):
                t = nc.tensor.matmul(psR[:, 0:NB], hotp[:, c, :], hotb[:, c, :], start=(c == 0), stop=(c == CH - 1))
            t.then_inc(answer, 1)
            pe.wait_ge(ask, 3)
            nc.tensor.matmul(psR[:, 0:NB], upto[:, :], hist[:, :], start=True, stop=False)
            nc.tensor.matmul(psR[:, 0:NB], ones[:, :], sums[1][:, :], start=False, stop=True).then_inc(answer, 1)
            pe.wait_ge(ask, 4)
            for c in range(CH):
                bank, at = (psR, c) if c < 4 else (psK, c - 4)
                t = nc.tensor.matmul(bank[0:CQ, at * P:(at + 1) * P], freshT[:, c * CQ:(c + 1) * CQ], upto[:, :], start=True, stop=True)
            t.then_inc(answer, 1)
            pe.wait_ge(ask, 5)
            nc.tensor.matmul(psR[0:CQ, 0:CH], under[0:CQ, 0:CQ], total[:, :], start=True, stop=False)
            nc.tensor.matmul(psR[0:CQ, 0:CH], ones[0:CQ, 0:CQ], before[:, :], start=False, stop=True).then_inc(answer, 1)
            pe.wait_ge(ask, 6)
            for c in range(4):
                turn(count[:, c, :], psR[:, c * CQ:(c + 1) * CQ])
            for c in range(4, CH):
                turn(count[:, c, :], psK[:, (c - 4) * CQ:(c - 3) * CQ])
            turn(block[:, :], psK[:, 3 * CQ:4 * CQ]).then_inc(answer, 1)
            pe.wait_ge(ask, 7)
            for c in range(4):
                turn(rawf["src"][:, c, :], psR[:, c * CQ:(c + 1) * CQ])
            for c in range(4, CH):
                t = turn(rawf["src"][:, c, :], psK[:, (c - 4) * CQ:(c - 3) * CQ])
            t.then_inc(answer, 1)
            pe.wait_ge(weights_in, 128)
            for n, (source, _) in enumerate(jobs):
                if n >= 2:
                    pe.wait_ge(kept, n - 1)
                turn(source, psJ[n % 2]).then_inc(turned, 1)
            pe.wait_ge(kept, len(jobs))
            pe.wait_ge(ask, 8)
            nc.tensor.matmul(psR[:, 0:NB], upto[:, :], K["any"][:, :], start=True, stop=False)
            nc.tensor.matmul(psR[:, 0:NB], ones[:, :], sums[1][:, :], start=False, stop=True).then_inc(answer, 1)
            with pe.Fori(0, NI) as i:
                def turn_x(j):
                    pe.wait_ge(xT_ready, i * UNR + max(j - 1, 0))
                    pe.wait_ge(x_in[j], i * 16 + 16)
                    for k in range(HC):
                        t = nc.tensor.transpose(psX[j % 2][:, k * P:(k + 1) * P], xs[:, j, k * P:(k + 1) * P], K["ident"][:, :])
                    t.then_inc(x_turned, 1)
                turn_x(0)
                for j in range(UNR):
                    if j < UNR - 1:
                        turn_x(j + 1)
                    pe.wait_ge(xT_ready, i * UNR + (j + 1))
                    pe.wait_ge(a_ready, i * UNR + max(j - 1, 0))
                    for k in range(HC):
                        t = nc.tensor.matmul(psA[j % 2][:, :], xT[:, j, k * P:(k + 1) * P], W1abT[:, k, :],
                                             start=(k == 0), stop=(k == HC - 1))
                    t.then_inc(ab_done, 1)

        @blk.vector
        def _(dve):
            c = Chain(dve, dve_step)
            link = c.link

            def asked(n, ins=None):
                ins.then_inc(ask, 1)
                dve.wait_ge(answer, n)

            nc.vector.memset(rawi["dst"][:, :, :], PAD).then_inc(consts, 1)
            nc.vector.memset(rawi["src"][:, :, :], PAD).then_inc(consts, 1)
            nc.vector.memset(minus[:, :], -1.0)
            nc.vector.memset(padrow[:, :], float(PAD))
            nc.vector.memset(locpad[:, :], 0.0)
            nc.vector.memset(zero[:, :], 0.0)
            nc.vector.memset(ones[:, :], 1.0)
            nc.vector.memset(K["bu"][:, NH:2 * NH], 0.0)
            nc.vector.memset(K["eps"][:, :], EPS)
            nc.vector.memset(K["neghalf"][:, :], -0.5)
            nc.vector.memset(K["srcT"][:, NT:NTX], float(PAD))
            nc.vector.memset(K["locT"][:, NT:NTX], 0.0)
            nc.vector.memset(K["blocks"][:, :], 0)
            nc.vector.memset(K["own_row"][:, NB:], 0.0)
            nc.vector.memset(K["ends_row"][:, NB:], 0.0)
            nc.vector.memset(zeros[:, :], 0.0)
            dve.wait_ge(edges_in, 96)
            nc.vector.tensor_copy(rawf["dst"][:, :, :], rawi["dst"][:, :, :]).then_inc(floats, 1)
            nc.vector.tensor_copy(rawf["src"][:, :, :], rawi["src"][:, :, :]).then_inc(floats, 1)
            nc.vector.tensor_scalar(hi_i[:, :], rawi["dst"][:, :, 0], 7, None, ALU.arith_shift_right)
            link(nc.vector.tensor_scalar(lo_i[:, :], rawi["dst"][:, :, 0], P - 1, None, ALU.bitwise_and))
            nc.vector.tensor_copy(hi[:, :], hi_i[:, :])
            nc.vector.tensor_copy(lo[:, :], lo_i[:, :])
            dve.wait_ge(masks, 6)
            nc.vector.tensor_copy(node[:, :], node_i[:, :])
            link(nc.vector.tensor_copy(column[:, :], column_i[:, :]))
            nc.vector.tensor_scalar(K["winid"][:, 0:1], node[:, 0:1], 0.0, None, ALU.add)
            nc.vector.tensor_scalar(K["winid"][:, 1:2], node[:, 0:1], float(P), None, ALU.add)
            nc.vector.tensor_scalar(K["spare"][:, :], node[:, 0:1], float(NP), None, ALU.add)
            nc.vector.tensor_tensor(hotp[:, :, :], column[0:CQ, :].unsqueeze(1).to_broadcast([CQ, CH, P]),
                                    lo[:, :].unsqueeze(2).to_broadcast([CQ, CH, P]), ALU.is_equal)
            link(nc.vector.tensor_tensor(hotb[:, :, :], column[0:CQ, 0:NB].unsqueeze(1).to_broadcast([CQ, CH, NB]),
                                         hi[:, :].unsqueeze(2).to_broadcast([CQ, CH, NB]), ALU.is_equal))
            dve.wait_ge(prev_in, 16)
            asked(1, nc.vector.tensor_tensor(fresh[:, :, :], rawf["dst"][:, :, :], prev[:, :, :], ALU.not_equal))
            nc.vector.tensor_copy(freshT[:, 0:4 * CQ], psR[:, 0:4 * CQ])
            asked(2, nc.vector.tensor_copy(freshT[:, 4 * CQ:NT], psK[:, 0:3 * CQ]))
            nc.vector.tensor_scalar(K["startT"][:, :], freshT[:, :], LOW, None, ALU.mult)

            def prefix(n, values):
                link(nc.vector.tensor_copy(sums[0][:, :], values))
                total_to = running_sums(nc, c, sums[0], sums[1], NB)
                assert total_to is sums[0]
                asked(n, nc.vector.tensor_tensor(sums[1][:, :], sums[0][:, :], values, ALU.subtract))

            link(nc.vector.tensor_copy(hist[:, :], psR[:, 0:NB]))
            prefix(3, hist[:, :])
            link(nc.vector.tensor_scalar(tile[:, :], psR[:, 0:NB], -1.0, 0.0, ALU.add, ALU.max))
            asked(4, nc.vector.tensor_scalar(tile_i[:, :], tile[:, :], 1.0, None, ALU.add))
            nc.vector.tensor_copy(count[:, 0:4, :], psR[0:CQ, :].rearrange("q (c p) -> q c p", p=P))
            link(nc.vector.tensor_copy(count[:, 4:CH, :], psK[0:CQ, 0:3 * P].rearrange("q (c p) -> q c p", p=P)))
            link(nc.vector.tensor_copy(total[:, :], count[:, :, P - 1]))
            link(nc.vector.tensor_copy(run[0][:, :], total[:, :]))
            run_to = running_sums(nc, c, run[0], run[1], CH)
            asked(5, nc.vector.tensor_tensor(before[:, :], run_to[:, :], total[:, :], ALU.subtract))
            link(nc.vector.tensor_copy(total[:, :], psR[0:CQ, 0:CH]))
            link(nc.vector.tensor_tensor(rank0[:, :], total[:, :], fresh[:, :, 0], ALU.add))
            link(nc.vector.tensor_scalar(rank0_i[:, :], rank0[:, :], -1.0, None, ALU.add))
            link(nc.vector.tensor_scalar(hi_i[:, :], rank0_i[:, :], 7, None, ALU.arith_shift_right))
            link(nc.vector.tensor_scalar(block[:, :], hi_i[:, :], float(NB - 1), None, ALU.min))
            link(nc.vector.tensor_scalar(shift[:, :], block[:, :], -float(P), -1.0, ALU.mult, ALU.add))
            link(nc.vector.tensor_tensor(shift[:, :], shift[:, :], total[:, :], ALU.add))
            link(nc.vector.tensor_tensor(count[:, :, :], count[:, :, :], shift[:, :].unsqueeze(2).to_broadcast([CQ, CH, P]), ALU.add))
            asked(6, nc.vector.tensor_copy(loc16[:, :, :], count[:, :, :]))
            nc.vector.tensor_copy(K["locT"][:, 0:4 * CQ], psR[:, 0:4 * CQ])
            nc.vector.tensor_copy(K["locT"][:, 4 * CQ:NT], psK[:, 0:3 * CQ])
            link(nc.vector.tensor_copy(blockT[:, :, :], psK[0:CH, 3 * CQ:4 * CQ].rearrange("c (n k) -> c n k", k=PACK)))
            link(nc.vector.tensor_copy(word[:, :], blockT[:, :, PACK - 1]))
            for k in reversed(range(PACK - 1)):
                link(nc.vector.scalar_tensor_tensor(word[:, :], word[:, :], 64.0, blockT[:, :, k], ALU.mult, ALU.add))
            asked(7, nc.vector.tensor_copy(word_i[:, :], word[:, :]))
            nc.vector.tensor_copy(K["srcT"][:, 0:4 * CQ], psR[:, 0:4 * CQ])
            link(nc.vector.tensor_copy(K["srcT"][:, 4 * CQ:NT], psK[:, 0:3 * CQ]))
            for n, (source, target) in enumerate(jobs):
                nrows, ncols = source.shape
                dve.wait_ge(turned, n + 1)
                nc.vector.tensor_copy(target, psJ[n % 2][0:ncols, 0:nrows]).then_inc(kept, 1)
            dve.wait_ge(bias_in, 96)
            link(nc.vector.tensor_tensor(K["bgate"][:, 0:2 * H], K["bgate"][:, 0:2 * H], bhh[:, :], ALU.add))
            dve.wait_ge(gathered, 16 * NB)
            link(nc.vector.tensor_tensor(rows[:, :, :], rows[:, :, :], node[:, :].unsqueeze(2).to_broadcast([P, NB, P]), ALU.is_le))
            link(nc.vector.tensor_reduce(within[:, :], rows[:, :, :], AX.X, ALU.add))
            link(nc.vector.tensor_scalar(begin[:, :], tile[:, :], float(P), None, ALU.mult))
            nc.vector.tensor_tensor(edges_to[:, :], begin[:, :], within[:, :], ALU.add).then_inc(edges_ready, 1)
            dve.wait_ge(before_in, 16)
            dve.wait_ge(edges_ready, 1)
            link(nc.vector.tensor_tensor(K["any"][:, :], edges_to[:, :], edges_before[:, :], ALU.is_gt))
            prefix(8, K["any"][:, :])
            link(nc.vector.tensor_scalar(cross[:, :], psR[:, 0:NB], -1.0, K["spare"][:, 0:1], ALU.add, ALU.subtract))
            link(nc.vector.tensor_tensor(cross[:, :], cross[:, :], K["any"][:, :], ALU.mult))
            link(nc.vector.tensor_scalar(K["rank"][:, :], cross[:, :], K["spare"][:, 0:1], None, ALU.add))
            nc.vector.tensor_copy(rank_i[:, :], K["rank"][:, :]).then_inc(ranked, 1)
            def split(i, j):
                dve.wait_ge(hi_ready, i * UNR + (j + 1))
                nc.vector.tensor_tensor(b_rest[:, j, :], b_rows[:, j, :], parts[:, j, 0:H], ALU.subtract).then_inc(rest_ready, 1)
                dve.wait_ge(rest_ready, i * (2 * UNR) + (2 * j + 1))
                nc.vector.tensor_copy(parts[:, j, H:2 * H], b_rest[:, j, :]).then_inc(rest_ready, 1)
                dve.wait_ge(rest_ready, i * (2 * UNR) + (2 * j + 2))
                nc.vector.tensor_tensor(parts[:, j, 2 * H:3 * H], b_rest[:, j, :], parts[:, j, H:2 * H],
                                        ALU.subtract).then_inc(parts_ready, 1)

            with dve.Fori(0, NI) as i:
                for j in range(UNR):
                    dve.wait_ge(ab_done, i * UNR + (j + 1))
                    nc.vector.tensor_tensor(b_rows[:, j, :], psA[j % 2][:, H:2 * H], bias1[:, :], ALU.add).then_inc(b_ready, 1)
                    if j > 0:
                        split(i, j - 1)
                split(i, UNR - 1)
            link(nc.vector.tensor_scalar(full[:, :], within[:, :], float(P), None, ALU.is_equal))
            dve.wait_ge(ranked, 1)
            link(nc.vector.tensor_tensor(cross[:, :], edges_before[:, :], begin[:, :], ALU.is_lt))
            link(nc.vector.tensor_tensor(cross[:, :], cross[:, :], full[:, :], ALU.max))
            link(nc.vector.tensor_tensor(K["ends"][:, :], cross[:, :], K["any"][:, :], ALU.mult))
            link(nc.vector.tensor_scalar(cross[:, :], full[:, :], -1.0, 1.0, ALU.mult, ALU.add))
            link(nc.vector.tensor_tensor(K["own"][:, :], cross[:, :], K["any"][:, :], ALU.mult))
            link(nc.vector.tensor_scalar(K["own_row"][:, 0:NB], edges_to[:, :], -1.0, 0.0, ALU.add, ALU.max))
            link(nc.vector.tensor_tensor(tile[:, :], tile[:, :], cross[:, :], ALU.subtract))
            link(nc.vector.tensor_scalar(K["ends_row"][:, 0:NB], tile[:, :], 0.0, None, ALU.max))
        phase.close()
        m.clear_sems()


def layer0_phase(nc, K, D, A):
    with ExitStack() as st:
        m = Mem(nc, st, "l0_")
        SLOTS = HALF
        ga = m.sb("ga", [P, SLOTS, H])
        table = m.sb("table", [P, NB + 1, NSPLIT * H], BF16)
        locb = [m.sb(f"locb{h}", [P, HALF, P], BF16) for h in range(2)]
        onehot = [m.sb(f"onehot{h}", [P, WIN, HALF, P], BF16) for h in range(2)]
        gsrc = [m.sb(f"gsrc{h}", [P, HALF], I32) for h in range(2)]
        sink = [m.sb(f"sink{h}", [P, HALF], I32) for h in range(2)]
        srcb = [m.sb(f"srcb{h}", [P, HALF, P]) for h in range(2)]
        same = [m.sb(f"same{h}", [P, HALF, P]) for h in range(2)]
        attr = [m.sb(f"attr{h}", [P, HALF, ED]) for h in range(2)]
        earlier = m.sb("earlier", [P, HALF, P])
        dup = m.sb("dup", [P, HALF])
        togo = m.sb("togo", [P, HALF])
        attrT = [m.sb(f"attrT{q}", [2 * ED, 2 * P]) for q in range(2)]
        hid = m.sb("hid", [P, 4, UW])
        msum = m.sb("msum", [P, 4, UW])
        psT = [m.ps(f"psT{q}", [P, 512]) for q in range(2)]
        psC = [m.ps(f"psC{q}", [P, 512]) for q in range(4)]
        psU = [m.ps(f"psU{q}", [P, 512]) for q in range(2)]
        gathered = [m.sem(f"gathered{s}") for s in range(SLOTS)]
        scattered = [m.sem(f"scattered{t}") for t in range(NTAB)]
        src_in = [m.sem(f"src_in{h}") for h in range(2)]
        table_in = m.sem("table_in")
        onehot_ready = m.sem("onehot_ready")
        attr_in = [m.sem(f"attr_in{h}") for h in range(2)]
        index_ready = m.sem("index_ready")
        same_ready = m.sem("same_ready")
        dve_step = m.sem("dve_step")
        pre_ready = m.sem("pre_ready")
        hid_ready = m.sem("hid_ready")
        attr_turned = m.sem("attr_turned")
        attrT_ready = m.sem("attrT_ready")
        c_done = m.sem("c_done")
        agg_done = m.sem("agg_done")
        msum_ready = m.sem("msum_ready")
        ones = m.sem("ones")
        pool_waited = m.sem("pool_waited")
        attr_end = m.sem("attr_end")
        block = st.enter_context(nc.Block())

        def pc(t):
            return psC[t % 4][:, 0:H]

        @block.sync
        def _(sp):
            def src_rows(h, row):
                sp.dma_start(srcb[h][:, :, :].rearrange("p t e -> p (t e)"),
                             D["src_rows"][row, :].rearrange("t e -> (t e)").partition_broadcast(P)).then_inc(src_in[h], 16)
                sp.dma_start(locb[h][:, :, :].rearrange("p t e -> p (t e)"),
                             D["loc_rows"][row, :].rearrange("t e -> (t e)").partition_broadcast(P)).then_inc(src_in[h], 16)

            def attr_tiles(h, edge):
                sp.dma_start(attr[h][:, :, :],
                             A["edge_attr"][edge, :].rearrange("(t p) d -> p t d", p=P)).then_inc(attr_in[h], 16)

            sp.dma_start(table[:, :, :], D["B"].rearrange("(b p) w -> p b w", p=P)).then_inc(table_in, 16)
            for h in range(2):
                src_rows(h, slice(h * HALF, (h + 1) * HALF))
                attr_tiles(h, slice(h * HALF * P, (h + 1) * HALF * P))
            with sp.Fori(0, NG - 2) as g:
                for h in range(2):
                    sp.wait_ge(same_ready, g * 2 + (h + 1))
                    src_rows(h, bass.ds(g * GROUP + (GROUP + h * HALF), HALF))
                    sp.wait_ge(attr_turned, g * 4 + 2 * (h + 1))
                    attr_tiles(h, bass.ds(g * (GROUP * P) + (GROUP + h * HALF) * P, HALF * P))
            g = NG - 2
            for h in range(2):
                sp.wait_ge(same_ready, g * 2 + (h + 1))
                src_rows(h, slice((g + 1) * GROUP + h * HALF, (g + 1) * GROUP + (h + 1) * HALF))
                sp.wait_ge(attr_turned, g * 4 + 2 * (h + 1))
                first = (g + 1) * GROUP * P + h * HALF * P
                if h == 0:
                    attr_tiles(h, slice(first, first + HALF * P))
                else:
                    whole = (E - first) // P
                    sp.dma_start(attr[h][0:E - first - whole * P, whole, :],
                                 A["edge_attr"][first + whole * P:E, :]).then_inc(attr_end, 16)
                    sp.wait_ge(attr_end, 16)
                    sp.dma_start(attr[h][:, 0:whole, :],
                                 A["edge_attr"][first:first + whole * P, :].rearrange("(t p) d -> p t d", p=P)).then_inc(attr_in[h], 16)
            sp.wait_ge(same_ready, 2 * NG - 1)
            src_rows(0, slice(NT, NT + HALF))
            sp.wait_ge(attr_turned, 4 * NG - 2)
            attr_tiles(0, slice(0, HALF * P))
            sp.wait_ge(src_in[0], 32 * (NG + 1))
            sp.wait_ge(attr_in[0], 16 * (NG + 1))

        @block.gpsimd
        def _(pool):
            def gather(j):
                s, h = j % SLOTS, j // HALF
                pool.indirect_dma_start(ga[:, s, :], None, D["A"],
                                        bass.IndirectOffsetOnAxis(ap=gsrc[h][:, s:s + 1], axis=0)).then_inc(gathered[s], 16)

            pool.wait_ge(index_ready, 2)
            for j in range(SLOTS):
                gather(j)

            def group(g, last=False):
                for j in range(GROUP):
                    pool.wait_ge(msum_ready, g * GROUP + (j + 1))
                    pool.wait_ge(scattered[j % NTAB], g * (16 * GROUP // NTAB) + 16 * (j // NTAB))
                    pool.sem_inc(pool_waited, 1)
                    pool.indirect_dma_start(D[f"S{j % NTAB}"],
                                            bass.IndirectOffsetOnAxis(ap=sink[j // HALF][:, j % HALF:j % HALF + 1], axis=0),
                                            msum[:, j % 4, :], None, compute_op=ALU.add).then_inc(scattered[j % NTAB], 16)
                    if last and j >= HALF:
                        continue
                    if j == 0 or j == HALF:
                        pool.wait_ge(index_ready, g * 2 + (2 + j // HALF))
                    pool.wait_ge(hid_ready, g * GROUP + (j + 1))
                    pool.sem_inc(pool_waited, 1)
                    gather((j + SLOTS) % GROUP)

            with pool.Fori(0, NG - 1) as g:
                group(g)
            group(NG - 1, last=True)
            for t in range(NTAB):
                pool.wait_ge(scattered[t], 16 * NT // NTAB)
            for s in range(SLOTS):
                pool.wait_ge(gathered[s], 16 * (NT // SLOTS))

        @block.tensor
        def _(pe):
            def turn(g, q):
                h, at = q % 4 // 2, q % 2 * 4
                if q % 2 == 0:
                    pe.wait_ge(attr_in[h], g * 16 + 16 * (1 + q // 4))
                for n in range(2):
                    pair = attr[h][:, at + 2 * n:at + 2 * n + 2, :].rearrange("p t d -> p (t d)")
                    t = nc.tensor.transpose(psT[q % 2][:, n * P:(n + 1) * P], pair, K["ident"][:, :])
                t.then_inc(attr_turned, 1)

            def project(g, j):
                if j % 4 == 0:
                    pe.wait_ge(attrT_ready, g * 4 + (j // 4 + 1))
                side = slice(j % 2 * ED, (j % 2 + 1) * ED)
                nc.tensor.matmul(pc(j), attrT[j // 4 % 2][side, j % 4 // 2 * P:(j % 4 // 2 + 1) * P], K["W1cT"][side, :],
                                 start=True, stop=False)
                if j % HALF == 0:
                    pe.wait_ge(onehot_ready, g * 2 + (j // HALF + 1))
                for w in range(WIN):
                    for n in range(NSPLIT):
                        t = nc.tensor.matmul(pc(j), onehot[j // HALF % 2][:, w, j % HALF, :],
                                             flat(table[:, bass.ds(blocks[j % 4] + w, 1), n * H:(n + 1) * H]),
                                             start=False, stop=(w == WIN - 1 and n == NSPLIT - 1))
                t.then_inc(c_done, 1)

            turn(0, 0)
            turn(0, 1)
            pe.wait_ge(table_in, 16)
            blocks = window_blocks(nc, pe, K, 0)
            for j in range(4):
                project(0, j)
            with pe.Fori(0, NG) as g:
                for j in range(GROUP):
                    if j % 4 == 0:
                        blocks = window_blocks(nc, pe, K, g * (GROUP // PACK) + (j // 4 + 1))
                        pe.wait_ge(attrT_ready, g * 4 + (j // 4 + 1))
                        turn(g, j // 4 + 2)
                    pe.wait_ge(pre_ready, g * GROUP + (j + 1))
                    project(g, j + 4)
                    if j % HALF == 0:
                        pe.wait_ge(same_ready, g * 2 + (j // HALF + 1))
                    pe.wait_ge(hid_ready, g * GROUP + (j + 1))
                    nc.tensor.matmul(psU[j % 2][:, 0:UW], same[j // HALF][:, j % HALF, :], hid[:, j % 4, :],
                                     start=True, stop=True).then_inc(agg_done, 1)

        @block.scalar
        def _(act):
            def keep_attr(g, q):
                act.wait_ge(attr_turned, g * 4 + (q + 1))
                nc.scalar.copy(attrT[q % 2][:, :], psT[q % 2][:, 0:2 * P]).then_inc(attrT_ready, 1)

            act.wait_ge(ones, 1)
            keep_attr(0, 0)
            keep_attr(0, 1)
            with act.Fori(0, NG) as g:
                for j in range(GROUP):
                    if j % 4 == 0:
                        act.wait_ge(c_done, g * GROUP + (j + 4))
                        keep_attr(g, j // 4 + 2)
                    act.wait_ge(pre_ready, g * GROUP + (j + 1))
                    nc.scalar.activation(hid[:, j % 4, 0:H], ga[:, j % SLOTS, :], ACT.Relu).then_inc(hid_ready, 1)
                    act.wait_ge(agg_done, g * GROUP + (j + 1))
                    act.wait_ge(scattered[j % NTAB], g * (16 * GROUP // NTAB) + max(16 * (j // NTAB) - 16, 0))
                    nc.scalar.copy(msum[:, j % 4, :], psU[j % 2][:, 0:UW]).then_inc(msum_ready, 1)

        @block.vector
        def _(dve):
            def stage_index(g, h):
                at = bass.ds(g * GROUP + h * HALF, HALF)
                nc.vector.tensor_copy(gsrc[h % 2][:, :], K["srcT"][:, at]).then_inc(index_ready, 1)

            def compare(chain, g, h):
                ids = K["srcT"][:, bass.ds(g * GROUP + h * HALF, HALF)]
                dve.wait_ge(src_in[h % 2], g * 32 + 32 * (1 + h // 2))
                for w in range(WIN):
                    t = nc.vector.tensor_scalar(onehot[h % 2][:, w, :, :], locb[h % 2][:, :, :], K["winid"][:, w:w + 1], None, ALU.is_equal)
                t.then_inc(onehot_ready, 1)
                chain.link(nc.vector.tensor_tensor(same[h % 2][:, :, :], srcb[h % 2][:, :, :],
                                                   ids.unsqueeze(2).to_broadcast([P, HALF, P]), ALU.is_equal))
                chain.link(nc.vector.tensor_tensor(earlier[:, :, :], same[h % 2][:, :, :],
                                                   K["before"][:, :].unsqueeze(1).to_broadcast([P, HALF, P]), ALU.mult))
                chain.link(nc.vector.tensor_reduce(dup[:, :], earlier[:, :, :], AX.X, ALU.max))
                chain.link(nc.vector.tensor_scalar(togo[:, :], ids, -1.0, K["spare"][:, 0:1], ALU.mult, ALU.add))
                chain.link(nc.vector.tensor_tensor(togo[:, :], togo[:, :], dup[:, :], ALU.mult))
                nc.vector.tensor_tensor(sink[h % 2][:, :], togo[:, :], ids, ALU.add).then_inc(same_ready, 1)

            nc.vector.memset(hid[:, :, :], 1.0).then_inc(ones, 1)
            first = Chain(dve, dve_step)
            stage_index(0, 0)
            stage_index(0, 1)
            compare(first, 0, 0)
            PER = 10
            with dve.Fori(0, NG) as g:
                chain = Chain(dve, dve_step, g * PER + first.n)
                for j in range(GROUP):
                    s = j % SLOTS
                    dve.wait_ge(gathered[s], g * (16 * GROUP // SLOTS) + 16 * (j // SLOTS + 1))
                    dve.wait_ge(c_done, g * GROUP + (j + 1))
                    nc.vector.tensor_tensor(ga[:, s, :], ga[:, s, :], pc(j), ALU.add).then_inc(pre_ready, 1)
                    if j % HALF == HALF // 2:
                        h = j // HALF
                        dve.wait_ge(agg_done, g * GROUP + h * HALF)
                        dve.wait_ge(c_done, g * GROUP + h * HALF)
                        for t in range(NTAB):
                            dve.wait_ge(scattered[t], g * (16 * GROUP // NTAB) + h * (16 * HALF // NTAB))
                        compare(chain, g, h + 1)
                    if j % HALF == HALF - 1:
                        stage_index(g, 2 + j // HALF)
                assert chain.n == PER


def nodes_phase(nc, K, D, A):
    with ExitStack() as st:
        m = Mem(nc, st, "nd_")
        sums = [m.sb(f"sums{t}", [P, UNR, UW]) for t in range(NTAB)]
        xs = m.sb("xs", [P, UNR, H])
        turnedT = m.sb("turnedT", [P, UNR, 4 * P])
        degT = m.sb("degT", [1, UNR, P])
        aggT = m.sb("aggT", [P, UNR, H])
        rz = m.sb("rz", [P, UNR, 2 * H])
        cand = m.sb("cand", [P, UNR, 2 * H])
        tmp = m.sb("tmp", [P, UNR, H])
        y = m.sb("y", [P, UNR, H])
        stats = m.sb("stats", [P, UNR, 6])
        moments = m.sb("moments", [P, UNR, 2])
        rstd = m.sb("rstd", [P, UNR, 1])
        x1 = m.sb("x1", [P, UNR, H + 2 * NH])
        x1T = m.sb("x1T", [P, UNR, H])
        psT = m.ps("psT", [P, 512])
        psD = m.ps("psD", [P, 512])
        psG = m.ps("psG", [P, 512])
        psRZ = m.ps("psRZ", [P, 512])
        psN = m.ps("psN", [P, 512])
        psX = m.ps("psX", [P, 512])
        psS = m.ps("psS", [P, 512])
        loaded = [m.sem(f"loaded{j}") for j in range(UNR)]
        stored = [m.sem(f"stored{j}") for j in range(UNR)]
        summed, turned, turned_kept = m.sem("summed"), m.sem("turned"), m.sem("turned_kept")
        agg_done, agg_kept = m.sem("agg_done"), m.sem("agg_kept")
        gates_done, gates_kept, gates_open = m.sem("gates_done"), m.sem("gates_kept"), m.sem("gates_open")
        cand_ready, cand_done = m.sem("cand_ready"), m.sem("cand_done")
        x1_ready, x1_turned, x1T_ready = m.sem("x1_ready"), m.sem("x1_turned"), m.sem("x1T_ready")
        scores_done, rows_ready = m.sem("scores_done"), m.sem("rows_ready")
        var_ready = m.sem("var_ready")
        moments_ready, rstd_ready = m.sem("moments_ready"), m.sem("rstd_ready")
        dve_step = m.sem("dve_step")
        dve_waited, pool_waited = m.sem("dve_waited"), m.sem("pool_waited")
        scattered = [m.sem(f"scattered{j}") for j in range(UNR)]
        rank = m.sb("rank", [P, UNR], I32)
        block = st.enter_context(nc.Block())

        def iterations(engine, body):
            body(0, True, False)
            with engine.Fori(1, NI - 1) as i:
                body(i, False, False)
            body(NI - 1, False, True)

        @block.sync
        def _(sp):
            def load(row, j, count=P):
                for t in range(NTAB):
                    sp.dma_start(sums[t][:, j, :], D[f"S{t}"][bass.ds(row, P), :]).then_inc(loaded[j], 16)
                sp.dma_start(xs[0:count, j, :], A["x"][bass.ds(row, count), :]).then_inc(loaded[j], 16)

            def store(i, j):
                sp.wait_ge(rows_ready, i * UNR + (j + 1))
                rows = bass.ds(i * (UNR * P) + j * P, P)
                sp.dma_start(D["X1"][rows, :], x1[:, j, 0:XW]).then_inc(stored[j], 16)

            for j in range(UNR):
                load(j * P, j)
            with sp.Fori(0, NI - 2) as i:
                for j in range(UNR):
                    store(i, j)
                    load(i * (UNR * P) + (UNR + j) * P, j)
            for j in range(UNR):
                store(NI - 2, j)
                row = (NI - 1) * UNR * P + j * P
                load(row, j, min(P, N - row))
            for j in range(UNR):
                store(NI - 1, j)
            for j in range(UNR):
                sp.wait_ge(stored[j], 16 * NI)

        @block.gpsimd
        def _(pool):
            def scatter(i, j):
                pool.wait_ge(rows_ready, i * UNR + (j + 1))
                pool.sem_inc(pool_waited, 1)
                pool.indirect_dma_start(D["sv"], bass.IndirectOffsetOnAxis(ap=rank[:, j:j + 1], axis=0),
                                        x1[:, j, XW:XW + NH], None).then_inc(scattered[j], 16)

            def body(i, first, last):
                for j in range(UNR):
                    if j >= 2 or not first:
                        scatter(*((i, j - 2) if j >= 2 else (i - 1, UNR + j - 2)))
                    pool.wait_ge(moments_ready, i * UNR + (j + 1))
                    nc.gpsimd.tensor_tensor(rstd[:, j, :], moments[:, j, 1:2], K["eps"][:, :], ALU.add).then_inc(var_ready, 1)
                    pool.wait_ge(var_ready, i * UNR + (j + 1))
                    nc.gpsimd.tensor_tensor(rstd[:, j, :], rstd[:, j, :], K["neghalf"][:, :], ALU.pow).then_inc(rstd_ready, 1)

            iterations(pool, body)
            scatter(NI - 1, UNR - 2)
            scatter(NI - 1, UNR - 1)
            for j in range(UNR):
                pool.wait_ge(scattered[j], 16 * NI)

        @block.tensor
        def _(pe):
            def turn(i, j):
                pe.wait_ge(turned_kept, i * UNR + j)
                pe.wait_ge(summed, i * UNR + (j + 1))
                for k in range(HC):
                    nc.tensor.transpose(psT[:, k * P:(k + 1) * P], sums[0][:, j, k * P:(k + 1) * P], K["ident"][:, :])
                    nc.tensor.transpose(psT[:, (HC + k) * P:(HC + k + 1) * P], xs[:, j, k * P:(k + 1) * P], K["ident"][:, :])
                nc.tensor.transpose(psD[0:1, 0:P], sums[0][:, j, H:UW], K["ident"][:, :]).then_inc(turned, 1)

            def aggregate(i, j):
                pe.wait_ge(agg_kept, i * UNR + j)
                pe.wait_ge(turned_kept, i * UNR + (j + 1))
                for f in range(HC):
                    cols = slice(f * P, (f + 1) * P)
                    for k in range(HC):
                        nc.tensor.matmul(psG[:, cols], K["W2T"][:, k, cols], turnedT[:, j, k * P:(k + 1) * P],
                                         start=(k == 0), stop=False)
                    t = nc.tensor.matmul(psG[:, cols], K["b2row"][:, cols], degT[:, j, :], start=False, stop=True)
                t.then_inc(agg_done, 1)

            def gates(i, j):
                pe.wait_ge(gates_kept, i * UNR + j)
                pe.wait_ge(agg_kept, i * UNR + (j + 1))
                for k in range(HC):
                    a, xk = aggT[:, j, k * P:(k + 1) * P], turnedT[:, j, (HC + k) * P:(HC + k + 1) * P]
                    nc.tensor.matmul(psRZ[:, :], a, K["WihT"][:, k, 0:2 * H], start=(k == 0), stop=False)
                    nc.tensor.matmul(psRZ[:, :], xk, K["WhhT"][:, k, 0:2 * H], start=False, stop=(k == HC - 1))
                for w, at in (("WihT", 0), ("WhhT", H)):
                    for k in range(HC):
                        lhs = aggT[:, j, k * P:(k + 1) * P] if at == 0 else turnedT[:, j, (HC + k) * P:(HC + k + 1) * P]
                        t = nc.tensor.matmul(psN[:, at:at + H], lhs, K[w][:, k, 2 * H:3 * H],
                                             start=(k == 0), stop=(k == HC - 1))
                t.then_inc(gates_done, 1)

            def turn_x1(i, j):
                pe.wait_ge(x1T_ready, i * UNR + j)
                pe.wait_ge(x1_ready, i * UNR + (j + 1))
                for k in range(HC):
                    t = nc.tensor.transpose(psX[:, k * P:(k + 1) * P], x1[:, j, k * P:(k + 1) * P], K["ident"][:, :])
                t.then_inc(x1_turned, 1)

            def scores(i, j):
                pe.wait_ge(rows_ready, i * UNR + j)
                pe.wait_ge(x1T_ready, i * UNR + (j + 1))
                for k in range(HC):
                    t = nc.tensor.matmul(psS[:, 0:2 * NH], x1T[:, j, k * P:(k + 1) * P], K["WuvT"][:, k, :],
                                         start=(k == 0), stop=(k == HC - 1))
                t.then_inc(scores_done, 1)

            def before(i, j, n, first):
                if j >= n:
                    return i, j - n
                return None if first else (i - 1, UNR + j - n)

            turn(0, 0)
            aggregate(0, 0)

            def body(i, first, last):
                for j in range(UNR):
                    if at := before(i, j, 2, first):
                        scores(*at)
                    gates(i, j)
                    after = (i, j + 1) if j + 1 < UNR else (None if last else (i + 1, 0))
                    if after:
                        turn(*after)
                    if at := before(i, j, 1, first):
                        turn_x1(*at)
                    if after:
                        aggregate(*after)

            iterations(pe, body)
            scores(NI - 1, UNR - 2)
            turn_x1(NI - 1, UNR - 1)
            scores(NI - 1, UNR - 1)

        @block.scalar
        def _(act):
            def keep_turned(i, j):
                act.wait_ge(turned, i * UNR + (j + 1))
                nc.scalar.copy(degT[:, j, :], psD[0:1, 0:P])
                nc.scalar.copy(turnedT[:, j, :], psT[:, :]).then_inc(turned_kept, 1)

            def keep_agg(i, j):
                act.wait_ge(agg_done, i * UNR + (j + 1))
                nc.scalar.copy(aggT[:, j, :], psG[:, 0:H]).then_inc(agg_kept, 1)

            def keep_x1(i, j):
                act.wait_ge(x1_turned, i * UNR + (j + 1))
                nc.scalar.copy(x1T[:, j, :], psX[:, 0:H]).then_inc(x1T_ready, 1)

            keep_turned(0, 0)
            keep_agg(0, 0)

            def body(i, first, last):
                for j in range(UNR):
                    act.wait_ge(gates_kept, i * UNR + (j + 1))
                    nc.scalar.activation(rz[:, j, :], rz[:, j, :], ACT.Sigmoid).then_inc(gates_open, 1)
                    after = (i, j + 1) if j + 1 < UNR else (None if last else (i + 1, 0))
                    if after:
                        keep_turned(*after)
                    if j >= 1 or not first:
                        keep_x1(*((i, j - 1) if j >= 1 else (i - 1, UNR - 1)))
                    act.wait_ge(cand_ready, i * UNR + (j + 1))
                    nc.scalar.activation(cand[:, j, 0:H], cand[:, j, 0:H], ACT.Tanh).then_inc(cand_done, 1)
                    if after:
                        keep_agg(*after)

            iterations(act, body)
            keep_x1(NI - 1, UNR - 1)

        @block.vector
        def _(dve):
            def add_tables(i, j):
                dve.wait_ge(loaded[j], i * (16 * (NTAB + 1)) + 16 * (NTAB + 1))
                for t in range(1, NTAB):
                    nc.vector.tensor_tensor(sums[0][:, j, :], sums[0][:, j, :], sums[t][:, j, :], ALU.add).then_inc(summed, 1)

            def finish(i, j):
                dve.wait_ge(scores_done, i * UNR + (j + 1))
                nc.vector.tensor_tensor(x1[:, j, H:H + 2 * NH], psS[:, 0:2 * NH], K["bu"][:, :], ALU.add).then_inc(rows_ready, 1)

            add_tables(0, 0)
            PER = 6 * UNR

            def body(i, first, last):
                c = Chain(dve, dve_step, i * PER)
                for j in range(UNR):
                    after = (i, j + 1) if j + 1 < UNR else (None if last else (i + 1, 0))
                    if after:
                        add_tables(*after)
                    if j >= 2 or not first:
                        finish(*((i, j - 2) if j >= 2 else (i - 1, UNR + j - 2)))
                    dve.wait_ge(gates_done, i * UNR + (j + 1))
                    nc.vector.tensor_tensor(rz[:, j, :], psRZ[:, :], K["bgate"][:, 0:2 * H], ALU.add)
                    nc.vector.tensor_tensor(cand[:, j, :], psN[:, :], K["bgate"][:, 2 * H:4 * H], ALU.add).then_inc(gates_kept, 1)
                    dve.wait_ge(gates_open, i * UNR + (j + 1))
                    c.link(nc.vector.tensor_tensor(tmp[:, j, :], rz[:, j, 0:H], cand[:, j, H:2 * H], ALU.mult))
                    nc.vector.tensor_tensor(cand[:, j, 0:H], cand[:, j, 0:H], tmp[:, j, :], ALU.add).then_inc(cand_ready, 1)
                    dve.wait_ge(cand_done, i * UNR + (j + 1))
                    c.link(nc.vector.tensor_tensor(tmp[:, j, :], xs[:, j, :], cand[:, j, 0:H], ALU.subtract))
                    c.link(nc.vector.tensor_tensor(tmp[:, j, :], tmp[:, j, :], rz[:, j, H:2 * H], ALU.mult))
                    c.link(nc.vector.tensor_tensor(y[:, j, :], xs[:, j, :], cand[:, j, 0:H], ALU.add))
                    c.link(nc.vector.tensor_tensor(y[:, j, :], y[:, j, :], tmp[:, j, :], ALU.add))
                    c.link(nc.vector.bn_stats(stats[:, j, :], y[:, j, :]))
                    dve.sem_inc(dve_waited, 1)
                    nc.vector.bn_aggr(moments[:, j, :], stats[:, j, :]).then_inc(moments_ready, 1)
                    dve.wait_ge(rstd_ready, i * UNR + (j + 1))
                    dve.wait_ge(stored[j], i * 16)
                    dve.wait_ge(scattered[j], i * 16)
                    nc.vector.tensor_copy(rank[:, j:j + 1], K["rank"][:, bass.ds(i * UNR + j, 1)])
                    nc.vector.tensor_scalar(x1[:, j, 0:H], y[:, j, :], moments[:, j, 0:1], rstd[:, j, :],
                                            ALU.subtract, ALU.mult).then_inc(x1_ready, 1)
                assert c.n == PER, c.n

            iterations(dve, body)
            finish(NI - 1, UNR - 2)
            finish(NI - 1, UNR - 1)


def layer1_phase(nc, K, D, A):
    with ExitStack() as st:
        m = Mem(nc, st, "l1_")
        feats = [m.sb(f"feats{r}", [P, GROUP, XW]) for r in range(2)]
        gsrc = [m.sb(f"gsrc{r}", [P, GROUP], I32) for r in range(2)]
        locb = [m.sb(f"locb{r}", [P, GROUP, P], BF16) for r in range(2)]
        onehot = [m.sb(f"onehot{r}", [P, WIN, GROUP, P], BF16) for r in range(2)]
        svf = m.sb("svf", [P, NB + 1, NH])
        svrest = m.sb("svrest", [P, NB + 1, NH])
        table = m.sb("table", [P, NB + 1, NSPLIT * NH], BF16)
        same = [m.sb(f"same{r}", [P, GROUP, P]) for r in range(2)]
        part = [m.sb(f"part{r}", [P, GROUP, PW]) for r in range(2)]
        score = m.sb("score", [P, GROUP, NH])
        below = m.sb("below", [P, GROUP, NH])
        start8 = m.sb("start8", [P, GROUP, NH])
        turned = m.sb("turned", [P, 2 * P + 1])
        run = m.sb("run", [P, P])
        psE = m.ps("psE", [P, 512])
        psM = m.ps("psM", [P, 512])
        psU = [m.ps(f"psU{q}", [P, 512]) for q in range(4)]
        psV = m.ps("psV", [P, 512])
        table_in, table_ready = m.sem("table_in"), m.sem("table_ready")
        onehot_ready, sv_done, sv_taken = m.sem("onehot_ready"), m.sem("sv_done"), m.sem("sv_taken")
        gathered = [m.sem(f"gathered{r}") for r in range(2)]
        dst_in = [m.sem(f"dst_in{r}") for r in range(2)]
        stored = [m.sem(f"stored{r}") for r in range(2)]
        index_ready, same_ready = m.sem("index_ready"), m.sem("same_ready")
        scores_ready, scores_turned = m.sem("scores_ready"), m.sem("scores_turned")
        max_ready, max_turned = m.sem("max_ready"), m.sem("max_turned")
        below_ready, weights_ready = m.sem("below_ready"), m.sem("weights_ready")
        weighted, agg_done, part_ready = m.sem("weighted"), m.sem("agg_done"), m.sem("part_ready")
        max_kept, scores_kept = m.sem("max_kept"), m.sem("scores_kept")
        dve_step = m.sem("dve_step")
        pool_waited = m.sem("pool_waited")
        block = st.enter_context(nc.Block())

        def groups(engine, body, count=NG):
            with engine.Fori(0, count // 2) as u:
                for r in range(2):
                    body(u * 2 + r, r, u, False)
            if count % 2:
                body(count - 1, 0, count // 2, True)

        @block.sync
        def _(sp):
            def dst_rows(r, row):
                sp.dma_start(locb[r][:, :, :].rearrange("p t e -> p (t e)"),
                             D["loc_rows"][row, :].rearrange("t e -> (t e)").partition_broadcast(P)).then_inc(dst_in[r], 16)

            sp.dma_start(svf[:, :, :], D["sv"].rearrange("(b p) h -> p b h", p=P)).then_inc(table_in, 16)
            for r in range(2):
                dst_rows(r, slice(r * GROUP, (r + 1) * GROUP))

            def body(g, r, u, last):
                sp.wait_ge(same_ready, g + 1)
                dst_rows(r, bass.ds(g * GROUP + 2 * GROUP, GROUP))
                sp.wait_ge(part_ready, g * GROUP + GROUP)
                sp.wait_ge(max_kept, g + 1)
                sp.dma_start(D["PT"][bass.ds(g * (GROUP * P), GROUP * P), :].rearrange("(t p) w -> p t w", p=P),
                             part[r][:, :, :]).then_inc(stored[r], 16)

            groups(sp, body)
            for r in range(2):
                sp.wait_ge(stored[r], 16 * ((NG + 1 - r) // 2))
                sp.wait_ge(dst_in[r], 16 * ((NG + 1 - r) // 2 + 1))

        @block.gpsimd
        def _(pool):
            def gather(r, t):
                pool.indirect_dma_start(feats[r][:, t, :], None, D["X1"],
                                        bass.IndirectOffsetOnAxis(ap=gsrc[r][:, t:t + 1], axis=0)).then_inc(gathered[r], 16)

            pool.wait_ge(index_ready, 2)
            for r in range(2):
                for t in range(GROUP):
                    gather(r, t)

            def body(g, r, u, last):
                pool.wait_ge(index_ready, g + 3)
                for t in range(GROUP):
                    pool.wait_ge(agg_done, g * GROUP + (t + 1))
                    pool.sem_inc(pool_waited, 1)
                    gather(r, t)

            groups(pool, body, NG - 2)
            for r in range(2):
                pool.wait_ge(gathered[r], 16 * GROUP * ((NG + 1 - r) // 2))

        @block.tensor
        def _(pe):
            def dst_scores(g, r):
                pe.wait_ge(onehot_ready, g + 1)
                for t in range(GROUP):
                    if t % PACK == 0:
                        blocks = window_blocks(nc, pe, K, g * (GROUP // PACK) + t // PACK)
                    for w in range(WIN):
                        i = nc.tensor.matmul(psV[:, t * NSPLIT * NH:(t + 1) * NSPLIT * NH], onehot[r][:, w, t, :],
                                             flat(table[:, bass.ds(blocks[t % PACK] + w, 1), :]),
                                             start=(w == 0), stop=(w == WIN - 1))
                i.then_inc(sv_done, 1)

            pe.wait_ge(table_ready, 1)
            dst_scores(0, 0)

            def body(g, r, u, last):
                pe.wait_ge(scores_ready, g + 1)
                nc.tensor.transpose(psE[:, 0:P], score[:, :, :].rearrange("p t h -> p (t h)"), K["ident"][:, :])
                nc.tensor.transpose(psE[:, P:2 * P], start8[:, :, :].rearrange("p t h -> p (t h)"),
                                    K["ident"][:, :]).then_inc(scores_turned, 1)
                pe.wait_ge(max_ready, g + 1)
                nc.tensor.transpose(psM[:, 0:P], turned[:, 0:P], K["ident"][:, :]).then_inc(max_turned, 1)
                if not last:
                    dst_scores(g + 1, 1 - r)
                pe.wait_ge(same_ready, g + 1)
                for t in range(GROUP):
                    if t % 4 == 0:
                        pe.wait_ge(weighted, g * (GROUP // 4) + (t // 4 + 1))
                    pe.wait_ge(part_ready, g * GROUP + t - 3) if t >= 4 else pe.wait_ge(part_ready, g * GROUP)
                    nc.tensor.matmul(psU[t % 4][:, 0:XW], same[r][:, t, :], feats[r][:, t, :],
                                     start=True, stop=True).then_inc(agg_done, 1)

            groups(pe, body)

        @block.scalar
        def _(act):
            def body(g, r, u, last):
                act.wait_ge(scores_turned, g + 1)
                nc.scalar.copy(turned[:, 0:2 * P], psE[:, 0:2 * P]).then_inc(scores_kept, 1)
                act.wait_ge(below_ready, g + 1)
                nc.scalar.activation(feats[r][:, :, H:XW], below[:, :, :], ACT.Exp).then_inc(weights_ready, 1)
                act.wait_ge(stored[r], u * 16)
                nc.scalar.copy(part[r][:, :, XW:PW], psM[:, 0:P].rearrange("p (t h) -> p t h", h=NH)).then_inc(max_kept, 1)
                for t in range(GROUP):
                    act.wait_ge(agg_done, g * GROUP + (t + 1))
                    nc.scalar.copy(part[r][:, t, 0:XW], psU[t % 4][:, 0:XW]).then_inc(part_ready, 1)

            groups(act, body)

        @block.vector
        def _(dve):
            def stage_index(g, r):
                at = bass.ds(g * GROUP, GROUP)
                nc.vector.tensor_copy(gsrc[r][:, :], K["srcT"][:, at]).then_inc(index_ready, 1)

            def find_node(g, r, u):
                dve.wait_ge(dst_in[r], u * 16 + 16)
                for w in range(WIN):
                    t = nc.vector.tensor_scalar(onehot[r][:, w, :, :], locb[r][:, :, :], K["winid"][:, w:w + 1], None, ALU.is_equal)
                t.then_inc(onehot_ready, 1)

            def compare(g, r):
                nc.vector.tensor_tensor(same[r][:, :, :], locb[r][:, :, :],
                                        K["locT"][:, bass.ds(g * GROUP, GROUP)].unsqueeze(2).to_broadcast([P, GROUP, P]),
                                        ALU.is_equal).then_inc(same_ready, 1)

            stage_index(0, 0)
            stage_index(1, 1)
            find_node(0, 0, 0)
            compare(0, 0)
            first = Chain(dve, dve_step)
            first.link(nc.vector.memset(turned[:, 2 * P:2 * P + 1], 0.0))
            dve.wait_ge(table_in, 16)
            split_float(nc, first, svf[:, :, :], svrest[:, :, :],
                        [table[:, :, n * NH:(n + 1) * NH] for n in range(NSPLIT)])
            dve.sem_inc(table_ready, 1)
            PER = 2

            def body(g, r, u, last):
                c = Chain(dve, dve_step, g * PER + first.n)
                dve.wait_ge(gathered[r], u * (16 * GROUP) + 16 * GROUP)
                stage_index(g + 2, r)
                nc.vector.tensor_copy(start8[:, :, :],
                                      K["startT"][:, bass.ds(g * GROUP, GROUP)].unsqueeze(2).to_broadcast([P, GROUP, NH]))
                dve.wait_ge(sv_done, g + 1)
                nc.vector.tensor_reduce(score[:, :, :], psV[:, 0:GROUP * NSPLIT * NH].rearrange("p (t n h) -> p t h n", n=NSPLIT, h=NH),
                                        AX.X, ALU.add).then_inc(sv_taken, 1)
                dve.wait_ge(sv_taken, g + 1)
                c.link(nc.vector.tensor_tensor(score[:, :, :], feats[r][:, :, H:XW], score[:, :, :], ALU.add))
                nc.vector.scalar_tensor_tensor(score[:, :, :], score[:, :, :], SLOPE, score[:, :, :],
                                               ALU.mult, ALU.max).then_inc(scores_ready, 1)
                if not last:
                    find_node(g + 1, 1 - r, u + r)
                dve.wait_ge(scores_kept, g + 1)
                segment_max(nc, c, turned[:, 0:P], turned[:, P:2 * P + 1], P, run).then_inc(max_ready, 1)
                if not last:
                    dve.wait_ge(agg_done, g * GROUP)
                    compare(g + 1, 1 - r)
                dve.wait_ge(max_turned, g + 1)
                nc.vector.tensor_tensor(below[:, :, :], score[:, :, :], psM[:, 0:P].rearrange("p (t h) -> p t h", h=NH),
                                        ALU.subtract).then_inc(below_ready, 1)
                dve.wait_ge(weights_ready, g + 1)
                for q in range(GROUP // 4):
                    f = feats[r][:, q * 4:(q + 1) * 4, :]
                    f3 = f[:, :, 0:H].rearrange("p t (c h) -> p t c h", h=NH)
                    w3 = f[:, :, H:XW].unsqueeze(2).to_broadcast([P, 4, H // NH, NH])
                    nc.vector.tensor_tensor(f3, f3, w3, ALU.mult).then_inc(weighted, 1)
                assert c.n == PER

            groups(dve, body)


def merge_phase(nc, K, D, A):
    with ExitStack() as st:
        m = Mem(nc, st, "mg_")
        rows = m.sb("rows", [CQ, CH, PW])
        t2 = m.sb("t2", [CQ, CH, PW])
        last = m.sb("last", [CQ, CH])
        lastb = m.sb("lastb", [CQ, NT])
        same = m.sb("same", [CQ, CH, NT])
        maxT = m.sb("maxT", [NH, NT])
        start = m.sb("start", [NH, NT + 1])
        run = m.sb("run", [NH, NT])
        scale = m.sb("scale", [CQ, CH, NH])
        psA = [m.ps(f"psA{i}", [P, 512]) for i in range(2)]
        psM = m.ps("psM", [P, 512])
        psS = [m.ps(f"psS{i}", [P, 512]) for i in range(2)]
        rows_in, last_in = m.sem("rows_in"), m.sem("last_in")
        turned, kept, max_ready, max_turned = m.sem("turned"), m.sem("kept"), m.sem("max_ready"), m.sem("max_turned")
        below_ready, scale_ready, scaled = m.sem("below_ready"), m.sem("scale_ready"), m.sem("scaled")
        summed, t2_ready, t2_out = m.sem("summed"), m.sem("t2_ready"), m.sem("t2_out")
        dve_step = m.sem("dve_step")
        block = st.enter_context(nc.Block())
        split = 4

        @block.sync
        def _(sp):
            sp.dma_start(rows[:, :, :], D["PT"].rearrange("(c q p) w -> q c p w", q=CQ, p=P)[:, :, P - 1, :]).then_inc(rows_in, 16)
            sp.dma_start(lastb[:, :], D["last"].rearrange("t o -> (t o)").partition_broadcast(CQ)).then_inc(last_in, 16)
            with nc.allow_non_contiguous_dma(reason="one word of each tile"):
                sp.dma_start(last[:, :], D["last"].rearrange("(c q) o -> q (c o)", q=CQ)).then_inc(last_in, 16)
            sp.wait_ge(t2_ready, CH + 1)
            sp.dma_start(D["T2"].rearrange("(c q) w -> q c w", q=CQ), t2[:, :, :]).then_inc(t2_out, 16)
            sp.wait_ge(t2_out, 16)

        @block.tensor
        def _(pe):
            pe.wait_ge(rows_in, 16)
            for c in range(CH):
                at = c % split * CQ
                i = nc.tensor.transpose(psA[c // split][0:NH, at:at + CQ], rows[:, c, XW:PW], K["ident"][0:CQ, 0:CQ])
            i.then_inc(turned, 1)
            pe.wait_ge(max_ready, 1)
            for c in range(CH):
                i = nc.tensor.transpose(psM[0:CQ, c * NH:(c + 1) * NH], maxT[:, c * CQ:(c + 1) * CQ], K["ident"][0:NH, 0:NH])
            i.then_inc(max_turned, 1)
            pe.wait_ge(scaled, 2)
            for a in range(CH):
                if a >= 2:
                    pe.wait_ge(t2_ready, a)
                for c in range(CH):
                    i = nc.tensor.matmul(psS[a % 2][0:CQ, 0:XW], same[:, c, a * CQ:(a + 1) * CQ], rows[:, c, 0:XW],
                                         start=(c == 0), stop=(c == CH - 1))
                i.then_inc(summed, 1)

        @block.scalar
        def _(act):
            act.wait_ge(below_ready, 1)
            nc.scalar.activation(scale[:, :, :], scale[:, :, :], ACT.Exp).then_inc(scale_ready, 1)
            nc.scalar.copy(t2[:, :, XW:PW], psM[0:CQ, 0:CH * NH].rearrange("p (c h) -> p c h", h=NH)).then_inc(t2_ready, 1)
            for a in range(CH):
                act.wait_ge(summed, a + 1)
                nc.scalar.copy(t2[:, a, 0:XW], psS[a % 2][0:CQ, 0:XW]).then_inc(t2_ready, 1)

        @block.vector
        def _(dve):
            c = Chain(dve, dve_step)
            dve.wait_ge(turned, 1)
            dve.wait_ge(last_in, 32)
            c.link(nc.vector.tensor_copy(maxT[:, 0:split * CQ], psA[0][0:NH, 0:split * CQ]))
            c.link(nc.vector.tensor_copy(maxT[:, split * CQ:NT], psA[1][0:NH, 0:NT - split * CQ]))
            c.link(nc.vector.memset(start[:, :], LOW))
            c.link(nc.vector.tensor_tensor(start[:, 1:NT], lastb[0:NH, 1:NT], lastb[0:NH, 0:NT - 1], ALU.not_equal))
            c.link(nc.vector.tensor_scalar(start[:, 1:NT], start[:, 1:NT], LOW, None, ALU.mult))
            segment_max(nc, c, maxT, start, NT, run).then_inc(max_ready, 1)
            nc.vector.tensor_tensor(same[:, :, :], lastb[:, :].unsqueeze(1).to_broadcast([CQ, CH, NT]),
                                    last[:, :].unsqueeze(2).to_broadcast([CQ, CH, NT]), ALU.is_equal).then_inc(scaled, 1)
            dve.wait_ge(max_turned, 1)
            nc.vector.tensor_tensor(scale[:, :, :], rows[:, :, XW:PW],
                                    psM[0:CQ, 0:CH * NH].rearrange("p (c h) -> p c h", h=NH), ALU.subtract).then_inc(below_ready, 1)
            dve.wait_ge(scale_ready, 1)
            u = rows[:, :, 0:XW].rearrange("p c (n h) -> p c n h", h=NH)
            nc.vector.tensor_tensor(u, u, scale[:, :, :].unsqueeze(2).to_broadcast([CQ, CH, XW // NH, NH]),
                                    ALU.mult).then_inc(scaled, 1)


def output_phase(nc, K, D, A):
    with ExitStack() as st:
        m = Mem(nc, st, "ot_")
        idx = [m.sb(f"idx{r}", [P, 2, UNR], I32) for r in range(2)]
        ends = [m.sb(f"ends{r}", [P, UNR, PW]) for r in range(2)]
        own = [m.sb(f"own{r}", [P, UNR, PW]) for r in range(2)]
        x1 = [m.sb(f"x1{r}", [P, UNR, H]) for r in range(2)]
        y = [m.sb(f"y{r}", [P, UNR, H]) for r in range(2)]
        w = m.sb("w", [P, 2, UNR, NH])
        den = m.sb("den", [P, 2, UNR, NH])
        top = m.sb("top", [P, UNR, NH])
        valid = m.sb("valid", [P, 2, UNR])
        mask = m.sb("mask", [P, 2, UNR])
        none = m.sb("none", [P, UNR])
        stats = m.sb("stats", [P, UNR, 6])
        moments = m.sb("moments", [P, UNR, 2])
        rstd = m.sb("rstd", [P, UNR])
        index_ready = m.sem("index_ready")
        gathered = [m.sem(f"gathered{r}") for r in range(2)]
        x1_in = [m.sem(f"x1_in{r}") for r in range(2)]
        out_sent = [m.sem(f"out_sent{r}") for r in range(2)]
        below_ready, weights_ready, added = m.sem("below_ready"), m.sem("weights_ready"), m.sem("added")
        moments_ready, var_ready, rstd_ready, y_ready = m.sem("moments_ready"), m.sem("var_ready"), m.sem("rstd_ready"), m.sem("y_ready")
        dve_step = m.sem("dve_step")
        pool_waited, dve_waited = m.sem("pool_waited"), m.sem("dve_waited")
        block = st.enter_context(nc.Block())

        def units(engine, body):
            with engine.Fori(0, NI // 2) as u:
                for r in range(2):
                    body(u * 2 + r, r, u, False)
            body(NI - 1, 0, NI // 2, True)

        span = UNR * P

        @block.sync
        def _(sp):
            def load(u, r):
                sp.dma_start(x1[r][:, :, :], D["X1"][bass.ds(u * span, span), 0:H].rearrange("(b p) h -> p b h", p=P)).then_inc(x1_in[r], 16)

            for r in range(2):
                load(r, r)

            def step(u, ahead):
                for r in range(2):
                    sp.wait_ge(y_ready, u * (2 * UNR) + UNR * (r + 1))
                    sp.dma_start(A["out"][bass.ds(u * (2 * span) + r * span, span), :].rearrange("(b p) h -> p b h", p=P),
                                 y[r][:, :, :]).then_inc(out_sent[r], 16)
                    if r < ahead:
                        sp.wait_ge(added, u * 2 + (r + 1))
                        load(u * 2 + (2 + r), r)

            with sp.Fori(0, NI // 2 - 1) as u:
                step(u, 2)
            step(NI // 2 - 1, 1)
            first = (NI - 1) * span
            whole = (N - first) // P
            sp.wait_ge(y_ready, NI * UNR)
            sp.dma_start(A["out"][first:first + whole * P, :].rearrange("(b p) h -> p b h", p=P),
                         y[0][:, 0:whole, :]).then_inc(out_sent[0], 16)
            sp.dma_start(A["out"][first + whole * P:N, :], y[0][0:N - first - whole * P, whole, :]).then_inc(out_sent[0], 16)
            sp.wait_ge(out_sent[0], 16 * (NI // 2 + 2))
            sp.wait_ge(out_sent[1], 16 * (NI // 2))

        @block.gpsimd
        def _(pool):
            def norm(u):
                pool.wait_ge(moments_ready, u * UNR + UNR)
                nc.gpsimd.tensor_tensor(rstd[:, :], moments[:, :, 1], K["eps"][:, 0:1].to_broadcast([P, UNR]), ALU.add).then_inc(var_ready, 1)
                pool.wait_ge(var_ready, u + 1)
                nc.gpsimd.tensor_tensor(rstd[:, :], rstd[:, :], K["neghalf"][:, 0:1].to_broadcast([P, UNR]), ALU.pow).then_inc(rstd_ready, 1)

            def gather(u, r):
                pool.wait_ge(index_ready, u + 1)
                pool.sem_inc(pool_waited, 1)
                for j in range(UNR):
                    pool.indirect_dma_start(ends[r][:, j, :], None, D["T2"],
                                            bass.IndirectOffsetOnAxis(ap=idx[r][:, 0, j:j + 1], axis=0)).then_inc(gathered[r], 16)
                    pool.indirect_dma_start(own[r][:, j, :], None, D["PT"],
                                            bass.IndirectOffsetOnAxis(ap=idx[r][:, 1, j:j + 1], axis=0)).then_inc(gathered[r], 16)

            gather(0, 0)
            gather(1, 1)
            with pool.Fori(0, NI // 2 - 1) as u:
                norm(u * 2)
                gather(u * 2 + 2, 0)
                norm(u * 2 + 1)
                gather(u * 2 + 3, 1)
            norm(NI - 3)
            gather(NI - 1, 0)
            norm(NI - 2)
            norm(NI - 1)
        @block.scalar
        def _(act):
            def body(u, r, v, last):
                act.wait_ge(below_ready, u + 1)
                nc.scalar.activation(w[:, :, :, :], w[:, :, :, :], ACT.Exp).then_inc(weights_ready, 1)

            units(act, body)

        @block.vector
        def _(dve):
            def stage_index(u, r):
                at = bass.ds(u * UNR, UNR)
                nc.vector.tensor_copy(idx[r][:, 0, :], K["ends_row"][:, at])
                nc.vector.tensor_copy(idx[r][:, 1, :], K["own_row"][:, at]).then_inc(index_ready, 1)

            stage_index(0, 0)
            stage_index(1, 1)
            PER = 13

            def body(u, r, v, last):
                c = Chain(dve, dve_step, u * PER)
                at = bass.ds(u * UNR, UNR)
                pair = (ends[r], own[r])
                dve.wait_ge(gathered[r], v * (32 * UNR) + 32 * UNR)
                if not last:
                    stage_index(u + 2, r)
                nc.vector.tensor_scalar(none[:, :], K["any"][:, at], -1.0, 1.0, ALU.mult, ALU.add)
                nc.vector.tensor_copy(valid[:, 0, :], K["ends"][:, at])
                c.link(nc.vector.tensor_copy(valid[:, 1, :], K["own"][:, at]))
                c.link(nc.vector.tensor_scalar(mask[:, :, :], valid[:, :, :], -1.0, -LOW, ALU.add, ALU.mult))
                for n in range(2):
                    t = nc.vector.tensor_tensor(w[:, n, :, :], pair[n][:, :, XW:PW],
                                                mask[:, n, :].unsqueeze(2).to_broadcast([P, UNR, NH]), ALU.add)
                c.link(t)
                c.link(nc.vector.tensor_tensor(top[:, :, :], w[:, 0, :, :], w[:, 1, :, :], ALU.max))
                nc.vector.tensor_tensor(w[:, :, :, :], w[:, :, :, :], top[:, :, :].unsqueeze(1).to_broadcast([P, 2, UNR, NH]),
                                        ALU.subtract).then_inc(below_ready, 1)
                dve.wait_ge(weights_ready, u + 1)
                c.link(nc.vector.tensor_tensor(w[:, :, :, :], w[:, :, :, :],
                                               valid[:, :, :].unsqueeze(3).to_broadcast([P, 2, UNR, NH]), ALU.mult))
                for n in range(2):
                    t = nc.vector.tensor_tensor(den[:, n, :, :], pair[n][:, :, H:XW], w[:, n, :, :], ALU.mult)
                c.link(t)
                c.link(nc.vector.tensor_tensor(top[:, :, :], den[:, 0, :, :], den[:, 1, :, :], ALU.add))
                c.link(nc.vector.tensor_tensor(top[:, :, :], top[:, :, :], none[:, :].unsqueeze(2).to_broadcast([P, UNR, NH]), ALU.add))
                c.link(nc.vector.reciprocal(top[:, :, :], top[:, :, :]))
                c.link(nc.vector.tensor_tensor(w[:, :, :, :], w[:, :, :, :], top[:, :, :].unsqueeze(1).to_broadcast([P, 2, UNR, NH]), ALU.mult))
                for n in range(2):
                    f = pair[n][:, :, 0:H].rearrange("p b (c h) -> p b c h", h=NH)
                    t = nc.vector.tensor_tensor(f, f, w[:, n, :, :].unsqueeze(2).to_broadcast([P, UNR, H // NH, NH]), ALU.mult)
                c.link(t)
                c.link(nc.vector.tensor_tensor(ends[r][:, :, 0:H], ends[r][:, :, 0:H], own[r][:, :, 0:H], ALU.add))
                dve.wait_ge(x1_in[r], v * 16 + 16)
                dve.wait_ge(out_sent[r], v * 16)
                nc.vector.tensor_tensor(y[r][:, :, :], ends[r][:, :, 0:H], x1[r][:, :, :], ALU.add).then_inc(added, 1)
                dve.wait_ge(added, u + 1)
                for j in range(UNR):
                    t = nc.vector.bn_stats(stats[:, j, :], y[r][:, j, :])
                c.link(t)
                dve.sem_inc(dve_waited, 1)
                for j in range(UNR):
                    nc.vector.bn_aggr(moments[:, j, :], stats[:, j, :]).then_inc(moments_ready, 1)
                dve.wait_ge(rstd_ready, u + 1)
                for j in range(UNR):
                    nc.vector.tensor_scalar(y[r][:, j, :], y[r][:, j, :], moments[:, j, 0:1], rstd[:, j:j + 1],
                                            ALU.subtract, ALU.mult).then_inc(y_ready, 1)
                assert c.n == PER, c.n

            units(dve, body)


def build(nc, x, src, dst, edge_attr, W1, b1, W2, b2, W_ih, b_ih, W_hh, b_hh, W_u, b_u, W_v, out, stop=99):
    A = dict(x=x, src=src, dst=dst, edge_attr=edge_attr, W1=W1, b1=b1, W2=W2, b2=b2, W_ih=W_ih, b_ih=b_ih,
             W_hh=W_hh, b_hh=b_hh, W_u=W_u, b_u=b_u, W_v=W_v, out=out)

    def dram(name, shape, dt=F32):
        return nc.dram_tensor(name, shape, dt, kind="Internal").ap()

    D = {"A": dram("A_rows", [NP, H]), "B": dram("B_rows", [NP + P, NSPLIT * H], BF16),
         "src_rows": dram("src_rows", [NTX, P]), "dst_rows": dram("dst_rows", [NT + 1, P]),
         "loc_rows": dram("loc_rows", [NTX, P], BF16), "blocks": dram("block_words", [NT // PACK, 1], I32)}
    D["last"], D["upto"] = dram("last", [NT, 1]), dram("upto", [NP + 1, 1])
    D["T2"] = dram("T2", [NT, PW])
    D["PT"] = dram("PT", [NT * P, PW])
    D["X1"], D["sv"] = dram("X1_rows", [NP, XW]), dram("sv_rows", [NP + P, NH])
    for t in range(NTAB):
        D[f"S{t}"] = dram(f"S{t}", [NP + P, UW])
    with ExitStack() as st:
        m = Mem(nc, st)
        K = {"ident": m.sb("ident", [P, P]), "before": m.sb("before", [P, P]),
             "winid": m.sb("winid", [P, WIN]), "spare": m.sb("spare", [P, 1]),
             "srcT": m.sb("srcT", [P, NTX]), "startT": m.sb("startT", [P, NT]), "locT": m.sb("locT", [P, NTX]),
             "blocks": m.sb("blocks", [1, PACKED], I32), "rank": m.sb("rank", [P, NB]),
             "W1cT": m.sb("W1cT", [2 * ED, H]), "W2T": m.sb("W2T", [P, HC, H]),
             "WihT": m.sb("WihT", [P, HC, 3 * H]), "WhhT": m.sb("WhhT", [P, HC, 3 * H]),
             "WuvT": m.sb("WuvT", [P, HC, 2 * NH]),
             "any": m.sb("any", [P, NB]), "ends": m.sb("ends", [P, NB]), "own": m.sb("own", [P, NB]),
             
             "ends_row": m.sb("ends_row", [P, NB + UNR]), "own_row": m.sb("own_row", [P, NB + UNR]),
             "eps": m.sb("eps", [P, 1]), "neghalf": m.sb("neghalf", [P, 1]),
             "bgate": m.sb("bgate", [P, 4 * H]), "bu": m.sb("bu", [P, 2 * NH]), "b2row": m.sb("b2row", [1, H])}
        K["b_out"] = [m.sem(f"b_out{j}") for j in range(UNR)]
        K["edges_gathered"] = m.sem("edges_gathered")
        setup_phase(nc, K, D, A)
        if stop < 1:
            return
        layer0_phase(nc, K, D, A)
        if stop < 2:
            return
        nodes_phase(nc, K, D, A)
        if stop < 3:
            return
        layer1_phase(nc, K, D, A)
        if stop < 4:
            return
        merge_phase(nc, K, D, A)
        output_phase(nc, K, D, A)


def kernel(**inputs):
    import numpy as np
    import concourse.bacc as bacc
    from concourse.bass_utils import run_bass_kernel_spmd

    names = ["x", "src", "dst", "edge_attr_64", "L0_gnn_W1", "L0_gnn_b1", "L0_gnn_W2", "L0_gnn_b2", "L0_gnn_W_ih",
             "L0_gnn_b_ih", "L0_gnn_W_hh", "L0_gnn_b_hh", "L1_gnn_W_u", "L1_gnn_b_u", "L1_gnn_W_v"]
    nc = bacc.Bacc("TRN2", target_bir_lowering=False, num_devices=1)
    arrays, args = {}, []
    for name in names:
        a = np.ascontiguousarray(inputs[name])
        arrays[f"in_{name}"] = a
        args.append(nc.dram_tensor(f"in_{name}", a.shape, mybir.dt.from_np(a.dtype), kind="ExternalInput").ap())
    out = nc.dram_tensor("out_0", (N, H), F32, kind="ExternalOutput").ap()
    build(nc, *args, out)
    result = run_bass_kernel_spmd(nc, [arrays], core_ids=[0])
    return result.results[0]["out_0"]
```

```python
import concourse.bass as bass
from concourse import mybir
from contextlib import ExitStack

F32 = mybir.dt.float32
I32 = mybir.dt.int32
BF16 = mybir.dt.bfloat16
ALU = mybir.AluOpType
ACT = mybir.ActivationFunctionType
AX = mybir.AxisListType

P = 128
N, E, H, ED, NH = 6250, 100000, 256, 64, 8
NB = -(-N // P)
NP = NB * P
PAD = NP - 1
HALF = 8
GROUP = 2 * HALF
NG = -(-E // (P * GROUP))
NT = NG * GROUP
NTX = NT + 2 * GROUP
HC = H // P
CH = 7
CQ = NT // CH
UNR = 7
NI = NB // UNR
NTAB = 4
SROWS = NP + 5 * P
SPIECE = SROWS // P // (NI - 1) * (H + 1)
UW = H + 1
XW = H + NH
PW = H + 2 * NH
EPS = 1e-5
SLOPE = 0.2
LOW = -1e30
NSPLIT = 3
WIN = 2
PACK = 4
PACKED = NTX // PACK
assert NB + 1 < 64 and NTX % PACK == 0
assert SROWS // P % (NI - 1) == 0
assert NB == NG
assert NB % UNR == 0 and NT % CH == 0


def flat(ap):
    return ap.rearrange("p o n -> p (o n)")


def nth(i, j):
    return i * UNR + (j + 1)


def pipeline(engine, stages):
    def one_pass(i, first):
        for j in range(UNR):
            for behind, stage in stages:
                if j >= behind:
                    stage(i, j - behind)
                elif not first:
                    stage(i - 1, UNR + j - behind)

    one_pass(0, True)
    with engine.Fori(1, NI) as i:
        one_pass(i, False)
    for j in range(UNR, UNR + max(behind for behind, _ in stages)):
        for behind, stage in stages:
            if 0 <= j - behind < UNR:
                stage(NI - 1, j - behind)


class Mem:

    def __init__(self, nc, stack, prefix=""):
        self.nc, self.stack, self.prefix, self.sems = nc, stack, prefix, []

    def sb(self, name, shape, dt=F32):
        return self.stack.enter_context(self.nc.sbuf_tensor(self.prefix + name, shape, dt))

    def ps(self, name, shape, dt=F32):
        return self.stack.enter_context(self.nc.psum_tensor(self.prefix + name, shape, dt))

    def sem(self, name):
        self.sems.append(self.stack.enter_context(self.nc.semaphore(self.prefix + name)))
        return self.sems[-1]

    def clear_sems(self):
        with self.nc.Block() as block:
            @block.gpsimd
            def _(pool):
                pool.sem_clear(range(self.sems[0].num, self.sems[-1].num + 1))


class Chain:

    def __init__(self, engine, sem, base=0):
        self.engine, self.sem, self.base, self.n = engine, sem, base, 0

    def link(self, instruction):
        self.n += 1
        instruction.then_inc(self.sem, 1)
        self.engine.wait_ge(self.sem, self.base + self.n)


def segment_max(nc, chain, value, start, width, run):
    chain.link(nc.vector.tensor_tensor_scan(run[:, 0:width], start[:, 0:width], value[:, 0:width], LOW, ALU.add, ALU.max))
    return nc.vector.tensor_tensor_scan(value[:, 0:width][:, ::-1], start[:, 1:width + 1][:, ::-1], run[:, 0:width][:, ::-1],
                                        LOW, ALU.add, ALU.max)


def running_sums(nc, chain, a, b, width):
    d = 1
    while d < width:
        chain.link(nc.vector.tensor_copy(b[:, 0:d], a[:, 0:d]))
        chain.link(nc.vector.tensor_tensor(b[:, d:width], a[:, d:width], a[:, 0:width - d], ALU.add))
        a, b, d = b, a, 2 * d
    return a


def split_float(nc, chain, source, rest, parts):
    chain.link(nc.vector.tensor_copy(parts[0], source))
    chain.link(nc.vector.tensor_tensor(rest, source, parts[0], ALU.subtract))
    chain.link(nc.vector.tensor_copy(parts[1], rest))
    chain.link(nc.vector.tensor_tensor(parts[2], rest, parts[1], ALU.subtract))


def unpack(nc, word):
    return [nc.s_assert_within((word // 64 ** n) % 64, 0, NB - 1,
                               skip_runtime_bounds_check_because="a rank is below the number of nodes") for n in range(PACK)]


def window_blocks(nc, pe, K, at):
    word = pe.value_load(K["blocks"][0:1, bass.ds(at, 1)], min_val=0, max_val=64 ** PACK - 1)
    return unpack(nc, word)


def setup_phase(nc, K, D, A):
    CLEAR = NSPLIT * H * (NP + P) // P // 6
    with ExitStack() as st:
        m = Mem(nc, st, "su_")
        rawi = {"src": m.sb("srci", [CQ, CH, P], I32), "dst": m.sb("dsti", [CQ, CH, P], I32)}
        rawf = {"src": m.sb("srcf", [CQ, CH, P]), "dst": m.sb("dstf", [CQ, CH, P])}
        padrow = m.sb("padrow", [NTX - NT, P])
        locpad = m.sb("locpad", [NTX - NT, P], BF16)
        minus = m.sb("minus", [1, P])
        w1 = m.sb("w1", [P, HC, 2 * H + ED])
        w1c2 = m.sb("w1c2", [P, HC, 2 * ED])
        w2 = m.sb("w2", [P, HC, H])
        wih = m.sb("wih", [P, 3 * HC, H])
        whh = m.sb("whh", [P, 3 * HC, H])
        wuv = m.sb("wuv", [2 * NH, H])
        W1abT = m.sb("W1abT", [P, HC, 2 * H])
        wihT = m.sb("wihT", [P, HC, 3 * H])
        b2col = m.sb("b2col", [P, HC])
        b2cols = m.sb("b2cols", [P, HC, P])
        zeros = m.sb("zeros", [P, CLEAR // 2])
        bias1 = m.sb("bias1", [P, H])
        xs = m.sb("xs", [P, UNR, H])
        xT = m.sb("xT", [P, UNR, H])
        a_rows = m.sb("a_rows", [P, UNR, H])
        b_rows = m.sb("b_rows", [P, UNR, H])
        b_rest = m.sb("b_rest", [P, UNR, H])
        parts = m.sb("parts", [P, UNR, NSPLIT * H], BF16)
        bhh = m.sb("bhh", [P, 2 * H])
        upto = m.sb("upto", [P, P])
        under = m.sb("under", [P, P])
        ones = m.sb("ones", [P, P])
        prev = m.sb("prev", [CQ, CH, P])
        fresh = m.sb("fresh", [CQ, CH, P])
        freshT = m.sb("freshT", [P, NT])
        count = m.sb("count", [CQ, CH, P])
        total = m.sb("total", [CQ, CH])
        run = [m.sb(f"run{i}", [CQ, CH]) for i in range(2)]
        before = m.sb("before", [CQ, CH])
        rank0 = m.sb("rank0", [CQ, CH])
        rank0_i = m.sb("rank0_i", [CQ, CH], I32)
        block = m.sb("block", [CQ, CH])
        shift = m.sb("shift", [CQ, CH])
        loc16 = m.sb("loc16", [CQ, CH, P], BF16)
        blockT = m.sb("blockT", [CH, CQ // PACK, PACK])
        word = m.sb("word", [CH, CQ // PACK])
        word_i = m.sb("word_i", [CH, CQ // PACK], I32)
        node = m.sb("node", [P, NB])
        column = m.sb("column", [P, P])
        node_i = m.sb("node_i", [P, NB], I32)
        column_i = m.sb("column_i", [P, P], I32)
        hi_i = m.sb("hi_i", [CQ, CH], I32)
        lo_i = m.sb("lo_i", [CQ, CH], I32)
        hi = m.sb("hi", [CQ, CH])
        lo = m.sb("lo", [CQ, CH])
        hotp = m.sb("hotp", [CQ, CH, P])
        hotb = m.sb("hotb", [CQ, CH, NB])
        hist = m.sb("hist", [P, NB])
        sums = [m.sb(f"sums{i}", [P, NB]) for i in range(2)]
        tile = m.sb("tile", [P, NB])
        tile_i = m.sb("tile_i", [P, NB], I32)
        rows = m.sb("rows", [P, NB, P])
        within = m.sb("within", [P, NB])
        edges_to = m.sb("edges_to", [P, NB])
        edges_before = m.sb("edges_before", [P, NB])
        begin = m.sb("begin", [P, NB])
        full = m.sb("full", [P, NB])
        cross = m.sb("cross", [P, NB])
        rank_i = m.sb("rank_i", [P, NB], I32)
        zero = m.sb("zero", [1, 1])

        psJ = [m.ps(f"psJ{i}", [P, 512]) for i in range(2)]
        psR = m.ps("psR", [P, 512])
        psK = m.ps("psK", [P, 512])
        psX = [m.ps(f"psX{i}", [P, 512]) for i in range(2)]
        psA = [m.ps(f"psA{i}", [P, 512]) for i in range(2)] + psJ
        edges_in, weights_in, bias_in = m.sem("edges_in"), m.sem("weights_in"), m.sem("bias_in")
        consts, masks, floats, rows_out = m.sem("consts"), m.sem("masks"), m.sem("floats"), m.sem("rows_out")
        prev_in, turned, kept, dve_step = m.sem("prev_in"), m.sem("turned"), m.sem("kept"), m.sem("dve_step")
        x_in = [m.sem(f"x_in{j}") for j in range(UNR)]
        x_turned, xT_ready, ab_done = m.sem("x_turned"), m.sem("xT_ready"), m.sem("ab_done")
        a_ready, b_ready, parts_ready = m.sem("a_ready"), m.sem("b_ready"), m.sem("parts_ready")
        hi_ready, rest_ready = m.sem("hi_ready"), m.sem("rest_ready")
        a_out = [m.sem(f"a_out{j}") for j in range(UNR)]
        b_out, gathered = K["b_out"], K["edges_gathered"]
        tables_clear, b_clear, ranked = m.sem("tables_clear"), m.sem("b_clear"), m.sem("ranked")
        ask, answer = m.sem("ask"), m.sem("answer")
        loc_out, words_out, words_in = m.sem("loc_out"), m.sem("words_out"), m.sem("words_in")
        edges_ready, edges_out, before_in = m.sem("edges_ready"), m.sem("edges_out"), m.sem("before_in")

        jobs = []
        for o in range(HC):
            cols = slice(o * P, (o + 1) * P)
            for k in range(2 * HC):
                at = (k // HC) * H + o * P
                jobs.append((w1[:, o, k * P:(k + 1) * P], W1abT[:, k % HC, at:at + P]))
            jobs.append((w1c2[:, o, :], K["W1cT"][:, cols]))
        for o in range(3 * HC):
            for k in range(HC):
                jobs.append((wih[:, o, k * P:(k + 1) * P], wihT[:, k, o * P:(o + 1) * P]))
                jobs.append((whh[:, o, k * P:(k + 1) * P], K["WhhT"][:, k, o * P:(o + 1) * P]))
        jobs += [(wuv[:, k * P:(k + 1) * P], K["WuvT"][:, k, :]) for k in range(HC)]
        HALF3 = 3 * H // 2
        products = []
        for n in range(2):
            cols = slice(n * HALF3, (n + 1) * HALF3)
            products += [([w2[:, k, o * P:(o + 1) * P] for k in range(HC)], cols, K["WcT"][:, o, cols]) for o in range(HC)]
            products.append(([b2cols[:, k, :] for k in range(HC)], cols, K["b2ih"][:, cols]))

        b_clears = NSPLIT * H * (NP + P) // P // CLEAR
        phase = ExitStack()
        blk = phase.enter_context(nc.Block())

        @blk.sync
        def _(sp):
            sp.wait_ge(consts, 2)
            whole = (CH - 1) * CQ * P
            tail = (E - whole) // P
            for name in ("dst", "src"):
                e = A[name]
                sp.dma_start(rawi[name][:, 0:CH - 1, :],
                             e[0:whole].rearrange("(c q p) -> q c p", q=CQ, p=P)).then_inc(edges_in, 16)
                sp.dma_start(rawi[name][0:tail, CH - 1, :],
                             e[whole:whole + tail * P].rearrange("(q p) -> q p", p=P)).then_inc(edges_in, 16)
                sp.dma_start(rawi[name][tail:tail + 1, CH - 1, 0:E - whole - tail * P],
                             e[whole + tail * P:E].rearrange("(q p) -> q p", q=1)).then_inc(edges_in, 16)
            sp.dma_start(w1[:, :, :], A["W1"].rearrange("(o p) k -> p o k", p=P)).then_inc(weights_in, 16)
            for n in range(2):
                sp.dma_start(w1c2[:, :, n * ED:(n + 1) * ED],
                             A["W1"][:, 2 * H:2 * H + ED].rearrange("(o p) k -> p o k", p=P)).then_inc(weights_in, 16)
            for j in range(UNR):
                sp.dma_start(xs[:, j, :], A["x"][j * P:(j + 1) * P, :]).then_inc(x_in[j], 16)
            sp.dma_start(w2[:, :, :], A["W2"].rearrange("(o p) k -> p o k", p=P)).then_inc(weights_in, 16)
            sp.dma_start(wih[:, :, :], A["W_ih"].rearrange("(o p) k -> p o k", p=P)).then_inc(weights_in, 16)
            sp.dma_start(whh[:, :, :], A["W_hh"].rearrange("(o p) k -> p o k", p=P)).then_inc(weights_in, 16)
            sp.dma_start(wuv[0:NH, :], A["W_u"]).then_inc(weights_in, 16)
            sp.dma_start(wuv[NH:2 * NH, :], A["W_v"]).then_inc(weights_in, 16)

            def load_x(i, j, rows):
                sp.wait_ge(x_turned, i * UNR + (j + 1))
                sp.dma_start(xs[0:rows, j, :], A["x"][bass.ds(i * (UNR * P) + (UNR + j) * P, rows), :]).then_inc(x_in[j], 16)

            def store_a(i, j):
                sp.wait_ge(a_ready, i * UNR + (j + 1))
                sp.dma_start(D["A"][bass.ds(i * (UNR * P) + j * P, P), :], a_rows[:, j, :]).then_inc(a_out[j], 16)

            with sp.Fori(0, NI - 2) as i:
                for j in range(UNR):
                    load_x(i, j, P)
                    store_a(i, j)
            for j in range(UNR):
                load_x(NI - 2, j, P if j < UNR - 1 else N - (NB - 1) * P)
                store_a(NI - 2, j)
            for j in range(UNR):
                store_a(NI - 1, j)
            for j in range(UNR):
                sp.wait_ge(a_out[j], 16 * NI)

        @blk.gpsimd
        def _(pool):
            nc.gpsimd.memset(K["ident"][:, :], 0.0).then_inc(masks, 1)
            for mat in (K["before"], upto, under):
                nc.gpsimd.memset(mat[:, :], 1.0).then_inc(masks, 1)
            nc.gpsimd.iota(node_i[:, :], pattern=[[P, NB]], base=0, channel_multiplier=1).then_inc(masks, 1)
            nc.gpsimd.iota(column_i[:, :], pattern=[[1, P]], base=0, channel_multiplier=0).then_inc(masks, 1)
            pool.wait_ge(masks, 6)
            for mat, op, fill, sign in ((K["ident"], ALU.not_equal, 1.0, 1), (K["before"], ALU.is_gt, 0.0, 1),
                                        (upto, ALU.is_ge, 0.0, -1), (under, ALU.is_gt, 0.0, -1)):
                nc.gpsimd.affine_select(out=mat[:, :], in_=mat[:, :], compare_op=op, fill=fill, base=0,
                                        pattern=[[-sign, P]], channel_multiplier=sign).then_inc(masks, 1)
            pool.wait_ge(ask, 4)
            for b in range(NB):
                pool.indirect_dma_start(rows[:, b, :], None, D["dst_rows"],
                                        bass.IndirectOffsetOnAxis(ap=tile_i[:, b:b + 1], axis=0)).then_inc(gathered, 16)
            pool.wait_ge(gathered, 16 * NB)
            pool.wait_ge(ranked, 1)
            pool.wait_ge(b_clear, 16 * b_clears)
            for b in range(NB):
                pool.wait_ge(parts_ready, b + 1)
                pool.indirect_dma_start(D["B"], bass.IndirectOffsetOnAxis(ap=rank_i[:, b:b + 1], axis=0),
                                        parts[:, b % UNR, :], None).then_inc(b_out[b % UNR], 16)
            for j in range(UNR):
                pool.wait_ge(b_out[j], 16 * NI)

        @blk.scalar
        def _(act):
            act.wait_ge(floats, 1)
            act.dma_start(D["dst_rows"][1:NT + 1, :].rearrange("(c q) p -> q c p", q=CQ), rawf["dst"][:, :, :]).then_inc(rows_out, 16)
            act.dma_start(D["dst_rows"][0:1, :], minus[:, :]).then_inc(rows_out, 16)
            act.wait_ge(rows_out, 32)
            flat_dst = D["dst_rows"].rearrange("t p -> (t p)")
            act.dma_start(prev[:, :, :], flat_dst[P - 1:P - 1 + NT * P].rearrange("(c q p) -> q c p", q=CQ, p=P)).then_inc(prev_in, 16)
            act.wait_ge(floats, 2)
            act.dma_start(D["src_rows"][0:NT, :].rearrange("(c q) p -> q c p", q=CQ), rawf["src"][:, :, :]).then_inc(rows_out, 16)
            act.dma_start(D["src_rows"][NT:NTX, :], padrow[:, :]).then_inc(rows_out, 16)
            with nc.allow_non_contiguous_dma(reason="one word of each tile"):
                act.dma_start(D["last"], D["dst_rows"][1:NT + 1, P - 1:P]).then_inc(rows_out, 16)
            act.dma_start(bias1[:, :], A["b1"].partition_broadcast(P)).then_inc(bias_in, 16)
            act.dma_start(K["bgate"][:, 0:3 * H], A["b_ih"].partition_broadcast(P)).then_inc(bias_in, 16)
            act.dma_start(bhh[:, :], A["b_hh"][0:2 * H].partition_broadcast(P)).then_inc(bias_in, 16)
            act.dma_start(K["bgate"][:, 3 * H:4 * H], A["b_hh"][2 * H:3 * H].partition_broadcast(P)).then_inc(bias_in, 16)
            act.dma_start(K["bu"][:, 0:NH], A["b_u"].partition_broadcast(P)).then_inc(bias_in, 16)
            with nc.allow_non_contiguous_dma(reason="256 words over the partitions"):
                act.dma_start(b2col[:, :], A["b2"].rearrange("(o p) -> p o", p=P)).then_inc(bias_in, 16)
            b_table = D["B"].rearrange("n w -> (n w)").rearrange("(p r w) -> p r w", p=P, w=CLEAR)
            for r in range(b_table.shape[1]):
                act.dma_start(b_table[:, r, :], zeros[:, :].bitcast(BF16)).then_inc(b_clear, 16)
            act.dma_start(D["sv"].rearrange("n w -> (n w)").rearrange("(p w) -> p w", p=P), zeros[:, 0:(NP + P) * NH // P]).then_inc(tables_clear, 16)
            def clear_sums(t, piece):
                v = D[f"S{t}"].rearrange("n w -> (n w)").rearrange("(p r w) -> p r w", p=P, w=SPIECE)
                act.dma_start(v[:, bass.ds(piece, 1), :], zeros[:, 0:SPIECE].unsqueeze(1)).then_inc(tables_clear, 16)

            act.wait_ge(ask, 6)
            act.dma_start(D["loc_rows"][0:NT, :].rearrange("(c q) p -> q c p", q=CQ), loc16[:, :, :]).then_inc(loc_out, 16)
            act.dma_start(D["loc_rows"][NT:NTX, :], locpad[:, :]).then_inc(loc_out, 16)
            act.wait_ge(ask, 7)
            act.dma_start(D["blocks"].rearrange("(c n) o -> c (n o)", c=CH), word_i[:, :]).then_inc(words_out, 16)
            act.wait_ge(words_out, 16)
            act.dma_start(K["blocks"][0:1, 0:NT // PACK], D["blocks"].rearrange("n o -> o n")).then_inc(words_in, 16)
            for t in range(NTAB // 2):
                for piece in range(NI - 1):
                    clear_sums(t, piece)
            act.wait_ge(edges_ready, 1)
            with nc.allow_non_contiguous_dma(reason="the nodes are over partitions"):
                act.dma_start(D["upto"][0:1, :], zero[:, :]).then_inc(edges_out, 16)
                act.dma_start(D["upto"][1:NP + 1, :].rearrange("(b p) o -> p (b o)", p=P), edges_to[:, :]).then_inc(edges_out, 16)
                act.wait_ge(edges_out, 32)
                act.dma_start(edges_before[:, :], D["upto"][0:NP, :].rearrange("(b p) o -> p (b o)", p=P)).then_inc(before_in, 16)
            def keep(i, j):
                act.wait_ge(b_ready, i * UNR + (j + 1))
                act.wait_ge(a_out[j], i * 16)
                nc.scalar.copy(a_rows[:, j, :], psA[j % 4][:, 0:H]).then_inc(a_ready, 1)
                act.wait_ge(b_out[j], i * 16)
                nc.scalar.copy(parts[:, j, 0:H], b_rows[:, j, :]).then_inc(hi_ready, 1)

            def keep_xT(i, j):
                act.wait_ge(x_turned, nth(i, j))
                nc.scalar.copy(xT[:, j, :], psX[j % 2][:, 0:H]).then_inc(xT_ready, 1)

            def clear_rest(i, j):
                if j % 3 == 1 and j // 3 < NTAB // 2 and not (isinstance(i, int) and i == 0):
                    clear_sums(NTAB // 2 + j // 3, i - 1)

            pipeline(act, [(0, keep_xT), (2, keep), (0, clear_rest)])
            act.wait_ge(tables_clear, 16 * (NTAB * (NI - 1) + 1))
            act.wait_ge(rows_out, 80)
            act.wait_ge(loc_out, 32)
            act.wait_ge(words_in, 16)

        @blk.tensor
        def _(pe):
            def turn(source, target):
                nrows, ncols = source.shape
                return nc.tensor.transpose(target[0:ncols, 0:nrows], source, K["ident"][0:nrows, 0:nrows])

            pe.wait_ge(masks, 10)
            pe.wait_ge(ask, 1)
            for c in range(4):
                turn(fresh[:, c, :], psR[:, c * CQ:(c + 1) * CQ])
            for c in range(4, CH):
                t = turn(fresh[:, c, :], psK[:, (c - 4) * CQ:(c - 3) * CQ])
            t.then_inc(answer, 1)
            pe.wait_ge(ask, 2)
            for c in range(CH):
                t = nc.tensor.matmul(psR[:, 0:NB], hotp[:, c, :], hotb[:, c, :], start=(c == 0), stop=(c == CH - 1))
            t.then_inc(answer, 1)
            pe.wait_ge(ask, 3)
            nc.tensor.matmul(psR[:, 0:NB], upto[:, :], hist[:, :], start=True, stop=False)
            nc.tensor.matmul(psR[:, 0:NB], ones[:, :], sums[1][:, :], start=False, stop=True).then_inc(answer, 1)
            pe.wait_ge(ask, 4)
            for c in range(CH):
                bank, at = (psR, c) if c < 4 else (psK, c - 4)
                t = nc.tensor.matmul(bank[0:CQ, at * P:(at + 1) * P], freshT[:, c * CQ:(c + 1) * CQ], upto[:, :], start=True, stop=True)
            t.then_inc(answer, 1)
            pe.wait_ge(ask, 5)
            nc.tensor.matmul(psR[0:CQ, 0:CH], under[0:CQ, 0:CQ], total[:, :], start=True, stop=False)
            nc.tensor.matmul(psR[0:CQ, 0:CH], ones[0:CQ, 0:CQ], before[:, :], start=False, stop=True).then_inc(answer, 1)
            pe.wait_ge(ask, 6)
            for c in range(4):
                turn(count[:, c, :], psR[:, c * CQ:(c + 1) * CQ])
            for c in range(4, CH):
                turn(count[:, c, :], psK[:, (c - 4) * CQ:(c - 3) * CQ])
            turn(block[:, :], psK[:, 3 * CQ:4 * CQ]).then_inc(answer, 1)
            pe.wait_ge(ask, 7)
            for c in range(4):
                turn(rawf["src"][:, c, :], psR[:, c * CQ:(c + 1) * CQ])
            for c in range(4, CH):
                t = turn(rawf["src"][:, c, :], psK[:, (c - 4) * CQ:(c - 3) * CQ])
            t.then_inc(answer, 1)
            pe.wait_ge(weights_in, 128)
            for n, (source, _) in enumerate(jobs):
                if n >= 2:
                    pe.wait_ge(kept, n - 1)
                turn(source, psJ[n % 2]).then_inc(turned, 1)
            pe.wait_ge(kept, len(jobs))
            for n, (stationary, cols, _) in enumerate(products):
                if n >= 2:
                    pe.wait_ge(kept, len(jobs) + n - 1)
                for k in range(HC):
                    t = nc.tensor.matmul(psJ[n % 2][:, 0:HALF3], stationary[k], wihT[:, k, cols], start=(k == 0), stop=(k == HC - 1))
                t.then_inc(turned, 1)
            pe.wait_ge(ask, 8)
            nc.tensor.matmul(psR[:, 0:NB], upto[:, :], K["any"][:, :], start=True, stop=False)
            nc.tensor.matmul(psR[:, 0:NB], ones[:, :], sums[1][:, :], start=False, stop=True).then_inc(answer, 1)
            def turn_x(i, j):
                pe.wait_ge(xT_ready, i * UNR + max(j - 1, 0))
                pe.wait_ge(x_in[j], i * 16 + 16)
                for k in range(HC):
                    t = nc.tensor.transpose(psX[j % 2][:, k * P:(k + 1) * P], xs[:, j, k * P:(k + 1) * P], K["ident"][:, :])
                t.then_inc(x_turned, 1)

            def project(i, j):
                pe.wait_ge(xT_ready, nth(i, j))
                pe.wait_ge(a_ready, i * UNR + (j - 2) if j >= 2 else i * UNR)
                for k in range(HC):
                    t = nc.tensor.matmul(psA[j % 4][:, :], xT[:, j, k * P:(k + 1) * P], W1abT[:, k, :],
                                         start=(k == 0), stop=(k == HC - 1))
                t.then_inc(ab_done, 1)

            pipeline(pe, [(0, turn_x), (1, project)])

        @blk.vector
        def _(dve):
            c = Chain(dve, dve_step)
            link = c.link

            def asked(n, ins=None):
                ins.then_inc(ask, 1)
                dve.wait_ge(answer, n)

            nc.vector.memset(rawi["dst"][:, :, :], PAD).then_inc(consts, 1)
            nc.vector.memset(rawi["src"][:, :, :], PAD).then_inc(consts, 1)
            nc.vector.memset(minus[:, :], -1.0)
            nc.vector.memset(padrow[:, :], float(PAD))
            nc.vector.memset(locpad[:, :], 0.0)
            nc.vector.memset(zero[:, :], 0.0)
            nc.vector.memset(ones[:, :], 1.0)
            nc.vector.memset(K["bu"][:, NH:2 * NH], 0.0)
            nc.vector.memset(K["eps"][:, :], EPS)
            nc.vector.memset(K["neghalf"][:, :], -0.5)
            nc.vector.memset(K["srcT"][:, NT:NTX], float(PAD))
            nc.vector.memset(K["locT"][:, NT:NTX], 0.0)
            nc.vector.memset(K["blocks"][:, :], 0)
            nc.vector.memset(K["own_row"][:, NB:], 0.0)
            nc.vector.memset(K["ends_row"][:, NB:], 0.0)
            nc.vector.memset(zeros[:, :], 0.0)
            dve.wait_ge(edges_in, 96)
            nc.vector.tensor_copy(rawf["dst"][:, :, :], rawi["dst"][:, :, :]).then_inc(floats, 1)
            nc.vector.tensor_copy(rawf["src"][:, :, :], rawi["src"][:, :, :]).then_inc(floats, 1)
            nc.vector.tensor_scalar(hi_i[:, :], rawi["dst"][:, :, 0], 7, None, ALU.arith_shift_right)
            link(nc.vector.tensor_scalar(lo_i[:, :], rawi["dst"][:, :, 0], P - 1, None, ALU.bitwise_and))
            nc.vector.tensor_copy(hi[:, :], hi_i[:, :])
            nc.vector.tensor_copy(lo[:, :], lo_i[:, :])
            dve.wait_ge(masks, 6)
            nc.vector.tensor_copy(node[:, :], node_i[:, :])
            link(nc.vector.tensor_copy(column[:, :], column_i[:, :]))
            nc.vector.tensor_scalar(K["winid"][:, 0:1], node[:, 0:1], 0.0, None, ALU.add)
            nc.vector.tensor_scalar(K["winid"][:, 1:2], node[:, 0:1], float(P), None, ALU.add)
            nc.vector.tensor_scalar(K["spare"][:, :], node[:, 0:1], float(NP), None, ALU.add)
            nc.vector.tensor_tensor(hotp[:, :, :], column[0:CQ, :].unsqueeze(1).to_broadcast([CQ, CH, P]),
                                    lo[:, :].unsqueeze(2).to_broadcast([CQ, CH, P]), ALU.is_equal)
            link(nc.vector.tensor_tensor(hotb[:, :, :], column[0:CQ, 0:NB].unsqueeze(1).to_broadcast([CQ, CH, NB]),
                                         hi[:, :].unsqueeze(2).to_broadcast([CQ, CH, NB]), ALU.is_equal))
            dve.wait_ge(prev_in, 16)
            asked(1, nc.vector.tensor_tensor(fresh[:, :, :], rawf["dst"][:, :, :], prev[:, :, :], ALU.not_equal))
            nc.vector.tensor_copy(freshT[:, 0:4 * CQ], psR[:, 0:4 * CQ])
            asked(2, nc.vector.tensor_copy(freshT[:, 4 * CQ:NT], psK[:, 0:3 * CQ]))
            nc.vector.tensor_scalar(K["startT"][:, :], freshT[:, :], LOW, None, ALU.mult)

            def prefix(n, values):
                link(nc.vector.tensor_copy(sums[0][:, :], values))
                total_to = running_sums(nc, c, sums[0], sums[1], NB)
                assert total_to is sums[0]
                asked(n, nc.vector.tensor_tensor(sums[1][:, :], sums[0][:, :], values, ALU.subtract))

            link(nc.vector.tensor_copy(hist[:, :], psR[:, 0:NB]))
            prefix(3, hist[:, :])
            link(nc.vector.tensor_scalar(tile[:, :], psR[:, 0:NB], -1.0, 0.0, ALU.add, ALU.max))
            asked(4, nc.vector.tensor_scalar(tile_i[:, :], tile[:, :], 1.0, None, ALU.add))
            nc.vector.tensor_copy(count[:, 0:4, :], psR[0:CQ, :].rearrange("q (c p) -> q c p", p=P))
            link(nc.vector.tensor_copy(count[:, 4:CH, :], psK[0:CQ, 0:3 * P].rearrange("q (c p) -> q c p", p=P)))
            link(nc.vector.tensor_copy(total[:, :], count[:, :, P - 1]))
            link(nc.vector.tensor_copy(run[0][:, :], total[:, :]))
            run_to = running_sums(nc, c, run[0], run[1], CH)
            asked(5, nc.vector.tensor_tensor(before[:, :], run_to[:, :], total[:, :], ALU.subtract))
            link(nc.vector.tensor_copy(total[:, :], psR[0:CQ, 0:CH]))
            link(nc.vector.tensor_tensor(rank0[:, :], total[:, :], fresh[:, :, 0], ALU.add))
            link(nc.vector.tensor_scalar(rank0_i[:, :], rank0[:, :], -1.0, None, ALU.add))
            link(nc.vector.tensor_scalar(hi_i[:, :], rank0_i[:, :], 7, None, ALU.arith_shift_right))
            link(nc.vector.tensor_scalar(block[:, :], hi_i[:, :], float(NB - 1), None, ALU.min))
            link(nc.vector.tensor_scalar(shift[:, :], block[:, :], -float(P), -1.0, ALU.mult, ALU.add))
            link(nc.vector.tensor_tensor(shift[:, :], shift[:, :], total[:, :], ALU.add))
            link(nc.vector.tensor_tensor(count[:, :, :], count[:, :, :], shift[:, :].unsqueeze(2).to_broadcast([CQ, CH, P]), ALU.add))
            asked(6, nc.vector.tensor_copy(loc16[:, :, :], count[:, :, :]))
            nc.vector.tensor_copy(K["locT"][:, 0:4 * CQ], psR[:, 0:4 * CQ])
            nc.vector.tensor_copy(K["locT"][:, 4 * CQ:NT], psK[:, 0:3 * CQ])
            link(nc.vector.tensor_copy(blockT[:, :, :], psK[0:CH, 3 * CQ:4 * CQ].rearrange("c (n k) -> c n k", k=PACK)))
            link(nc.vector.tensor_copy(word[:, :], blockT[:, :, PACK - 1]))
            for k in reversed(range(PACK - 1)):
                link(nc.vector.scalar_tensor_tensor(word[:, :], word[:, :], 64.0, blockT[:, :, k], ALU.mult, ALU.add))
            asked(7, nc.vector.tensor_copy(word_i[:, :], word[:, :]))
            nc.vector.tensor_copy(K["srcT"][:, 0:4 * CQ], psR[:, 0:4 * CQ])
            link(nc.vector.tensor_copy(K["srcT"][:, 4 * CQ:NT], psK[:, 0:3 * CQ]))
            dve.wait_ge(bias_in, 96)
            nc.vector.tensor_copy(b2cols[:, :, :], b2col[:, :].unsqueeze(2).to_broadcast([P, HC, P]))
            for n, (source, target) in enumerate(jobs):
                nrows, ncols = source.shape
                dve.wait_ge(turned, n + 1)
                nc.vector.tensor_copy(target, psJ[n % 2][0:ncols, 0:nrows]).then_inc(kept, 1)
            for n, (_, _, target) in enumerate(products):
                dve.wait_ge(turned, len(jobs) + n + 1)
                nc.vector.tensor_copy(target, psJ[n % 2][:, 0:HALF3]).then_inc(kept, 1)
            link(nc.vector.tensor_tensor(K["bgate"][:, 0:2 * H], K["bgate"][:, 0:2 * H], bhh[:, :], ALU.add))
            dve.wait_ge(gathered, 16 * NB)
            link(nc.vector.tensor_tensor(rows[:, :, :], rows[:, :, :], node[:, :].unsqueeze(2).to_broadcast([P, NB, P]), ALU.is_le))
            link(nc.vector.tensor_reduce(within[:, :], rows[:, :, :], AX.X, ALU.add))
            link(nc.vector.tensor_scalar(begin[:, :], tile[:, :], float(P), None, ALU.mult))
            nc.vector.tensor_tensor(edges_to[:, :], begin[:, :], within[:, :], ALU.add).then_inc(edges_ready, 1)
            dve.wait_ge(before_in, 16)
            dve.wait_ge(edges_ready, 1)
            link(nc.vector.tensor_tensor(K["any"][:, :], edges_to[:, :], edges_before[:, :], ALU.is_gt))
            prefix(8, K["any"][:, :])
            link(nc.vector.tensor_scalar(cross[:, :], psR[:, 0:NB], -1.0, K["spare"][:, 0:1], ALU.add, ALU.subtract))
            link(nc.vector.tensor_tensor(cross[:, :], cross[:, :], K["any"][:, :], ALU.mult))
            link(nc.vector.tensor_scalar(K["rank"][:, :], cross[:, :], K["spare"][:, 0:1], None, ALU.add))
            nc.vector.tensor_copy(rank_i[:, :], K["rank"][:, :]).then_inc(ranked, 1)
            def split(i, j):
                dve.wait_ge(hi_ready, i * UNR + (j + 1))
                nc.vector.tensor_tensor(b_rest[:, j, :], b_rows[:, j, :], parts[:, j, 0:H], ALU.subtract).then_inc(rest_ready, 1)
                dve.wait_ge(rest_ready, i * (2 * UNR) + (2 * j + 1))
                nc.vector.tensor_copy(parts[:, j, H:2 * H], b_rest[:, j, :]).then_inc(rest_ready, 1)
                dve.wait_ge(rest_ready, i * (2 * UNR) + (2 * j + 2))
                nc.vector.tensor_tensor(parts[:, j, 2 * H:3 * H], b_rest[:, j, :], parts[:, j, H:2 * H],
                                        ALU.subtract).then_inc(parts_ready, 1)

            def add_bias(i, j):
                dve.wait_ge(ab_done, nth(i, j))
                nc.vector.tensor_tensor(b_rows[:, j, :], psA[j % 4][:, H:2 * H], bias1[:, :], ALU.add).then_inc(b_ready, 1)

            pipeline(dve, [(1, add_bias), (3, split)])
            link(nc.vector.tensor_scalar(full[:, :], within[:, :], float(P), None, ALU.is_equal))
            dve.wait_ge(ranked, 1)
            link(nc.vector.tensor_tensor(cross[:, :], edges_before[:, :], begin[:, :], ALU.is_lt))
            link(nc.vector.tensor_tensor(cross[:, :], cross[:, :], full[:, :], ALU.max))
            link(nc.vector.tensor_tensor(K["ends"][:, :], cross[:, :], K["any"][:, :], ALU.mult))
            link(nc.vector.tensor_scalar(cross[:, :], full[:, :], -1.0, 1.0, ALU.mult, ALU.add))
            link(nc.vector.tensor_tensor(K["own"][:, :], cross[:, :], K["any"][:, :], ALU.mult))
            link(nc.vector.tensor_scalar(K["own_row"][:, 0:NB], edges_to[:, :], -1.0, 0.0, ALU.add, ALU.max))
            link(nc.vector.tensor_tensor(tile[:, :], tile[:, :], cross[:, :], ALU.subtract))
            link(nc.vector.tensor_scalar(K["ends_row"][:, 0:NB], tile[:, :], 0.0, None, ALU.max))
        phase.close()
        m.clear_sems()


def layer0_phase(nc, K, D, A):
    with ExitStack() as st:
        m = Mem(nc, st, "l0_")
        SLOTS = GROUP
        RING = 8
        ga = m.sb("ga", [P, SLOTS, H])
        table = m.sb("table", [P, NB + 1, NSPLIT * H], BF16)
        locb = [m.sb(f"locb{h}", [P, HALF, P], BF16) for h in range(2)]
        onehot = [m.sb(f"onehot{h}", [P, WIN, HALF, P], BF16) for h in range(2)]
        gsrc = [m.sb(f"gsrc{h}", [P, HALF], I32) for h in range(2)]
        sink = [m.sb(f"sink{h}", [P, HALF], I32) for h in range(2)]
        srcb = [m.sb(f"srcb{h}", [P, HALF, P]) for h in range(2)]
        same = [m.sb(f"same{h}", [P, HALF, P]) for h in range(2)]
        attr = [m.sb(f"attr{h}", [P, HALF, ED]) for h in range(2)]
        earlier = m.sb("earlier", [P, HALF, P])
        dup = m.sb("dup", [P, HALF])
        togo = m.sb("togo", [P, HALF])
        attrT = [m.sb(f"attrT{q}", [2 * ED, 2 * P]) for q in range(2)]
        hid = m.sb("hid", [P, RING, UW])
        msum = m.sb("msum", [P, RING, UW])
        xg = m.sb("xg", [P, H])
        xgT = m.sb("xgT", [P, H])
        hidden = m.sb("hidden", [P, 3 * H])
        psT = m.ps("psT", [P, 512])
        psG = m.ps("psG", [P, 512])
        xg_in, xg_turned, xgT_ready = m.sem("xg_in"), m.sem("xg_turned"), m.sem("xgT_ready")
        hidden_done, hidden_kept, hidden_out = m.sem("hidden_done"), m.sem("hidden_kept"), m.sem("hidden_out")
        psC = [m.ps(f"psC{q}", [P, 512]) for q in range(4)]
        psU = [m.ps(f"psU{q}", [P, 512]) for q in range(2)]
        gathered = [m.sem(f"gathered{s}") for s in range(SLOTS)]
        scattered = [m.sem(f"scattered{t}") for t in range(NTAB)]
        src_in = [m.sem(f"src_in{h}") for h in range(2)]
        table_in = m.sem("table_in")
        FIRST = GROUP + 2
        onehot_ready = m.sem("onehot_ready")
        attr_in = [m.sem(f"attr_in{h}") for h in range(2)]
        index_ready = m.sem("index_ready")
        same_ready, sink_ready = m.sem("same_ready"), m.sem("sink_ready")
        dve_step = m.sem("dve_step")
        pre_ready = m.sem("pre_ready")
        hid_ready = m.sem("hid_ready")
        attr_turned = m.sem("attr_turned")
        attrT_ready = m.sem("attrT_ready")
        c_done = m.sem("c_done")
        agg_done = m.sem("agg_done")
        msum_ready = m.sem("msum_ready")
        ones = m.sem("ones")
        scatter_waited, gather_waited = m.sem("scatter_waited"), m.sem("gather_waited")
        attr_end = m.sem("attr_end")
        block = st.enter_context(nc.Block())

        HIDDEN_AT = [3, 4, 7, 8, 11, 12]

        def pc(t):
            return psC[t % 4][:, 0:H]

        @block.sync
        def _(sp):
            def src_rows(h, row):
                sp.dma_start(srcb[h][:, :, :].rearrange("p t e -> p (t e)"),
                             D["src_rows"][row, :].rearrange("t e -> (t e)").partition_broadcast(P)).then_inc(src_in[h], 16)
                sp.dma_start(locb[h][:, :, :].rearrange("p t e -> p (t e)"),
                             D["loc_rows"][row, :].rearrange("t e -> (t e)").partition_broadcast(P)).then_inc(src_in[h], 16)

            def attr_tiles(h, edge):
                sp.dma_start(attr[h][:, :, :],
                             A["edge_attr"][edge, :].rearrange("(t p) d -> p t d", p=P)).then_inc(attr_in[h], 16)

            by_block = D["B"].rearrange("(b p) w -> p b w", p=P)
            def load_xg(block, rows=P):
                sp.dma_start(xg[0:rows, :], A["x"][bass.ds(block * P, rows), :]).then_inc(xg_in, 16)

            def store_hidden(g):
                sp.wait_ge(hidden_kept, g * 3 + 3)
                sp.dma_start(D["GH"][bass.ds(g * P, P), :], hidden[:, :]).then_inc(hidden_out, 16)

            for h in range(2):
                src_rows(h, slice(h * HALF, (h + 1) * HALF))
                attr_tiles(h, slice(h * HALF * P, (h + 1) * HALF * P))
                if h == 0:
                    sp.dma_start(table[:, 0:FIRST, :], by_block[:, 0:FIRST, :]).then_inc(table_in, 16)
            sp.sem_inc(hidden_out, 16)
            load_xg(0)
            sp.wait_ge(pre_ready, 1)
            sp.dma_start(table[:, FIRST:, :], by_block[:, FIRST:, :]).then_inc(table_in, 16)
            with sp.Fori(0, NG - 2) as g:
                for h in range(2):
                    sp.wait_ge(same_ready, g * 2 + (h + 1))
                    src_rows(h, bass.ds(g * GROUP + (GROUP + h * HALF), HALF))
                    sp.wait_ge(attr_turned, g * 4 + 2 * (h + 1))
                    attr_tiles(h, bass.ds(g * (GROUP * P) + (GROUP + h * HALF) * P, HALF * P))
                sp.wait_ge(xg_turned, g + 1)
                load_xg(g + 1)
                store_hidden(g)
            g = NG - 2
            for h in range(2):
                sp.wait_ge(same_ready, g * 2 + (h + 1))
                src_rows(h, slice((g + 1) * GROUP + h * HALF, (g + 1) * GROUP + (h + 1) * HALF))
                sp.wait_ge(attr_turned, g * 4 + 2 * (h + 1))
                first = (g + 1) * GROUP * P + h * HALF * P
                if h == 0:
                    attr_tiles(h, slice(first, first + HALF * P))
                else:
                    whole = (E - first) // P
                    sp.dma_start(attr[h][0:E - first - whole * P, whole, :],
                                 A["edge_attr"][first + whole * P:E, :]).then_inc(attr_end, 16)
                    sp.wait_ge(attr_end, 16)
                    sp.dma_start(attr[h][:, 0:whole, :],
                                 A["edge_attr"][first:first + whole * P, :].rearrange("(t p) d -> p t d", p=P)).then_inc(attr_in[h], 16)
            sp.wait_ge(xg_turned, NB - 1)
            load_xg(NB - 1, N - (NB - 1) * P)
            store_hidden(NB - 2)
            sp.wait_ge(same_ready, 2 * NG - 1)
            src_rows(0, slice(NT, NT + HALF))
            sp.wait_ge(attr_turned, 4 * NG - 2)
            attr_tiles(0, slice(0, HALF * P))
            store_hidden(NB - 1)
            sp.wait_ge(hidden_out, 16 * NB + 16)
            sp.wait_ge(src_in[0], 32 * (NG + 1))
            sp.wait_ge(attr_in[0], 16 * (NG + 1))

        @block.gpsimd
        def _(pool):
            def gather(j):
                s, h = j % SLOTS, j // HALF
                pool.indirect_dma_start(ga[:, s, :], None, D["A"],
                                        bass.IndirectOffsetOnAxis(ap=gsrc[h][:, j % HALF:j % HALF + 1], axis=0)).then_inc(gathered[s], 16)

            pool.sem_inc(scatter_waited, RING)
            pool.wait_ge(index_ready, 2)
            for j in range(SLOTS):
                gather(j)

            def group(g, first=False, last=False):
                for j in range(GROUP):
                    if j % HALF == 0:
                        pool.wait_ge(sink_ready, g * 2 + (j // HALF + 1))
                    pool.wait_ge(msum_ready, g * GROUP + (j + 1))
                    if j >= NTAB or not first:
                        pool.wait_ge(scattered[j % NTAB], g * (16 * GROUP // NTAB) + 16 * (j // NTAB))
                    pool.sem_inc(scatter_waited, 1)
                    pool.indirect_dma_start(D[f"S{j % NTAB}"],
                                            bass.IndirectOffsetOnAxis(ap=sink[j // HALF][:, j % HALF:j % HALF + 1], axis=0),
                                            msum[:, j % RING, :], None, compute_op=ALU.add).then_inc(scattered[j % NTAB], 16)
                    if last:
                        continue
                    if j == 0 or j == HALF:
                        pool.wait_ge(index_ready, g * 2 + (3 + j // HALF))
                    pool.wait_ge(hid_ready, g * GROUP + (j + 1))
                    pool.sem_inc(gather_waited, 1)
                    gather((j + SLOTS) % GROUP)

            group(0, first=True)
            with pool.Fori(1, NG - 1) as g:
                group(g)
            group(NG - 1, last=True)
            for t in range(NTAB):
                pool.wait_ge(scattered[t], 16 * NT // NTAB)
            for s in range(SLOTS):
                pool.wait_ge(gathered[s], 16 * (NT // SLOTS))

        @block.tensor
        def _(pe):
            def turn(g, q):
                h, at = q % 4 // 2, q % 2 * 4
                if q % 2 == 0:
                    pe.wait_ge(attr_in[h], g * 16 + 16 * (1 + q // 4))
                for n in range(2):
                    pair = attr[h][:, at + 2 * n:at + 2 * n + 2, :].rearrange("p t d -> p (t d)")
                    t = nc.tensor.transpose(psT[:, n * P:(n + 1) * P], pair, K["ident"][:, :])
                t.then_inc(attr_turned, 1)

            def project(g, j):
                if j % 4 == 0:
                    pe.wait_ge(attrT_ready, g * 4 + (j // 4 + 1))
                side = slice(j % 2 * ED, (j % 2 + 1) * ED)
                nc.tensor.matmul(pc(j), attrT[j // 4 % 2][side, j % 4 // 2 * P:(j % 4 // 2 + 1) * P], K["W1cT"][side, :],
                                 start=True, stop=False)
                if j % HALF == 0:
                    pe.wait_ge(onehot_ready, g * 2 + (j // HALF + 1))
                for w in range(WIN):
                    for n in range(NSPLIT):
                        t = nc.tensor.matmul(pc(j), onehot[j // HALF % 2][:, w, j % HALF, :],
                                             flat(table[:, bass.ds(blocks[j % 4] + w, 1), n * H:(n + 1) * H]),
                                             start=False, stop=(w == WIN - 1 and n == NSPLIT - 1))
                t.then_inc(c_done, 1)

            turn(0, 0)
            pe.wait_ge(attrT_ready, 1)
            turn(0, 1)
            pe.wait_ge(table_in, 16)
            blocks = window_blocks(nc, pe, K, 0)
            for j in range(4):
                project(0, j)
            with pe.Fori(0, NG) as g:
                for j in range(GROUP):
                    if j % 4 == 0:
                        blocks = window_blocks(nc, pe, K, g * (GROUP // PACK) + (j // 4 + 1))
                        pe.wait_ge(attrT_ready, g * 4 + (j // 4 + 2))
                        turn(g, j // 4 + 2)
                    pe.wait_ge(pre_ready, g * GROUP + (j + 1))
                    if j == GROUP - 4:
                        pe.wait_ge(table_in, 32)
                    project(g, j + 4)
                    if j % HALF == 0:
                        pe.wait_ge(same_ready, g * 2 + (j // HALF + 1))
                    pe.wait_ge(hid_ready, g * GROUP + (j + 1))
                    nc.tensor.matmul(psU[j % 2][:, 0:UW], same[j // HALF][:, j % HALF, :], hid[:, j % RING, :],
                                     start=True, stop=True).then_inc(agg_done, 1)
                    if j == 0:
                        pe.wait_ge(xg_in, g * 16 + 16)
                        for k in range(HC):
                            t = nc.tensor.transpose(psG[:, k * P:(k + 1) * P], xg[:, k * P:(k + 1) * P], K["ident"][:, :])
                        t.then_inc(xg_turned, 1)
                    if j in HIDDEN_AT:
                        n, k = HIDDEN_AT.index(j) // HC, HIDDEN_AT.index(j) % HC
                        if n == 0 and k == 0:
                            pe.wait_ge(xgT_ready, g + 1)
                        elif k == 0:
                            pe.wait_ge(hidden_kept, g * 3 + n)
                        t = nc.tensor.matmul(psG[:, 0:H], xgT[:, k * P:(k + 1) * P], K["WhhT"][:, k, n * H:(n + 1) * H],
                                             start=(k == 0), stop=(k == HC - 1))
                        if k == HC - 1:
                            t.then_inc(hidden_done, 1)

        @block.scalar
        def _(act):
            def keep_attr(g, q):
                act.wait_ge(attr_turned, g * 4 + (q + 1))
                nc.scalar.copy(attrT[q % 2][:, :], psT[:, 0:2 * P]).then_inc(attrT_ready, 1)

            act.wait_ge(ones, 1)
            keep_attr(0, 0)
            keep_attr(0, 1)
            with act.Fori(0, NG) as g:
                for j in range(GROUP):
                    if j % 4 == 0:
                        act.wait_ge(c_done, g * GROUP + (j + 4))
                        keep_attr(g, j // 4 + 2)
                    act.wait_ge(pre_ready, g * GROUP + (j + 1))
                    nc.scalar.activation(hid[:, j % RING, 0:H], ga[:, j % SLOTS, :], ACT.Relu).then_inc(hid_ready, 1)
                    act.wait_ge(agg_done, g * GROUP + (j + 1))
                    act.wait_ge(scatter_waited, g * GROUP + (j + 1 + NTAB))
                    nc.scalar.copy(msum[:, j % RING, :], psU[j % 2][:, 0:UW]).then_inc(msum_ready, 1)
                    if j == 1:
                        act.wait_ge(xg_turned, g + 1)
                        nc.scalar.copy(xgT[:, :], psG[:, 0:H]).then_inc(xgT_ready, 1)

        @block.vector
        def _(dve):
            def stage_index(g, h):
                at = bass.ds(g * GROUP + h * HALF, HALF)
                nc.vector.tensor_copy(gsrc[h % 2][:, :], K["srcT"][:, at]).then_inc(index_ready, 1)

            def compare(chain, g, h, part):
                ids = K["srcT"][:, bass.ds(g * GROUP + h * HALF, HALF)]
                if part == 0:
                    dve.wait_ge(src_in[h % 2], g * 32 + 32 * (1 + h // 2))
                    for w in range(WIN):
                        t = nc.vector.tensor_scalar(onehot[h % 2][:, w, :, :], locb[h % 2][:, :, :], K["winid"][:, w:w + 1], None, ALU.is_equal)
                    t.then_inc(onehot_ready, 1)
                if part == 1:
                    nc.vector.tensor_tensor(same[h % 2][:, :, :], srcb[h % 2][:, :, :],
                                            ids.unsqueeze(2).to_broadcast([P, HALF, P]), ALU.is_equal).then_inc(same_ready, 1)
                    dve.wait_ge(same_ready, g * 2 + (h + 1))
                if part == 2:
                    chain.link(nc.vector.tensor_tensor(earlier[:, :, :], same[h % 2][:, :, :],
                                                       K["before"][:, :].unsqueeze(1).to_broadcast([P, HALF, P]), ALU.mult))
                if part == 3:
                    chain.link(nc.vector.tensor_reduce(dup[:, :], earlier[:, :, :], AX.X, ALU.max))
                if part == 4:
                    chain.link(nc.vector.tensor_scalar(togo[:, :], ids, -1.0, K["spare"][:, 0:1], ALU.mult, ALU.add))
                    chain.link(nc.vector.tensor_tensor(togo[:, :], togo[:, :], dup[:, :], ALU.mult))
                    nc.vector.tensor_tensor(sink[h % 2][:, :], togo[:, :], ids, ALU.add).then_inc(sink_ready, 1)

            nc.vector.memset(hid[:, :, :], 1.0).then_inc(ones, 1)
            first = Chain(dve, dve_step)
            stage_index(0, 0)
            stage_index(0, 1)
            for part in range(4):
                compare(first, 0, 0, part)
            PER = 8
            with dve.Fori(0, NG) as g:
                chain = Chain(dve, dve_step, g * PER + first.n)
                for j in range(GROUP):
                    s = j % SLOTS
                    dve.wait_ge(gathered[s], g * (16 * GROUP // SLOTS) + 16 * (j // SLOTS + 1))
                    dve.wait_ge(c_done, g * GROUP + (j + 1))
                    nc.vector.tensor_tensor(ga[:, s, :], ga[:, s, :], pc(j), ALU.add).then_inc(pre_ready, 1)
                    h = j // HALF
                    if j % HALF == 0:
                        compare(chain, g, h + 1, 0)
                    if j % HALF == 3:
                        dve.wait_ge(agg_done, g * GROUP + (h * HALF + 1))
                        compare(chain, g, h + 1, 1)
                    if j % HALF in (4, 5):
                        compare(chain, g, h + 1, j % HALF - 2)
                    if j % HALF == 1:
                        dve.wait_ge(scatter_waited, g * GROUP + (h * HALF + NTAB))
                        compare(chain, g, h, 4)
                    if j % HALF == HALF - 1:
                        stage_index(g, 2 + j // HALF)
                    if j - 1 in HIDDEN_AT[HC - 1::HC]:
                        n = HIDDEN_AT.index(j - 1) // HC
                        dve.wait_ge(hidden_done, g * 3 + (n + 1))
                        if n == 0:
                            dve.wait_ge(hidden_out, g * 16 + 16)
                        at = n * H if n < 2 else 3 * H
                        nc.vector.tensor_tensor(hidden[:, n * H:(n + 1) * H], psG[:, 0:H], K["bgate"][:, at:at + H],
                                                ALU.add).then_inc(hidden_kept, 1)
                assert chain.n == PER


def nodes_phase(nc, K, D, A):
    with ExitStack() as st:
        m = Mem(nc, st, "nd_")
        sums = m.sb("sums", [P, NTAB, UNR, UW])
        count = m.sb("count", [P, UNR])
        xs = m.sb("xs", [P, UNR, H])
        hidden = m.sb("hidden", [P, UNR, 3 * H])
        sumsT = m.sb("sumsT", [P, UNR, H])
        addend = m.sb("addend", [P, UNR, 3 * H])
        rz = m.sb("rz", [P, UNR, 2 * H])
        cand = m.sb("cand", [P, UNR, H])
        tmp = m.sb("tmp", [P, UNR, H])
        y = m.sb("y", [P, UNR, H])
        stats = m.sb("stats", [P, UNR, 6])
        moments = m.sb("moments", [P, UNR, 2])
        rstd = m.sb("rstd", [P, UNR, 1])
        shift = m.sb("shift", [P, UNR, 1])
        x1 = m.sb("x1", [P, UNR, H + 2 * NH])
        x1T = m.sb("x1T", [P, UNR, H])
        rank = m.sb("rank", [P, UNR], I32)
        psT = m.ps("psT", [P, 512])
        psRZ = [m.ps(f"psRZ{q}", [P, 512]) for q in range(2)]
        psN = [m.ps(f"psN{q}", [P, 512]) for q in range(2)]
        psX = m.ps("psX", [P, 512])
        psS = m.ps("psS", [P, 512])
        loaded = [m.sem(f"loaded{j}") for j in range(UNR)]
        stored = [m.sem(f"stored{j}") for j in range(UNR)]
        scattered = [m.sem(f"scattered{j}") for j in range(UNR)]
        pair_added = [m.sem(f"pair_added{n}") for n in range(NTAB // 2)]
        counted, sums_turned, sumsT_ready = m.sem("counted"), m.sem("sums_turned"), m.sem("sumsT_ready")
        gates_done, gates_kept, gates_open = m.sem("gates_done"), m.sem("gates_kept"), m.sem("gates_open")
        cand_ready, cand_done, mixed = m.sem("cand_ready"), m.sem("cand_done"), m.sem("mixed")
        x1_ready, x1_turned, x1T_ready = m.sem("x1_ready"), m.sem("x1_turned"), m.sem("x1T_ready")
        scores_done, rows_ready = m.sem("scores_done"), m.sem("rows_ready")
        moments_ready, var_ready, rstd_ready = m.sem("moments_ready"), m.sem("var_ready"), m.sem("rstd_ready")
        addend_ready, reset_done, held = m.sem("addend_ready"), m.sem("reset_done"), m.sem("held")
        y_ready, stats_ready = m.sem("y_ready"), m.sem("stats_ready")
        dve_waited, pool_waited = m.sem("dve_waited"), m.sem("pool_waited")
        block = st.enter_context(nc.Block())

        @block.sync
        def _(sp):
            def load(row, j, count=P):
                for t in range(NTAB):
                    sp.dma_start(sums[:, t, j, :], D[f"S{t}"][bass.ds(row, P), :]).then_inc(loaded[j], 16)
                sp.dma_start(hidden[:, j, :], D["GH"][bass.ds(row, P), :]).then_inc(loaded[j], 16)
                sp.dma_start(xs[0:count, j, :], A["x"][bass.ds(row, count), :]).then_inc(loaded[j], 16)

            def store(i, j):
                sp.wait_ge(rows_ready, nth(i, j))
                sp.dma_start(D["X1"][bass.ds(i * (UNR * P) + j * P, P), :], x1[:, j, 0:XW]).then_inc(stored[j], 16)

            for j in range(UNR):
                load(j * P, j)
            with sp.Fori(0, NI - 2) as i:
                for j in range(UNR):
                    sp.wait_ge(mixed, i * (2 * UNR) + 2 * (j + 1))
                    load(i * (UNR * P) + (UNR + j) * P, j)
                    store(i, j)
            for j in range(UNR):
                sp.wait_ge(mixed, (NI - 2) * 2 * UNR + 2 * (j + 1))
                row = (NI - 1) * UNR * P + j * P
                load(row, j, min(P, N - row))
                store(NI - 2, j)
            for j in range(UNR):
                store(NI - 1, j)
            for j in range(UNR):
                sp.wait_ge(stored[j], 16 * NI)

        @block.gpsimd
        def _(pool):
            def add_pair(i, j):
                pool.wait_ge(loaded[j], i * (16 * (NTAB + 2)) + 16 * (NTAB + 2))
                nc.gpsimd.tensor_tensor(sums[:, 2, j, 0:H], sums[:, 2, j, 0:H], sums[:, 3, j, 0:H], ALU.add).then_inc(pair_added[1], 1)

            def mix(i, j):
                pool.wait_ge(cand_done, nth(i, j))
                nc.gpsimd.tensor_tensor(tmp[:, j, :], xs[:, j, :], cand[:, j, :], ALU.subtract).then_inc(mixed, 1)
                nc.gpsimd.tensor_tensor(y[:, j, :], xs[:, j, :], cand[:, j, :], ALU.add).then_inc(mixed, 1)

            def deviation(i, j):
                pool.wait_ge(moments_ready, nth(i, j))
                nc.gpsimd.tensor_tensor(rstd[:, j, :], moments[:, j, 1:2], K["eps"][:, :], ALU.add).then_inc(var_ready, 1)
                pool.wait_ge(var_ready, i * (3 * UNR) + (3 * j + 1))
                nc.gpsimd.tensor_tensor(rstd[:, j, :], rstd[:, j, :], K["neghalf"][:, :], ALU.pow).then_inc(var_ready, 1)
                nc.gpsimd.tensor_scalar(shift[:, j, :], moments[:, j, 0:1], -1.0, None, ALU.mult).then_inc(var_ready, 1)
                pool.wait_ge(var_ready, i * (3 * UNR) + (3 * j + 3))
                nc.gpsimd.tensor_tensor(shift[:, j, :], shift[:, j, :], rstd[:, j, :], ALU.mult).then_inc(rstd_ready, 1)

            def scatter(i, j):
                pool.wait_ge(rows_ready, nth(i, j))
                pool.sem_inc(pool_waited, 1)
                pool.indirect_dma_start(D["sv"], bass.IndirectOffsetOnAxis(ap=rank[:, j:j + 1], axis=0),
                                        x1[:, j, XW:XW + NH], None).then_inc(scattered[j], 16)

            pipeline(pool, [(0, add_pair), (3, deviation), (2, mix), (6, scatter)])
            for j in range(UNR):
                pool.wait_ge(scattered[j], 16 * NI)

        @block.tensor
        def _(pe):
            def turn_sums(i, j):
                pe.wait_ge(sumsT_ready, i * UNR + j)
                pe.wait_ge(pair_added[0], nth(i, j))
                pe.wait_ge(pair_added[1], nth(i, j))
                for k in range(HC):
                    for t in range(0, NTAB, 2):
                        last = nc.tensor.matmul(psT[:, k * P:(k + 1) * P], sums[:, t, j, k * P:(k + 1) * P], K["ident"][:, :],
                                                start=(t == 0), stop=(t == NTAB - 2))
                last.then_inc(sums_turned, 1)

            def gates(i, j):
                pe.wait_ge(gates_kept, i * UNR + max(j - 1, 0))
                pe.wait_ge(sumsT_ready, nth(i, j))
                for target, cols in ((psRZ[j % 2][:, :], slice(0, 2 * H)), (psN[j % 2][:, 0:H], slice(2 * H, 3 * H))):
                    for k in range(HC):
                        t = nc.tensor.matmul(target, sumsT[:, j, k * P:(k + 1) * P], K["WcT"][:, k, cols],
                                             start=(k == 0), stop=(k == HC - 1))
                t.then_inc(gates_done, 1)

            def turn_x1(i, j):
                pe.wait_ge(x1T_ready, i * UNR + j)
                pe.wait_ge(x1_ready, nth(i, j))
                for k in range(HC):
                    t = nc.tensor.transpose(psX[:, k * P:(k + 1) * P], x1[:, j, k * P:(k + 1) * P], K["ident"][:, :])
                t.then_inc(x1_turned, 1)

            def scores(i, j):
                pe.wait_ge(rows_ready, i * UNR + j)
                pe.wait_ge(x1T_ready, nth(i, j))
                for k in range(HC):
                    t = nc.tensor.matmul(psS[:, 0:2 * NH], x1T[:, j, k * P:(k + 1) * P], K["WuvT"][:, k, :],
                                         start=(k == 0), stop=(k == HC - 1))
                t.then_inc(scores_done, 1)

            pipeline(pe, [(1, gates), (0, turn_sums), (4, turn_x1), (5, scores)])

        @block.scalar
        def _(act):
            def keep_sums(i, j):
                act.wait_ge(sums_turned, nth(i, j))
                nc.scalar.copy(sumsT[:, j, :], psT[:, 0:H]).then_inc(sumsT_ready, 1)

            def open_gates(i, j):
                act.wait_ge(gates_kept, nth(i, j))
                nc.scalar.activation(rz[:, j, :], rz[:, j, :], ACT.Sigmoid).then_inc(gates_open, 1)

            def bound(i, j):
                act.wait_ge(cand_ready, nth(i, j))
                nc.scalar.activation(cand[:, j, :], cand[:, j, :], ACT.Tanh).then_inc(cand_done, 1)

            def normalise(i, j):
                act.wait_ge(rstd_ready, nth(i, j))
                act.wait_ge(stored[j], i * 16)
                act.wait_ge(scattered[j], i * 16)
                nc.scalar.activation(x1[:, j, 0:H], y[:, j, :], ACT.Identity, bias=shift[:, j, :],
                                     scale=rstd[:, j, :]).then_inc(x1_ready, 1)

            def keep_x1(i, j):
                act.wait_ge(x1_turned, nth(i, j))
                nc.scalar.copy(x1T[:, j, :], psX[:, 0:H]).then_inc(x1T_ready, 1)

            pipeline(act, [(2, bound), (0, keep_sums), (3, normalise), (1, open_gates), (4, keep_x1)])

        @block.vector
        def _(dve):
            def start(i, j):
                dve.wait_ge(loaded[j], i * (16 * (NTAB + 2)) + 16 * (NTAB + 2))
                nc.vector.tensor_tensor(sums[:, 0, j, 0:H], sums[:, 0, j, 0:H], sums[:, 1, j, 0:H], ALU.add).then_inc(pair_added[0], 1)
                nc.vector.tensor_reduce(count[:, j:j + 1], sums[:, :, j, H], AX.X, ALU.add).then_inc(counted, 1)
                dve.wait_ge(counted, nth(i, j))
                nc.vector.scalar_tensor_tensor(addend[:, j, 0:2 * H], K["b2ih"][:, 0:2 * H], count[:, j:j + 1], hidden[:, j, 0:2 * H],
                                               ALU.mult, ALU.add)
                nc.vector.scalar_tensor_tensor(addend[:, j, 2 * H:3 * H], K["b2ih"][:, 2 * H:3 * H], count[:, j:j + 1],
                                               K["bgate"][:, 2 * H:3 * H], ALU.mult, ALU.add).then_inc(addend_ready, 1)

            def keep_gates(i, j):
                dve.wait_ge(addend_ready, nth(i, j))
                dve.wait_ge(gates_done, nth(i, j))
                nc.vector.tensor_tensor(rz[:, j, :], psRZ[j % 2][:, :], addend[:, j, 0:2 * H], ALU.add)
                nc.vector.tensor_tensor(cand[:, j, :], psN[j % 2][:, 0:H], addend[:, j, 2 * H:3 * H], ALU.add).then_inc(gates_kept, 1)

            def candidate(i, j):
                dve.wait_ge(gates_open, nth(i, j))
                nc.vector.tensor_tensor(rz[:, j, 0:H], rz[:, j, 0:H], hidden[:, j, 2 * H:3 * H], ALU.mult).then_inc(reset_done, 1)
                dve.wait_ge(reset_done, nth(i, j))
                nc.vector.tensor_tensor(cand[:, j, :], cand[:, j, :], rz[:, j, 0:H], ALU.add).then_inc(cand_ready, 1)

            def update(i, j):
                dve.wait_ge(mixed, i * (2 * UNR) + 2 * (j + 1))
                nc.vector.tensor_tensor(tmp[:, j, :], tmp[:, j, :], rz[:, j, H:2 * H], ALU.mult).then_inc(held, 1)
                dve.wait_ge(held, nth(i, j))
                nc.vector.tensor_tensor(y[:, j, :], y[:, j, :], tmp[:, j, :], ALU.add).then_inc(y_ready, 1)
                dve.wait_ge(y_ready, nth(i, j))
                nc.vector.bn_stats(stats[:, j, :], y[:, j, :]).then_inc(stats_ready, 1)
                dve.wait_ge(stats_ready, nth(i, j))
                dve.wait_ge(scattered[j], i * 16)
                dve.sem_inc(dve_waited, 1)
                nc.vector.tensor_copy(rank[:, j:j + 1], K["rank"][:, bass.ds(i * UNR + j, 1)])
                nc.vector.bn_aggr(moments[:, j, :], stats[:, j, :]).then_inc(moments_ready, 1)

            def finish(i, j):
                dve.wait_ge(scores_done, nth(i, j))
                nc.vector.tensor_tensor(x1[:, j, H:H + 2 * NH], psS[:, 0:2 * NH], K["bu"][:, :], ALU.add).then_inc(rows_ready, 1)

            pipeline(dve, [(2, candidate), (0, start), (6, finish), (1, keep_gates), (2, update)])


def layer1_phase(nc, K, D, A):
    with ExitStack() as st:
        m = Mem(nc, st, "l1_")
        feats = [m.sb(f"feats{r}", [P, GROUP, XW]) for r in range(2)]
        gsrc = [m.sb(f"gsrc{r}", [P, GROUP], I32) for r in range(2)]
        locb = [m.sb(f"locb{r}", [P, GROUP, P], BF16) for r in range(2)]
        onehot = [m.sb(f"onehot{r}", [P, WIN, GROUP, P], BF16) for r in range(2)]
        svf = m.sb("svf", [P, NB + 1, NH])
        svrest = m.sb("svrest", [P, NB + 1, NH])
        table = m.sb("table", [P, NB + 1, NSPLIT * NH], BF16)
        same = [m.sb(f"same{r}", [P, GROUP, P]) for r in range(2)]
        part = [m.sb(f"part{r}", [P, GROUP, PW]) for r in range(2)]
        score = m.sb("score", [P, GROUP, NH])
        below = m.sb("below", [P, GROUP, NH])
        start8 = m.sb("start8", [P, GROUP, NH])
        turned = m.sb("turned", [P, 2 * P + 1])
        run = m.sb("run", [P, P])
        psE = m.ps("psE", [P, 512])
        psM = m.ps("psM", [P, 512])
        psU = [m.ps(f"psU{q}", [P, 512]) for q in range(4)]
        psV = m.ps("psV", [P, 512])
        table_in, table_ready = m.sem("table_in"), m.sem("table_ready")
        onehot_ready, sv_done, sv_taken = m.sem("onehot_ready"), m.sem("sv_done"), m.sem("sv_taken")
        gathered = [m.sem(f"gathered{r}") for r in range(2)]
        dst_in = [m.sem(f"dst_in{r}") for r in range(2)]
        stored = [m.sem(f"stored{r}") for r in range(2)]
        index_ready, same_ready = m.sem("index_ready"), m.sem("same_ready")
        scores_ready, scores_turned = m.sem("scores_ready"), m.sem("scores_turned")
        max_ready, max_turned = m.sem("max_ready"), m.sem("max_turned")
        below_ready, weights_ready = m.sem("below_ready"), m.sem("weights_ready")
        weighted, agg_done, part_ready = m.sem("weighted"), m.sem("agg_done"), m.sem("part_ready")
        max_kept, scores_kept = m.sem("max_kept"), m.sem("scores_kept")
        dve_step = m.sem("dve_step")
        pool_waited = m.sem("pool_waited")
        block = st.enter_context(nc.Block())

        def groups(engine, body, count=NG):
            with engine.Fori(0, count // 2) as u:
                for r in range(2):
                    body(u * 2 + r, r, u, False)
            if count % 2:
                body(count - 1, 0, count // 2, True)

        @block.sync
        def _(sp):
            def dst_rows(r, row):
                sp.dma_start(locb[r][:, :, :].rearrange("p t e -> p (t e)"),
                             D["loc_rows"][row, :].rearrange("t e -> (t e)").partition_broadcast(P)).then_inc(dst_in[r], 16)

            sp.dma_start(svf[:, :, :], D["sv"].rearrange("(b p) h -> p b h", p=P)).then_inc(table_in, 16)
            for r in range(2):
                sp.sem_inc(stored[r], 16)
                dst_rows(r, slice(r * GROUP, (r + 1) * GROUP))

            def body(g, r, u, last):
                sp.wait_ge(same_ready, g + 1)
                dst_rows(r, bass.ds(g * GROUP + 2 * GROUP, GROUP))
                sp.wait_ge(part_ready, g * GROUP + GROUP)
                sp.wait_ge(max_kept, g + 1)
                sp.dma_start(D["PT"][bass.ds(g * (GROUP * P), GROUP * P), :].rearrange("(t p) w -> p t w", p=P),
                             part[r][:, :, :]).then_inc(stored[r], 16)

            groups(sp, body)
            for r in range(2):
                sp.wait_ge(stored[r], 16 * ((NG + 1 - r) // 2) + 16)
                sp.wait_ge(dst_in[r], 16 * ((NG + 1 - r) // 2 + 1))

        @block.gpsimd
        def _(pool):
            def gather(r, t):
                pool.indirect_dma_start(feats[r][:, t, :], None, D["X1"],
                                        bass.IndirectOffsetOnAxis(ap=gsrc[r][:, t:t + 1], axis=0)).then_inc(gathered[r], 16)

            pool.wait_ge(index_ready, 2)
            for r in range(2):
                for t in range(GROUP):
                    gather(r, t)

            def body(g, r, u, last):
                pool.wait_ge(index_ready, g + 3)
                for t in range(GROUP):
                    pool.wait_ge(agg_done, g * GROUP + (t + 1))
                    pool.sem_inc(pool_waited, 1)
                    gather(r, t)

            groups(pool, body, NG - 2)
            for r in range(2):
                pool.wait_ge(gathered[r], 16 * GROUP * ((NG + 1 - r) // 2))

        @block.tensor
        def _(pe):
            def load_blocks(g):
                _, words = nc.values_load_multi_w_load_instructions(
                    K["blocks"][0:1, bass.ds(g * (GROUP // PACK), GROUP // PACK)], [mybir.EngineType.PE], min_val=0,
                    max_val=64 ** PACK - 1, skip_runtime_bounds_check_because="a word packs four numbers below 64")
                return words

            def dst_scores(g, r, words, half):
                if half == 0:
                    pe.wait_ge(onehot_ready, g + 1)
                for t in range(half * HALF, (half + 1) * HALF):
                    if t % PACK == 0:
                        blocks = unpack(nc, words[t // PACK])
                    for w in range(WIN):
                        i = nc.tensor.matmul(psV[:, t * NSPLIT * NH:(t + 1) * NSPLIT * NH], onehot[r][:, w, t, :],
                                             flat(table[:, bass.ds(blocks[t % PACK] + w, 1), :]),
                                             start=(w == 0), stop=(w == WIN - 1))
                if half == 1:
                    i.then_inc(sv_done, 1)

            pe.wait_ge(table_ready, 1)
            words = load_blocks(0)
            dst_scores(0, 0, words, 0)
            dst_scores(0, 0, words, 1)

            def body(g, r, u, last):
                pe.wait_ge(scores_ready, g + 1)
                nc.tensor.transpose(psE[:, 0:P], score[:, :, :].rearrange("p t h -> p (t h)"), K["ident"][:, :])
                nc.tensor.transpose(psE[:, P:2 * P], start8[:, :, :].rearrange("p t h -> p (t h)"),
                                    K["ident"][:, :]).then_inc(scores_turned, 1)
                if not last:
                    words = load_blocks(g + 1)
                    dst_scores(g + 1, 1 - r, words, 0)
                pe.wait_ge(max_ready, g + 1)
                nc.tensor.transpose(psM[:, 0:P], turned[:, 0:P], K["ident"][:, :]).then_inc(max_turned, 1)
                if not last:
                    dst_scores(g + 1, 1 - r, words, 1)
                pe.wait_ge(same_ready, g + 1)
                for t in range(GROUP):
                    if t % 4 == 0:
                        pe.wait_ge(weighted, g * (GROUP // 4) + (t // 4 + 1))
                    if t >= 4:
                        pe.wait_ge(part_ready, g * GROUP + (t - 3))
                    nc.tensor.matmul(psU[t % 4][:, 0:XW], same[r][:, t, :], feats[r][:, t, :],
                                     start=True, stop=True).then_inc(agg_done, 1)

            groups(pe, body)

        @block.scalar
        def _(act):
            def body(g, r, u, last):
                act.wait_ge(scores_turned, g + 1)
                nc.scalar.copy(turned[:, 0:2 * P], psE[:, 0:2 * P]).then_inc(scores_kept, 1)
                act.wait_ge(below_ready, g + 1)
                nc.scalar.activation(feats[r][:, :, H:XW], below[:, :, :], ACT.Exp).then_inc(weights_ready, 1)
                act.wait_ge(stored[r], u * 16 + 16)
                nc.scalar.copy(part[r][:, :, XW:PW], psM[:, 0:P].rearrange("p (t h) -> p t h", h=NH)).then_inc(max_kept, 1)
                for t in range(GROUP):
                    act.wait_ge(agg_done, g * GROUP + (t + 1))
                    nc.scalar.copy(part[r][:, t, 0:XW], psU[t % 4][:, 0:XW]).then_inc(part_ready, 1)

            groups(act, body)

        @block.vector
        def _(dve):
            def stage_index(g, r):
                at = bass.ds(g * GROUP, GROUP)
                nc.vector.tensor_copy(gsrc[r][:, :], K["srcT"][:, at]).then_inc(index_ready, 1)

            def find_node(g, r, u):
                dve.wait_ge(dst_in[r], u * 16 + 16)
                for w in range(WIN):
                    t = nc.vector.tensor_scalar(onehot[r][:, w, :, :], locb[r][:, :, :], K["winid"][:, w:w + 1], None, ALU.is_equal)
                t.then_inc(onehot_ready, 1)

            def compare(g, r):
                nc.vector.tensor_tensor(same[r][:, :, :], locb[r][:, :, :],
                                        K["locT"][:, bass.ds(g * GROUP, GROUP)].unsqueeze(2).to_broadcast([P, GROUP, P]),
                                        ALU.is_equal).then_inc(same_ready, 1)

            stage_index(0, 0)
            stage_index(1, 1)
            find_node(0, 0, 0)
            compare(0, 0)
            first = Chain(dve, dve_step)
            first.link(nc.vector.memset(turned[:, 2 * P:2 * P + 1], 0.0))
            dve.wait_ge(table_in, 16)
            split_float(nc, first, svf[:, :, :], svrest[:, :, :],
                        [table[:, :, n * NH:(n + 1) * NH] for n in range(NSPLIT)])
            dve.sem_inc(table_ready, 1)
            PER = 2

            def body(g, r, u, last):
                c = Chain(dve, dve_step, g * PER + first.n)
                dve.wait_ge(gathered[r], u * (16 * GROUP) + 16 * GROUP)
                stage_index(g + 2, r)
                nc.vector.tensor_copy(start8[:, :, :],
                                      K["startT"][:, bass.ds(g * GROUP, GROUP)].unsqueeze(2).to_broadcast([P, GROUP, NH]))
                dve.wait_ge(sv_done, g + 1)
                nc.vector.tensor_reduce(score[:, :, :], psV[:, 0:GROUP * NSPLIT * NH].rearrange("p (t n h) -> p t h n", n=NSPLIT, h=NH),
                                        AX.X, ALU.add).then_inc(sv_taken, 1)
                dve.wait_ge(sv_taken, g + 1)
                c.link(nc.vector.tensor_tensor(score[:, :, :], feats[r][:, :, H:XW], score[:, :, :], ALU.add))
                nc.vector.scalar_tensor_tensor(score[:, :, :], score[:, :, :], SLOPE, score[:, :, :],
                                               ALU.mult, ALU.max).then_inc(scores_ready, 1)
                if not last:
                    find_node(g + 1, 1 - r, u + r)
                dve.wait_ge(scores_kept, g + 1)
                segment_max(nc, c, turned[:, 0:P], turned[:, P:2 * P + 1], P, run).then_inc(max_ready, 1)
                if not last:
                    compare(g + 1, 1 - r)
                dve.wait_ge(max_turned, g + 1)
                nc.vector.tensor_tensor(below[:, :, :], score[:, :, :], psM[:, 0:P].rearrange("p (t h) -> p t h", h=NH),
                                        ALU.subtract).then_inc(below_ready, 1)
                dve.wait_ge(weights_ready, g + 1)
                for q in range(GROUP // 4):
                    f = feats[r][:, q * 4:(q + 1) * 4, :]
                    f3 = f[:, :, 0:H].rearrange("p t (c h) -> p t c h", h=NH)
                    w3 = f[:, :, H:XW].unsqueeze(2).to_broadcast([P, 4, H // NH, NH])
                    nc.vector.tensor_tensor(f3, f3, w3, ALU.mult).then_inc(weighted, 1)
                assert c.n == PER

            groups(dve, body)


def merge_phase(nc, K, D, A, O):
    with ExitStack() as st:
        m = Mem(nc, st, "mg_")
        rows = m.sb("rows", [CQ, CH, PW])
        t2 = m.sb("t2", [CQ, CH, PW])
        last = m.sb("last", [CQ, CH])
        lastb = m.sb("lastb", [CQ, NT])
        same = m.sb("same", [CQ, CH, NT])
        maxT = m.sb("maxT", [NH, NT])
        start = m.sb("start", [NH, NT + 1])
        run = m.sb("run", [NH, NT])
        scale = m.sb("scale", [CQ, CH, NH])
        psA = [m.ps(f"psA{i}", [P, 512]) for i in range(2)]
        psM = m.ps("psM", [P, 512])
        psS = [m.ps(f"psS{i}", [P, 512]) for i in range(2)]
        rows_in, last_in = m.sem("rows_in"), m.sem("last_in")
        turned, max_ready, max_turned = m.sem("turned"), m.sem("max_ready"), m.sem("max_turned")
        below_ready, scale_ready, scaled = m.sem("below_ready"), m.sem("scale_ready"), m.sem("scaled")
        summed, t2_ready, t2_out = m.sem("summed"), m.sem("t2_ready"), m.sem("t2_out")
        dve_step = m.sem("dve_step")
        block = st.enter_context(nc.Block())
        split = 4

        index_ready, x1_in = m.sem("index_ready"), m.sem("x1_in")

        @block.gpsimd
        def _(pool):
            pool.wait_ge(index_ready, 1)
            for b in range(NB):
                pool.indirect_dma_start(O["own"][:, b, :], None, D["PT"],
                                        bass.IndirectOffsetOnAxis(ap=O["own_i"][:, b:b + 1], axis=0)).then_inc(O["own_in"], 16)
            pool.wait_ge(O["own_in"], 16 * NB)

        @block.sync
        def _(sp):
            sp.dma_start(rows[:, :, :], D["PT"].rearrange("(c q p) w -> q c p w", q=CQ, p=P)[:, :, P - 1, :]).then_inc(rows_in, 16)
            sp.dma_start(lastb[:, :], D["last"].rearrange("t o -> (t o)").partition_broadcast(CQ)).then_inc(last_in, 16)
            with nc.allow_non_contiguous_dma(reason="one word of each tile"):
                sp.dma_start(last[:, :], D["last"].rearrange("(c q) o -> q (c o)", q=CQ)).then_inc(last_in, 16)
            sp.dma_start(O["x1"][:, :, :], D["X1"][:, 0:H].rearrange("(b p) h -> p b h", p=P)).then_inc(x1_in, 16)
            sp.wait_ge(x1_in, 16)
            sp.wait_ge(t2_ready, CH + 1)
            sp.dma_start(D["T2"].rearrange("(c q) w -> q c w", q=CQ), t2[:, :, :]).then_inc(t2_out, 16)
            sp.wait_ge(t2_out, 16)

        @block.tensor
        def _(pe):
            pe.wait_ge(rows_in, 16)
            for c in range(CH):
                at = c % split * CQ
                i = nc.tensor.transpose(psA[c // split][0:NH, at:at + CQ], rows[:, c, XW:PW], K["ident"][0:CQ, 0:CQ])
            i.then_inc(turned, 1)
            pe.wait_ge(max_ready, 1)
            for c in range(CH):
                i = nc.tensor.transpose(psM[0:CQ, c * NH:(c + 1) * NH], maxT[:, c * CQ:(c + 1) * CQ], K["ident"][0:NH, 0:NH])
            i.then_inc(max_turned, 1)
            pe.wait_ge(scaled, 2)
            for a in range(CH):
                if a >= 2:
                    pe.wait_ge(t2_ready, a)
                for c in range(CH):
                    i = nc.tensor.matmul(psS[a % 2][0:CQ, 0:XW], same[:, c, a * CQ:(a + 1) * CQ], rows[:, c, 0:XW],
                                         start=(c == 0), stop=(c == CH - 1))
                i.then_inc(summed, 1)

        @block.scalar
        def _(act):
            act.wait_ge(below_ready, 1)
            nc.scalar.activation(scale[:, :, :], scale[:, :, :], ACT.Exp).then_inc(scale_ready, 1)
            nc.scalar.copy(t2[:, :, XW:PW], psM[0:CQ, 0:CH * NH].rearrange("p (c h) -> p c h", h=NH)).then_inc(t2_ready, 1)
            for a in range(CH):
                act.wait_ge(summed, a + 1)
                nc.scalar.copy(t2[:, a, 0:XW], psS[a % 2][0:CQ, 0:XW]).then_inc(t2_ready, 1)

        @block.vector
        def _(dve):
            c = Chain(dve, dve_step)
            nc.vector.tensor_copy(O["ends_i"][:, :], K["ends_row"][:, 0:NB])
            nc.vector.tensor_copy(O["own_i"][:, :], K["own_row"][:, 0:NB]).then_inc(index_ready, 1)
            dve.wait_ge(turned, 1)
            dve.wait_ge(last_in, 32)
            c.link(nc.vector.tensor_copy(maxT[:, 0:split * CQ], psA[0][0:NH, 0:split * CQ]))
            c.link(nc.vector.tensor_copy(maxT[:, split * CQ:NT], psA[1][0:NH, 0:NT - split * CQ]))
            c.link(nc.vector.memset(start[:, :], LOW))
            c.link(nc.vector.tensor_tensor(start[:, 1:NT], lastb[0:NH, 1:NT], lastb[0:NH, 0:NT - 1], ALU.not_equal))
            c.link(nc.vector.tensor_scalar(start[:, 1:NT], start[:, 1:NT], LOW, None, ALU.mult))
            segment_max(nc, c, maxT, start, NT, run).then_inc(max_ready, 1)
            nc.vector.tensor_tensor(same[:, :, :], lastb[:, :].unsqueeze(1).to_broadcast([CQ, CH, NT]),
                                    last[:, :].unsqueeze(2).to_broadcast([CQ, CH, NT]), ALU.is_equal).then_inc(scaled, 1)
            dve.wait_ge(max_turned, 1)
            nc.vector.tensor_tensor(scale[:, :, :], rows[:, :, XW:PW],
                                    psM[0:CQ, 0:CH * NH].rearrange("p (c h) -> p c h", h=NH), ALU.subtract).then_inc(below_ready, 1)
            dve.wait_ge(scale_ready, 1)
            u = rows[:, :, 0:XW].rearrange("p c (n h) -> p c n h", h=NH)
            nc.vector.tensor_tensor(u, u, scale[:, :, :].unsqueeze(2).to_broadcast([CQ, CH, XW // NH, NH]),
                                    ALU.mult).then_inc(scaled, 1)


def output_phase(nc, K, D, A, O):
    with ExitStack() as st:
        m = Mem(nc, st, "ot_")
        ends = [m.sb(f"ends{r}", [P, UNR, PW]) for r in range(2)]
        own, x1 = O["own"], O["x1"]
        y = [m.sb(f"y{r}", [P, UNR, H]) for r in range(2)]
        w = m.sb("w", [P, 2, UNR, NH])
        den = m.sb("den", [P, 2, UNR, NH])
        top = m.sb("top", [P, UNR, NH])
        valid = m.sb("valid", [P, 2, UNR])
        mask = m.sb("mask", [P, 2, UNR])
        none = m.sb("none", [P, UNR])
        stats = m.sb("stats", [P, UNR, 6])
        moments = m.sb("moments", [P, UNR, 2])
        rstd = m.sb("rstd", [P, UNR])
        shift = m.sb("shift", [P, UNR])
        psY = [m.ps(f"psY{q}", [P, 2, H]) for q in range(8)]
        scaled, summed = m.sem("scaled"), m.sem("summed")
        gathered = [m.sem(f"gathered{r}") for r in range(2)]
        out_sent = [m.sem(f"out_sent{r}") for r in range(2)]
        below_ready, weights_ready = m.sem("below_ready"), m.sem("weights_ready")
        moments_ready, norm_step, rstd_ready, y_ready = m.sem("moments_ready"), m.sem("norm_step"), m.sem("rstd_ready"), m.sem("y_ready")
        dve_step = m.sem("dve_step")
        dve_waited = m.sem("dve_waited")
        block = st.enter_context(nc.Block())

        def units(engine, body):
            with engine.Fori(0, NI // 2) as u:
                for r in range(2):
                    body(u * 2 + r, r, u, False)
            body(NI - 1, 0, NI // 2, True)

        span = UNR * P

        @block.sync
        def _(sp):
            def step(u):
                for r in range(2):
                    sp.wait_ge(y_ready, u * (2 * UNR) + UNR * (r + 3))
                    sp.dma_start(A["out"][bass.ds(u * (2 * span) + r * span, span), :].rearrange("(b p) h -> p b h", p=P),
                                 y[r][:, :, :]).then_inc(out_sent[r], 16)

            with sp.Fori(0, NI // 2) as u:
                step(u)
            first = (NI - 1) * span
            whole = (N - first) // P
            sp.wait_ge(y_ready, NI * UNR + 2 * UNR)
            sp.dma_start(A["out"][first:first + whole * P, :].rearrange("(b p) h -> p b h", p=P),
                         y[0][:, 0:whole, :]).then_inc(out_sent[0], 16)
            sp.dma_start(A["out"][first + whole * P:N, :], y[0][0:N - first - whole * P, whole, :]).then_inc(out_sent[0], 16)
            sp.wait_ge(out_sent[0], 16 * (NI // 2 + 2))
            sp.wait_ge(out_sent[1], 16 * (NI // 2))

        @block.gpsimd
        def _(pool):
            def gather(u):
                for j in range(UNR):
                    if u >= 2:
                        pool.wait_ge(summed, (u - 2) * UNR + (j + 1))
                    pool.indirect_dma_start(ends[u % 2][:, j, :], None, D["T2"],
                                            bass.IndirectOffsetOnAxis(ap=O["ends_i"][:, u * UNR + j:u * UNR + j + 1], axis=0)).then_inc(gathered[u % 2], 16)

            pool.sem_inc(rstd_ready, 1)
            gather(0)
            gather(1)
            for u in range(NI):
                if u + 2 < NI:
                    gather(u + 2)
                pool.wait_ge(moments_ready, u * UNR + 2 * UNR)
                if u >= 1:
                    pool.wait_ge(y_ready, u * UNR + 2 * UNR)
                nc.gpsimd.tensor_tensor(rstd[:, :], moments[:, :, 1], K["eps"][:, 0:1].to_broadcast([P, UNR]), ALU.add).then_inc(norm_step, 1)
                pool.wait_ge(norm_step, 3 * u + 1)
                nc.gpsimd.tensor_tensor(rstd[:, :], rstd[:, :], K["neghalf"][:, 0:1].to_broadcast([P, UNR]), ALU.pow).then_inc(norm_step, 1)
                nc.gpsimd.tensor_scalar(shift[:, :], moments[:, :, 0], -1.0, None, ALU.mult).then_inc(norm_step, 1)
                pool.wait_ge(norm_step, 3 * u + 3)
                nc.gpsimd.tensor_tensor(shift[:, :], shift[:, :], rstd[:, :], ALU.mult).then_inc(rstd_ready, 1)
            for r in range(2):
                pool.wait_ge(gathered[r], 16 * UNR * ((NI + 1 - r) // 2))

        def bank(r, j):
            return psY[r * 4 + j // 2][:, j % 2, :]

        @block.tensor
        def _(pe):
            def body(u, r, v, last):
                pe.wait_ge(scaled, u + 1)
                pe.wait_ge(y_ready, u * UNR + UNR)
                for j in range(UNR):
                    for n, part in enumerate((flat(ends[r][:, j:j + 1, 0:H]), flat(own[:, bass.ds(u * UNR + j, 1), 0:H]),
                                              flat(x1[:, bass.ds(u * UNR + j, 1), :]))):
                        t = nc.tensor.matmul(bank(r, j), K["ident"][:, :], part, start=(n == 0), stop=(n == 2))
                    t.then_inc(summed, 1)

            units(pe, body)

        @block.scalar
        def _(act):
            def weights(u):
                act.wait_ge(below_ready, u + 1)
                nc.scalar.activation(w[:, :, :, :], w[:, :, :, :], ACT.Exp).then_inc(weights_ready, 1)

            act.sem_inc(y_ready, 2 * UNR)
            weights(0)
            weights(1)
            for u in range(NI):
                if u + 2 < NI:
                    weights(u + 2)
                act.wait_ge(rstd_ready, u + 2)
                if u >= 2:
                    act.wait_ge(out_sent[u % 2], u // 2 * 16)
                for j in range(UNR):
                    nc.scalar.activation(y[u % 2][:, j, :], bank(u % 2, j), ACT.Identity, bias=shift[:, j:j + 1],
                                         scale=rstd[:, j:j + 1]).then_inc(y_ready, 1)

        @block.vector
        def _(dve):
            def scale(u, r, v, c):
                at = bass.ds(u * UNR, UNR)
                pair = (ends[r], own[:, at, :])
                dve.wait_ge(gathered[r], v * (16 * UNR) + 16 * UNR)
                nc.vector.tensor_scalar(none[:, :], K["any"][:, at], -1.0, 1.0, ALU.mult, ALU.add)
                nc.vector.tensor_copy(valid[:, 0, :], K["ends"][:, at])
                c.link(nc.vector.tensor_copy(valid[:, 1, :], K["own"][:, at]))
                c.link(nc.vector.tensor_scalar(mask[:, :, :], valid[:, :, :], -1.0, -LOW, ALU.add, ALU.mult))
                for n in range(2):
                    t = nc.vector.tensor_tensor(w[:, n, :, :], pair[n][:, :, XW:PW],
                                                mask[:, n, :].unsqueeze(2).to_broadcast([P, UNR, NH]), ALU.add)
                c.link(t)
                c.link(nc.vector.tensor_tensor(top[:, :, :], w[:, 0, :, :], w[:, 1, :, :], ALU.max))
                nc.vector.tensor_tensor(w[:, :, :, :], w[:, :, :, :], top[:, :, :].unsqueeze(1).to_broadcast([P, 2, UNR, NH]),
                                        ALU.subtract).then_inc(below_ready, 1)
                dve.wait_ge(weights_ready, u + 1)
                c.link(nc.vector.tensor_tensor(w[:, :, :, :], w[:, :, :, :],
                                               valid[:, :, :].unsqueeze(3).to_broadcast([P, 2, UNR, NH]), ALU.mult))
                for n in range(2):
                    t = nc.vector.tensor_tensor(den[:, n, :, :], pair[n][:, :, H:XW], w[:, n, :, :], ALU.mult)
                c.link(t)
                c.link(nc.vector.tensor_tensor(top[:, :, :], den[:, 0, :, :], den[:, 1, :, :], ALU.add))
                c.link(nc.vector.tensor_tensor(top[:, :, :], top[:, :, :], none[:, :].unsqueeze(2).to_broadcast([P, UNR, NH]), ALU.add))
                c.link(nc.vector.reciprocal(top[:, :, :], top[:, :, :]))
                c.link(nc.vector.tensor_tensor(w[:, :, :, :], w[:, :, :, :], top[:, :, :].unsqueeze(1).to_broadcast([P, 2, UNR, NH]), ALU.mult))
                for n in range(2):
                    f = pair[n][:, :, 0:H].rearrange("p b (c h) -> p b c h", h=NH)
                    t = nc.vector.tensor_tensor(f, f, w[:, n, :, :].unsqueeze(2).to_broadcast([P, UNR, H // NH, NH]), ALU.mult)
                t.then_inc(scaled, 1)

            first = Chain(dve, dve_step)
            dve.sem_inc(moments_ready, UNR)
            scale(0, 0, 0, first)
            PER = first.n + 1

            def body(u, r, v, last):
                c = Chain(dve, dve_step, u * PER + first.n)
                if not last:
                    scale(u + 1, 1 - r, v + r, c)
                dve.wait_ge(moments_ready, u * UNR + UNR)
                dve.wait_ge(summed, u * UNR + UNR)
                for j in range(UNR):
                    t = nc.vector.bn_stats(stats[:, j, :], bank(r, j))
                c.link(t)
                dve.wait_ge(rstd_ready, u + 1)
                dve.sem_inc(dve_waited, 1)
                for j in range(UNR):
                    nc.vector.bn_aggr(moments[:, j, :], stats[:, j, :]).then_inc(moments_ready, 1)
                assert c.n == PER or last

            units(dve, body)


def build(nc, x, src, dst, edge_attr, W1, b1, W2, b2, W_ih, b_ih, W_hh, b_hh, W_u, b_u, W_v, out, stop=99):
    A = dict(x=x, src=src, dst=dst, edge_attr=edge_attr, W1=W1, b1=b1, W2=W2, b2=b2, W_ih=W_ih, b_ih=b_ih,
             W_hh=W_hh, b_hh=b_hh, W_u=W_u, b_u=b_u, W_v=W_v, out=out)

    def dram(name, shape, dt=F32):
        return nc.dram_tensor(name, shape, dt, kind="Internal").ap()

    D = {"A": dram("A_rows", [NP, H]), "B": dram("B_rows", [NP + P, NSPLIT * H], BF16),
         "src_rows": dram("src_rows", [NTX, P]), "dst_rows": dram("dst_rows", [NT + 1, P]),
         "loc_rows": dram("loc_rows", [NTX, P], BF16), "blocks": dram("block_words", [NT // PACK, 1], I32)}
    D["last"], D["upto"] = dram("last", [NT, 1]), dram("upto", [NP + 1, 1])
    D["GH"] = dram("GH_rows", [NP, 3 * H])
    D["T2"] = dram("T2", [NT, PW])
    D["PT"] = dram("PT", [NT * P, PW])
    D["X1"], D["sv"] = dram("X1_rows", [NP, XW]), dram("sv_rows", [NP + P, NH])
    for t in range(NTAB):
        D[f"S{t}"] = dram(f"S{t}", [SROWS, UW])
    with ExitStack() as st:
        m = Mem(nc, st)
        K = {"ident": m.sb("ident", [P, P]), "before": m.sb("before", [P, P]),
             "winid": m.sb("winid", [P, WIN]), "spare": m.sb("spare", [P, 1]),
             "srcT": m.sb("srcT", [P, NTX]), "startT": m.sb("startT", [P, NT]), "locT": m.sb("locT", [P, NTX]),
             "blocks": m.sb("blocks", [1, PACKED], I32), "rank": m.sb("rank", [P, NB]),
             "W1cT": m.sb("W1cT", [2 * ED, H]),
             "WcT": m.sb("WcT", [P, HC, 3 * H]), "b2ih": m.sb("b2ih", [P, 3 * H]), "WhhT": m.sb("WhhT", [P, HC, 3 * H]),
             "WuvT": m.sb("WuvT", [P, HC, 2 * NH]),
             "any": m.sb("any", [P, NB]), "ends": m.sb("ends", [P, NB]), "own": m.sb("own", [P, NB]),
             
             "ends_row": m.sb("ends_row", [P, NB + UNR]), "own_row": m.sb("own_row", [P, NB + UNR]),
             "eps": m.sb("eps", [P, 1]), "neghalf": m.sb("neghalf", [P, 1]),
             "bgate": m.sb("bgate", [P, 4 * H]), "bu": m.sb("bu", [P, 2 * NH])}
        K["b_out"] = [m.sem(f"b_out{j}") for j in range(UNR)]
        K["edges_gathered"] = m.sem("edges_gathered")
        setup_phase(nc, K, D, A)
        if stop < 1:
            return
        layer0_phase(nc, K, D, A)
        if stop < 2:
            return
        nodes_phase(nc, K, D, A)
        if stop < 3:
            return
        layer1_phase(nc, K, D, A)
        if stop < 4:
            return
        O = {"own": m.sb("own_rows", [P, NB, PW]), "x1": m.sb("x1_rows", [P, NB, H]), "own_in": m.sem("own_in"),
             "own_i": m.sb("own_i", [P, NB], I32), "ends_i": m.sb("ends_i", [P, NB], I32)}
        merge_phase(nc, K, D, A, O)
        output_phase(nc, K, D, A, O)


def kernel(**inputs):
    import numpy as np
    import concourse.bacc as bacc
    from concourse.bass_utils import run_bass_kernel_spmd

    names = ["x", "src", "dst", "edge_attr_64", "L0_gnn_W1", "L0_gnn_b1", "L0_gnn_W2", "L0_gnn_b2", "L0_gnn_W_ih",
             "L0_gnn_b_ih", "L0_gnn_W_hh", "L0_gnn_b_hh", "L1_gnn_W_u", "L1_gnn_b_u", "L1_gnn_W_v"]
    nc = bacc.Bacc("TRN2", target_bir_lowering=False, num_devices=1)
    arrays, args = {}, []
    for name in names:
        a = np.ascontiguousarray(inputs[name])
        arrays[f"in_{name}"] = a
        args.append(nc.dram_tensor(f"in_{name}", a.shape, mybir.dt.from_np(a.dtype), kind="ExternalInput").ap())
    out = nc.dram_tensor("out_0", (N, H), F32, kind="ExternalOutput").ap()
    build(nc, *args, out)
    result = run_bass_kernel_spmd(nc, [arrays], core_ids=[0])
    return result.results[0]["out_0"]
```
